# Optimizing a Trainium2 kernel written in Bass

```python
import numpy as np
import jax
import jax.numpy as jnp

def _softmax(x, axis=-1):
    return jax.nn.softmax(x, axis=axis)

def _gelu(x):
    return jax.nn.gelu(x, approximate=True)

def _silu(x):
    return jax.nn.silu(x)

def _sigmoid(x):
    return jax.nn.sigmoid(x)

def _layernorm(x, axis=-1, eps=1e-05):
    m = jnp.mean(x, axis=axis, keepdims=True)
    v = jnp.var(x, axis=axis, keepdims=True)
    return (x - m) / jnp.sqrt(v + eps)

def _scatter_add(tgt, idx, src, axis=0):
    return tgt.at[idx].add(src)

def _segment_sum(src, seg, n):
    return jax.ops.segment_sum(src, seg, n)
kernel_name = 'mk_xattn_ffn_d2_seqx_r8_012333'

def setup_inputs(seed: int=0):
    np.random.seed(seed)
    _w = jnp.asarray

    def _rec_inputs():
        import jax
        import jax.numpy as jnp
        _rk = jax.random.key(seed)
        x = 7.22e-05 + 1 * jax.random.normal(jax.random.fold_in(_rk, 1), (8, 128, 256), jnp.float32)
        _lenS = 128 - jax.random.randint(jax.random.fold_in(_rk, 7), (8,), 0, max(1, 128 // 4) + 1, jnp.int32)
        _lenS2 = 128 - jax.random.randint(jax.random.fold_in(_rk, 8), (8,), 0, max(1, 128 // 4) + 1, jnp.int32)
        _ctx_2048P = jax.random.normal(jax.random.fold_in(_rk, 11), (8, 16, 256), jnp.float32)
        _ctx_2048c = jax.random.dirichlet(jax.random.fold_in(_rk, 511), 0.3 * jnp.ones((16,), jnp.float32), (8, 128))
        _ctx_2048t = jnp.einsum('bsk,bkd->bsd', _ctx_2048c, _ctx_2048P)
        _ctx_2048t = _ctx_2048t * jax.lax.rsqrt(jnp.mean(jnp.square(_ctx_2048t)) + 1e-12) * 0.953939
        ctx_2048 = 4.13588e-05 + 0.999923 * (_ctx_2048t + 0.3 * jax.random.normal(jax.random.fold_in(_rk, 611), (8, 128, 256), jnp.float32))
        return (x, ctx_2048)
    x, ctx_2048 = _rec_inputs()

    def _L0_xattn_setup():
        import jax, jax.numpy as jnp
        import numpy as np
        B, D, N, H = (4, 128, 256, 16)
        HD = D // H

        def rotate_half(x):
            x1 = x[..., 0::2]
            x2 = x[..., 1::2]
            return jnp.stack((-x2, x1), axis=-1).reshape(x.shape)

        def apply_cached_rotary_emb(freqs, t):
            return t * freqs[0] + rotate_half(t) * freqs[1]
        key = jax.random.key(seed)
        ks = jax.random.split(key, 13)
        s = 1.0 / np.sqrt(D)
        inp = {'query': jax.random.normal(ks[0], (B, D, N), jnp.float32), 'key': jax.random.normal(ks[1], (B, D, N), jnp.float32), 'value': jax.random.normal(ks[2], (B, D, N), jnp.float32), 'encoding': jax.random.normal(ks[3], (2, 1, 1, N, HD), jnp.float32), 'Wq': jax.random.normal(ks[4], (D, D), jnp.float32) * s, 'bq': jax.random.normal(ks[5], (D,), jnp.float32) * s, 'Wk': jax.random.normal(ks[6], (D, D), jnp.float32) * s, 'bk': jax.random.normal(ks[7], (D,), jnp.float32) * s, 'Wv': jax.random.normal(ks[8], (D, D), jnp.float32) * s, 'bv': jax.random.normal(ks[9], (D,), jnp.float32) * s, 'Wm': jax.random.normal(ks[10], (D, D), jnp.float32) * s, 'bm': jax.random.normal(ks[11], (D,), jnp.float32) * s}
        return inp
    _L0_xattn_all = _L0_xattn_setup()
    _L0_xattn_in = {k: v for k, v in _L0_xattn_all.items() if k in ('encoding', 'Wq', 'bq', 'Wk', 'bk', 'Wv', 'bv', 'Wm', 'bm')}
    del _L0_xattn_all

    def _L0_ffn_setup():
        import jax, jax.numpy as jnp
        import numpy as np
        NUM_EXPERTS = 64
        TOP_K = 8
        HIDDEN = 256
        INTER = 128
        key = jax.random.key(seed)
        k1, k2, k3, k4 = jax.random.split(key, 4)
        scale = 1.0 / np.sqrt(HIDDEN)
        hidden_states = jax.random.normal(k1, (4, 256, HIDDEN), dtype=jnp.float32)
        gate_w = jax.random.normal(k2, (NUM_EXPERTS, HIDDEN), dtype=jnp.float32) * scale
        w13 = jax.random.normal(k3, (NUM_EXPERTS, 2 * INTER, HIDDEN), dtype=jnp.float32) * scale
        w2 = jax.random.normal(k4, (NUM_EXPERTS, HIDDEN, INTER), dtype=jnp.float32) * (1.0 / np.sqrt(INTER))
        return {'hidden_states': hidden_states, 'gate_w': gate_w, 'w13': w13, 'w2': w2}
    _L0_ffn_all = _L0_ffn_setup()
    _L0_ffn_in = {k: v for k, v in _L0_ffn_all.items() if k in ('gate_w', 'w13', 'w2')}
    del _L0_ffn_all

    def _L1_xattn_setup():
        import jax, jax.numpy as jnp
        import numpy as np
        BS, S, DK = (8, 64, 256)
        key = jax.random.key(seed)
        kq, kk, kv = jax.random.split(key, 3)
        q = jax.random.normal(kq, (BS, S, DK), dtype=jnp.float32)
        k = jax.random.normal(kk, (BS, S, DK), dtype=jnp.float32)
        v = jax.random.normal(kv, (BS, S, DK), dtype=jnp.float32)
        return {'q': q, 'k': k, 'v': v}
    _L1_xattn_all = _L1_xattn_setup()
    _L1_xattn_in = {k: v for k, v in _L1_xattn_all.items() if k in ()}
    del _L1_xattn_all

    def _L1_ffn_setup():
        import jax, jax.numpy as jnp
        import numpy as np
        TOP_K = 4
        NUM_EXPERTS = 16
        key = jax.random.key(seed)
        ks = jax.random.split(key, 6)
        B, S, H, I, E = (2, 128, 256, 224, NUM_EXPERTS)
        return {'x': jax.random.normal(ks[0], (B, S, H), dtype=jnp.float32), 'router_w': jax.random.normal(ks[1], (E, H), dtype=jnp.float32) * 0.02, 'expert_bias': jnp.zeros((E,), dtype=jnp.float32), 'gate_proj': jax.random.normal(ks[2], (E, H, I), dtype=jnp.float32) * 0.02, 'up_proj': jax.random.normal(ks[3], (E, H, I), dtype=jnp.float32) * 0.02, 'down_proj': jax.random.normal(ks[4], (E, I, H), dtype=jnp.float32) * 0.02}
    _L1_ffn_all = _L1_ffn_setup()
    _L1_ffn_in = {k: v for k, v in _L1_ffn_all.items() if k in ('router_w', 'expert_bias', 'gate_proj', 'up_proj', 'down_proj')}
    del _L1_ffn_all
    return {'x': x, 'ctx_2048': ctx_2048, 'L0_xattn_encoding': _L0_xattn_in['encoding'], 'L0_xattn_Wq': _L0_xattn_in['Wq'], 'L0_xattn_bq': _L0_xattn_in['bq'], 'L0_xattn_Wk': _L0_xattn_in['Wk'], 'L0_xattn_bk': _L0_xattn_in['bk'], 'L0_xattn_Wv': _L0_xattn_in['Wv'], 'L0_xattn_bv': _L0_xattn_in['bv'], 'L0_xattn_Wm': _L0_xattn_in['Wm'], 'L0_xattn_bm': _L0_xattn_in['bm'], 'L0_ffn_gate_w': _L0_ffn_in['gate_w'], 'L0_ffn_w13': _L0_ffn_in['w13'], 'L0_ffn_w2': _L0_ffn_in['w2'], 'L1_ffn_router_w': _L1_ffn_in['router_w'], 'L1_ffn_expert_bias': _L1_ffn_in['expert_bias'], 'L1_ffn_gate_proj': _L1_ffn_in['gate_proj'], 'L1_ffn_up_proj': _L1_ffn_in['up_proj'], 'L1_ffn_down_proj': _L1_ffn_in['down_proj']}

def reference(x, ctx_2048, L0_xattn_encoding, L0_xattn_Wq, L0_xattn_bq, L0_xattn_Wk, L0_xattn_bk, L0_xattn_Wv, L0_xattn_bv, L0_xattn_Wm, L0_xattn_bm, L0_ffn_gate_w, L0_ffn_w13, L0_ffn_w2, L1_ffn_router_w, L1_ffn_expert_bias, L1_ffn_gate_proj, L1_ffn_up_proj, L1_ffn_down_proj):
    import jax
    import jax.numpy as jnp

    def _L0_xattn_ref(query, key, value, encoding, Wq, bq, Wk, bk, Wv, bv, Wm, bm):
        import jax, jax.numpy as jnp
        import numpy as np
        B, D, N, H = (4, 128, 256, 16)
        HD = D // H

        def rotate_half(x):
            x1 = x[..., 0::2]
            x2 = x[..., 1::2]
            return jnp.stack((-x2, x1), axis=-1).reshape(x.shape)

        def apply_cached_rotary_emb(freqs, t):
            return t * freqs[0] + rotate_half(t) * freqs[1]
        b, d_model, n = query.shape

        def proj(W, bias, x):
            return jnp.einsum('oi,bin->bon', W, x) + bias[None, :, None]
        q = proj(Wq, bq, query).reshape(b, HD, H, n)
        k = proj(Wk, bk, key).reshape(b, HD, H, n)
        v = proj(Wv, bv, value).reshape(b, HD, H, n)
        q = jnp.transpose(apply_cached_rotary_emb(encoding, jnp.transpose(q, (0, 2, 3, 1))), (0, 3, 1, 2))
        k = jnp.transpose(apply_cached_rotary_emb(encoding, jnp.transpose(k, (0, 2, 3, 1))), (0, 3, 1, 2))
        scores = jnp.einsum('bdhn,bdhm->bhnm', q, k) / np.float32(np.sqrt(HD))
        prob = jax.nn.softmax(scores, axis=-1)
        x = jnp.einsum('bhnm,bdhm->bdhn', prob, v)
        out = jnp.einsum('oi,bin->bon', Wm, x.reshape(b, d_model, n)) + bm[None, :, None]
        return out

    def _L0_ffn_ref(hidden_states, gate_w, w13, w2):
        import jax, jax.numpy as jnp
        import numpy as np
        NUM_EXPERTS = 64
        TOP_K = 8
        HIDDEN = 256
        INTER = 128
        orig_shape = hidden_states.shape
        x = hidden_states.reshape(-1, HIDDEN)
        logits = jnp.einsum('th,eh->te', x, gate_w)
        probs = jax.nn.softmax(logits, axis=-1)
        topk_w, topk_idx = jax.lax.top_k(probs, TOP_K)
        combine = (jax.nn.one_hot(topk_idx, NUM_EXPERTS, dtype=x.dtype) * topk_w[..., None]).sum(axis=1)

        def step(acc, inp):
            w13_e, w2_e, c = inp
            g = x @ w13_e[:INTER].T
            u = x @ w13_e[INTER:].T
            h = jax.nn.silu(g) * u
            o = h @ w2_e.T
            return (acc + c[:, None] * o, None)
        out0 = jnp.zeros_like(x)
        out, _ = jax.lax.scan(step, out0, (w13, w2, combine.T))
        return out.reshape(orig_shape)

    def _L1_xattn_ref(q, k, v):
        import jax, jax.numpy as jnp
        import numpy as np
        BS, S, DK = (8, 64, 256)
        dk = q.shape[-1]
        scale = 1.0 / jnp.sqrt(jnp.asarray(dk, dtype=q.dtype))
        scaled = jnp.einsum('bsd,bse->bde', q, k) * scale
        attn = jax.nn.softmax(scaled, axis=1)
        out = jnp.einsum('bde,bse->bsd', attn, v)
        return out

    def _L1_ffn_ref(x, router_w, expert_bias, gate_proj, up_proj, down_proj):
        import jax, jax.numpy as jnp
        import numpy as np
        TOP_K = 4
        NUM_EXPERTS = 16
        logits = jnp.einsum('bsh,eh->bse', x, router_w) + expert_bias
        scores = jax.nn.softmax(logits, axis=-1)
        top_w, top_idx = jax.lax.top_k(scores, TOP_K)
        top_w = top_w / jnp.sum(top_w, axis=-1, keepdims=True)
        g = jnp.einsum('bsh,khe->bske', x, gate_proj)
        u = jnp.einsum('bsh,khe->bske', x, up_proj)
        act = jax.nn.silu(g) * u
        out = jnp.einsum('bske,keh->bskh', act, down_proj)
        sel = jnp.take_along_axis(out, top_idx[..., None], axis=2)
        return jnp.sum(sel * top_w[..., None], axis=2)
    x = x + _L0_xattn_ref(_layernorm(x, axis=-1), ctx_2048, ctx_2048, L0_xattn_encoding, L0_xattn_Wq, L0_xattn_bq, L0_xattn_Wk, L0_xattn_bk, L0_xattn_Wv, L0_xattn_bv, L0_xattn_Wm, L0_xattn_bm)
    x = x + _L0_ffn_ref(_layernorm(x, axis=-1), L0_ffn_gate_w, L0_ffn_w13, L0_ffn_w2)
    x = x + _L1_xattn_ref(_layernorm(x, axis=-1), ctx_2048, ctx_2048)
    x = x + _L1_ffn_ref(_layernorm(x, axis=-1), L1_ffn_router_w, L1_ffn_expert_bias, L1_ffn_gate_proj, L1_ffn_up_proj, L1_ffn_down_proj)
    return x

_drawn_inputs = setup_inputs


def setup_inputs(seed=0):
    import zlib

    import numpy as np

    out = dict(_drawn_inputs(seed))
    spreads = {'L1_ffn_expert_bias': (0.0, 0.8)}
    factors = {'L1_ffn_router_w': 8.0,
     'L1_ffn_gate_proj': 8.0,
     'L1_ffn_up_proj': 8.0,
     'L1_ffn_down_proj': 8.0,
     'L0_xattn_bv': 4.512,
     'L0_xattn_bm': 4.687}
    for name, (base, spread) in spreads.items():
        noise = np.random.default_rng([zlib.crc32(name.encode()), seed]).standard_normal(out[name].shape)
        drawn = base * np.exp(spread * noise) if base else spread * noise
        out[name] = jnp.asarray(drawn.astype(out[name].dtype))
    for name, factor in factors.items():
        out[name] = (out[name] * factor).astype(out[name].dtype)
    return out
```

```python
from contextlib import ExitStack

import numpy as np

import concourse.bass as bass
from concourse import mybir

P = 128
B = 8
D = 256
TOKENS = B * P
H = 16
HD = P // H
EPS = 1e-5
PARTS = 3
TERMS = 6
STACK = TERMS * HD
VW = 32

F32 = mybir.dt.float32
BF16 = mybir.dt.bfloat16
I32 = mybir.dt.int32
U32 = mybir.dt.uint32
ALU = mybir.AluOpType
ACT = mybir.ActivationFunctionType
AX_X = mybir.AxisListType.X


class Layer:

    def __init__(self, name, experts, chosen, inter, unroll):
        self.name, self.experts, self.chosen, self.inter, self.unroll = name, experts, chosen, inter, unroll
        self.chunks = -(-inter // P)
        self.width = inter // self.chunks
        self.lists = TOKENS // P
        self.columns = experts * self.lists
        most = TOKENS * chosen // P + experts - 1
        self.tiles = -(-most // unroll) * unroll
        self.least = TOKENS * chosen // P
        assert self.width * self.chunks == inter and self.tiles <= P


LAYER0 = Layer("l0_", 64, 8, 128, 8)
LAYER1 = Layer("l1_", 16, 4, 224, 6)


class Link:

    def __init__(self, engine, semaphore):
        self.engine, self.semaphore, self.count = engine, semaphore, 0

    def __call__(self, instruction):
        self.count += 1
        instruction.then_inc(self.semaphore, 1)
        self.engine.wait_ge(self.semaphore, self.count)


class Space:

    def __init__(self, nc, stack, prefix):
        self.nc, self.stack, self.prefix = nc, stack, prefix
        self.semaphores = []
        stack.callback(self.clear)

    def sbuf(self, name, shape, dtype):
        return self.stack.enter_context(self.nc.sbuf_tensor(self.prefix + name, shape, dtype))

    def psum(self, name, shape, dtype=F32):
        return self.stack.enter_context(self.nc.psum_tensor(self.prefix + name, shape, dtype))

    def sem(self, name):
        self.semaphores.append(self.nc.alloc_semaphore(self.prefix + name))
        return self.semaphores[-1]

    def clear(self):
        if self.semaphores:
            self.nc.clear_and_free_semaphores(self.semaphores)
            self.nc.all_engine_barrier()


def normalise_stats(nc, link, x, stats, mean_var):
    link(nc.vector.bn_stats(stats[:], x))
    link(nc.vector.bn_aggr(mean_var[:, 0:2], stats[:]))
    link(nc.vector.tensor_scalar(mean_var[:, 1:2], mean_var[:, 1:2], EPS, None, ALU.add))


def reciprocal_root(nc, link, mean_var, work):
    bits, magic = work[:, 0:1].bitcast(I32), float(0x5F3759DF)
    link(nc.vector.tensor_scalar(work[:, 1:2].bitcast(I32), mean_var[:, 1:2].bitcast(I32), 1, None,
                                 ALU.logical_shift_right))
    link(nc.vector.tensor_scalar(bits, work[:, 1:2].bitcast(I32), -1.0, magic, ALU.mult, ALU.add))
    for _ in range(4):
        link(nc.vector.scalar_tensor_tensor(work[:, 1:2], work[:, 0:1], mean_var[:, 1:2], work[:, 0:1],
                                            ALU.mult, ALU.mult))
        link(nc.vector.tensor_scalar(work[:, 1:2], work[:, 1:2], -0.5, 1.5, ALU.mult, ALU.add))
        link(nc.vector.tensor_tensor(work[:, 0:1], work[:, 0:1], work[:, 1:2], ALU.mult))


def project_phase(nc, x, ctx, weights, biases, rotary, q_stack, k_stack, values):
    with ExitStack() as stack:
        s = Space(nc, stack, "pj_")
        w = s.sbuf("w", [P, 4, P], F32)
        w_turned = s.sbuf("w_turned", [P, 2, P], F32)
        bias = s.sbuf("bias", [P, 7], F32)
        bias_turned = s.sbuf("bias_turned", [P, 2], F32)
        rot = s.sbuf("rot", [P, 2, D], F32)
        x_in = [s.sbuf(f"x_in{n}", [P, D], F32) for n in range(2)]
        c_in = [s.sbuf(f"c_in{n}", [P, D], F32) for n in range(2)]
        x_norm = [s.sbuf(f"x_norm{n}", [P, D], F32) for n in range(2)]
        stats = s.sbuf("stats", [P, 6], F32)
        mean_var = s.sbuf("mean_var", [P, 2], F32)
        root = s.sbuf("root", [P, 2], F32)
        straight = s.sbuf("straight", [P, 2, D], F32)
        turned = s.sbuf("turned", [P, 2, D], F32)
        full = [s.sbuf(f"full{n}", [P, 2, D], F32) for n in range(2)]
        rest = [s.sbuf(f"rest{n}", [P, 2, D], F32) for n in range(2)]
        parts = [s.sbuf(f"parts{n}", [P, 2, PARTS, D], BF16) for n in range(2)]
        v_out = [s.sbuf(f"v_out{n}", [P, 2, H, VW], F32) for n in range(2)]
        ps_qk = [s.psum(f"ps_qk{n}", [P, 2, 2, D]) for n in range(2)]
        ps_v = [s.psum(f"ps_v{n}", [P, 2, P]) for n in range(2)]
        consts_loaded, link_v = s.sem("consts_loaded"), s.sem("link_v")
        x_loaded = [s.sem(f"x_loaded{n}") for n in range(2)]
        c_loaded = [s.sem(f"c_loaded{n}") for n in range(2)]
        stored = [s.sem(f"stored{n}") for n in range(2)]
        w_ready, normed, projected, roped = s.sem("w_ready"), s.sem("normed"), s.sem("projected"), s.sem("roped")
        summed, high_cut, rest_ready, mid_cut, low_cut = (
            s.sem(n) for n in ("summed", "high_cut", "rest_ready", "mid_cut", "low_cut"))
        ones_set, v_kept = s.sem("ones_set"), s.sem("v_kept")
        block = stack.enter_context(nc.Block())

        @block.sync
        def _(sp):
            def load(b):
                if b >= 2:
                    sp.wait_ge(normed, b - 1)
                sp.dma_start(x_in[b % 2][:], x[b]).then_inc(x_loaded[b % 2], 16)
                if b >= 2:
                    sp.wait_ge(projected, b - 1)
                sp.dma_start(c_in[b % 2][:], ctx[b]).then_inc(c_loaded[b % 2], 16)

            sp.dma_start(x_in[0][:], x[0]).then_inc(x_loaded[0], 16)
            sp.dma_start(w[:], weights).then_inc(consts_loaded, 16)
            sp.dma_start(bias[:], biases).then_inc(consts_loaded, 16)
            sp.dma_start(c_in[0][:], ctx[0]).then_inc(c_loaded[0], 16)
            sp.dma_start(rot[:], rotary).then_inc(consts_loaded, 16)
            load(1)
            for b in range(B):
                n = b % 2
                if b + 2 < B:
                    load(b + 2)
                sp.wait_ge(v_kept, b + 1)
                sp.dma_start(values[b], v_out[n][:]).then_inc(stored[n], 16)
                sp.wait_ge(low_cut, b + 1)
                row = 0
                for i in range(PARTS):
                    m = PARTS - i
                    q_to = q_stack[b, row:row + m].rearrange("j p n -> p j n")
                    k_to = k_stack[b, row:row + m].rearrange("j p n -> p j n")
                    q_from = parts[n][:, 0, i:i + 1, :].broadcast_to([P, m, D])
                    sp.dma_start(q_to, q_from).then_inc(stored[n], 16)
                    sp.dma_start(k_to, parts[n][:, 1, 0:m, :]).then_inc(stored[n], 16)
                    row += m
            for n in range(2):
                sp.wait_ge(stored[n], 16 * 7 * (B // 2))

        @block.tensor
        def _(pe):
            pe.wait_ge(w_ready, 1)
            for b in range(B):
                n = b % 2
                if b >= 2:
                    pe.wait_ge(roped, b - 1)
                    pe.wait_ge(v_kept, b - 1)
                pe.wait_ge(normed, b + 1)
                nc.tensor.matmul(ps_qk[n][:, 0, 0, :], w[:, 0, :], x_norm[n][:], start=True, stop=True)
                nc.tensor.matmul(ps_qk[n][:, 0, 1, :], w_turned[:, 0, :], x_norm[n][:], start=True, stop=True)
                pe.wait_ge(c_loaded[n], 16 * (b // 2 + 1))
                nc.tensor.matmul(ps_qk[n][:, 1, 0, :], w[:, 1, :], c_in[n][:], start=True, stop=True)
                nc.tensor.matmul(ps_qk[n][:, 1, 1, :], w_turned[:, 1, :], c_in[n][:], start=True, stop=True)
                for m in range(2):
                    last = nc.tensor.matmul(ps_v[n][:, m, :], c_in[n][:, m * P:(m + 1) * P], w[:, 2, :],
                                            start=True, stop=True)
                last.then_inc(projected, 1)

        @block.vector
        def _(dve):
            link = Link(dve, link_v)

            def normalise(b):
                n = b % 2
                dve.wait_ge(x_loaded[n], 16 * (b // 2 + 1))
                normalise_stats(nc, link, x_in[n][:], stats, mean_var)
                reciprocal_root(nc, link, mean_var, root)
                if b >= 2:
                    dve.wait_ge(projected, b - 1)
                nc.vector.tensor_scalar(x_norm[n][:], x_in[n][:], mean_var[:, 0:1], root[:, 0:1],
                                        ALU.subtract, ALU.mult).then_inc(normed, 1)

            normalise(0)
            dve.wait_ge(consts_loaded, 48)
            for t in range(2):
                to = w_turned[:, t, :].rearrange("p (j s h) -> p j s h", s=2, h=H)
                of = w[:, t, :].rearrange("p (j s h) -> p j s h", s=2, h=H)
                nc.vector.tensor_scalar(to[:, :, 0, :], of[:, :, 1, :], -1.0, None, ALU.mult)
                last = nc.vector.tensor_copy(to[:, :, 1, :], of[:, :, 0, :])
            last.then_inc(w_ready, 1)
            link(nc.vector.tensor_scalar(bias_turned[:], bias[:, 4:6], bias[:, 6:7], None, ALU.mult))
            for b in range(B):
                n = b % 2
                if b + 1 < B:
                    normalise(b + 1)
                dve.wait_ge(projected, b + 1)
                if b >= 1:
                    dve.wait_ge(summed, b)
                for t in range(2):
                    nc.vector.scalar_tensor_tensor(straight[:, t, :], ps_qk[n][:, t, 0, :], bias[:, t:t + 1],
                                                   rot[:, 0, :], ALU.add, ALU.mult)
                    last = nc.vector.scalar_tensor_tensor(turned[:, t, :], ps_qk[n][:, t, 1, :],
                                                          bias_turned[:, t:t + 1], rot[:, 1, :], ALU.add, ALU.mult)
                last.then_inc(roped, 1)

        @block.gpsimd
        def _(pool):
            for n in range(2):
                last = nc.gpsimd.memset(v_out[n][:], 1.0)
            last.then_inc(ones_set, 1)
            for b in range(B):
                n = b % 2
                pool.wait_ge(roped, b + 1)
                if b >= 2:
                    pool.wait_ge(low_cut, b - 1)
                nc.gpsimd.tensor_tensor(full[n][:], straight[:], turned[:], ALU.add).then_inc(summed, 1)
                pool.wait_ge(high_cut, b + 1)
                nc.gpsimd.tensor_tensor(rest[n][:], full[n][:], parts[n][:, :, 0, :], ALU.subtract).then_inc(rest_ready, 1)
                pool.wait_ge(mid_cut, b + 1)
                pool.wait_ge(rest_ready, b + 1)
                nc.gpsimd.tensor_tensor(parts[n][:, :, 2, :], rest[n][:], parts[n][:, :, 1, :],
                                        ALU.subtract).then_inc(low_cut, 1)

        @block.scalar
        def _(act):
            act.wait_ge(ones_set, 1)
            for b in range(B):
                n = b % 2
                act.wait_ge(projected, b + 1)
                if b >= 2:
                    act.wait_ge(stored[n], 16 * 7 * (b // 2))
                nc.scalar.activation(v_out[n][:, :, :, 0:HD], ps_v[n][:].rearrange("p m (d h) -> p m h d", h=H),
                                     ACT.Copy).then_inc(v_kept, 1)
                act.wait_ge(summed, b + 1)
                nc.scalar.activation(parts[n][:, :, 0, :], full[n][:], ACT.Copy).then_inc(high_cut, 1)
                act.wait_ge(rest_ready, b + 1)
                nc.scalar.activation(parts[n][:, :, 1, :], rest[n][:], ACT.Copy).then_inc(mid_cut, 1)


def attend_phase(nc, identity, q_stack, k_stack, values, attended, tails):
    ROWS = STACK + PARTS
    scale = 1.0 / float(np.sqrt(HD))
    HALF = H // 2
    with ExitStack() as stack:
        s = Space(nc, stack, "at_")
        DEEP = 3
        q_in = [s.sbuf(f"q_in{n}", [ROWS, H * D], BF16) for n in range(DEEP)]
        k_in = [s.sbuf(f"k_in{n}", [ROWS, H * D], BF16) for n in range(DEEP)]
        v_in = [s.sbuf(f"v_in{n}", [P, 2, H, VW], F32) for n in range(DEEP)]
        top = s.sbuf("top", [P, 2 * H], F32)
        top_rest = s.sbuf("top_rest", [P, 2, 2 * HALF], F32)
        top_parts = s.sbuf("top_parts", [P, 2, PARTS, 2 * HALF], F32)
        top_cut = s.sbuf("top_cut", [P, 2 * HALF], BF16)
        top_rows = [s.sbuf(f"top_rows{n}", [PARTS * 2 * HALF, P], BF16) for n in range(2)]
        RING = 8
        prob = [s.sbuf(f"prob{n}", [P, 2, D], F32) for n in range(RING)]
        out = [s.sbuf(f"out{n}", [P, 4, D], F32) for n in range(2)]
        ps_top = [s.psum(f"ps_top{n}", [P, 2, D]) for n in range(2)]
        ps_score = [s.psum(f"ps_score{n}", [P, 2, D]) for n in range(3)]
        ps_out = [s.psum(f"ps_out{n}", [P, 2, D]) for n in range(2)]
        ps_rows = s.psum("ps_rows", [P, P])
        zeros = s.sbuf("zeros", [P, D], F32)
        zeros_set, tails_zeroed = s.sem("zeros_set"), s.sem("tails_zeroed")
        loaded = [s.sem(f"loaded{n}") for n in range(DEEP)]
        ones_set, top_scored, top_found, parts_cut, rows_turned, rows_kept = (
            s.sem(n) for n in ("ones_set", "top_scored", "top_found", "parts_cut", "rows_turned", "rows_kept"))
        rows_placed = [s.sem(f"rows_placed{n}") for n in range(2)]
        scored, prob_ready, weighted, out_kept, link_v = (
            s.sem(n) for n in ("scored", "prob_ready", "weighted", "out_kept", "link_v"))
        stored = [s.sem(f"stored{n}") for n in range(2)]
        block = stack.enter_context(nc.Block())

        def head_columns(h, half=None):
            return slice(h * D, (h + 1) * D) if half is None else slice(h * D + half * P, h * D + (half + 1) * P)

        @block.sync
        def _(sp):
            def load(b):
                n = b % DEEP
                if b >= DEEP:
                    sp.wait_ge(weighted, 4 * (b - DEEP + 1))
                sp.dma_start(q_in[n][0:STACK, :], q_stack[b].rearrange("t (d h) n -> (t d) (h n)", h=H)).then_inc(loaded[n], 16)
                sp.dma_start(k_in[n][0:STACK, :], k_stack[b].rearrange("t (d h) n -> (t d) (h n)", h=H)).then_inc(loaded[n], 16)
                sp.dma_start(v_in[n][:], values[b]).then_inc(loaded[n], 16)

            def place(b, half):
                n = b % DEEP
                sp.wait_ge(rows_kept, 2 * b + half + 1)
                for i in range(PARTS):
                    to = q_in[n][STACK + i:STACK + i + 1, half * HALF * D:(half + 1) * HALF * D]
                    sp.dma_start(to.rearrange("a (r n) -> a r n", n=P),
                                 top_rows[half][i * 2 * HALF:(i + 1) * 2 * HALF, :]).then_inc(rows_placed[half], 16)

            sp.wait_ge(ones_set, 1)
            for b in range(DEEP):
                load(b)
            place(0, 0)
            place(0, 1)
            for b in range(B):
                if b + 1 < B:
                    place(b + 1, 0)
                    place(b + 1, 1)
                if b + DEEP < B:
                    load(b + DEEP)
                sp.wait_ge(out_kept, 2 * b + 2)
                sp.dma_start(attended[b], out[b % 2][:]).then_inc(stored[b % 2], 16)
            for n in range(2):
                sp.wait_ge(stored[n], 16 * (B // 2))

        @block.gpsimd
        def _(pool):
            nc.gpsimd.memset(zeros[:], 0.0).then_inc(zeros_set, 1)
            pool.wait_ge(zeros_set, 1)
            for tail in tails:
                pool.dma_start(tail.rearrange("t p n -> p t n"),
                               zeros[:].unsqueeze(1).broadcast_to([P, tail.shape[0], D])).then_inc(tails_zeroed, 16)
            pool.wait_ge(tails_zeroed, 16 * len(tails))

        @block.tensor
        def _(pe):
            def score_for_top(b, h):
                n, at = b % DEEP, b * H + h
                if h == 0:
                    pe.wait_ge(loaded[n], 48 * (b // DEEP + 1))
                if at >= 2:
                    pe.wait_ge(top_found, at - 1)
                for half in range(2):
                    last = nc.tensor.matmul(ps_top[at % 2][:, half, :], q_in[n][0:STACK, head_columns(h, half)],
                                            k_in[n][0:STACK, head_columns(h)], start=True, stop=True)
                last.then_inc(top_scored, 1)

            def turn_tops(b, half):
                at = 2 * b + half
                pe.wait_ge(parts_cut, at + 1)
                if at >= 1:
                    pe.wait_ge(rows_kept, at)
                nc.tensor.transpose(ps_rows[0:PARTS * 2 * HALF, :], top_parts[:, half].rearrange("p i c -> p (i c)"),
                                    identity[:]).then_inc(rows_turned, 1)

            def score(b, h):
                n, at = b % DEEP, b * H + h
                if h % HALF == 0:
                    pe.wait_ge(rows_placed[h // HALF], 16 * PARTS * (b + 1))
                if at >= 3:
                    pe.wait_ge(prob_ready, at - 2)
                for half in range(2):
                    last = nc.tensor.matmul(ps_score[at % 3][:, half, :], k_in[n][0:ROWS, head_columns(h, half)],
                                            q_in[n][0:ROWS, head_columns(h)], start=True, stop=True)
                last.then_inc(scored, 1)

            def weigh(b, g):
                n = b % DEEP
                pe.wait_ge(prob_ready, b * H + 4 * g + 4)
                if b >= 1 and g % 2 == 0:
                    pe.wait_ge(out_kept, 2 * (b - 1) + g // 2 + 1)
                for half in range(2):
                    for j in range(4):
                        h = 4 * g + j
                        last = nc.tensor.matmul(ps_out[g // 2][32 * j:32 * j + VW, g % 2, :], v_in[n][:, half, h, :],
                                                prob[(b * H + h) % RING][:, half, :], start=half == 0, stop=half == 1,
                                                skip_group_check=True)
                last.then_inc(weighted, 1)

            pe.wait_ge(ones_set, 1)
            for h in range(H):
                score_for_top(0, h)
                if h == HALF + 1:
                    turn_tops(0, 0)
            turn_tops(0, 1)
            for b in range(B):
                for h in range(H):
                    score(b, h)
                    if b + 1 < B:
                        score_for_top(b + 1, h)
                    if h == 2 and b >= 1:
                        weigh(b - 1, 3)
                    if h in (5, 9, 13):
                        weigh(b, (h - 5) // 4)
                    if h == HALF + 2 and b + 1 < B:
                        turn_tops(b + 1, 0)
                if b + 1 < B:
                    turn_tops(b + 1, 1)
            weigh(B - 1, 3)

        @block.vector
        def _(dve):
            link = Link(dve, link_v)
            for n in range(DEEP):
                last = nc.vector.memset(k_in[n][:], 1.0)
            last.then_inc(ones_set, 1)
            for b in range(B):
                for h in range(H):
                    at = b * H + h
                    dve.wait_ge(top_scored, at + 1)
                    nc.vector.reduce_max(top[:, 2 * h:2 * h + 2], ps_top[at % 2][:], AX_X).then_inc(top_found, 1)
                    if h % HALF == HALF - 1:
                        half = h // HALF
                        dve.wait_ge(top_found, at + 1)
                        if b >= 1:
                            dve.wait_ge(rows_turned, 2 * b + half - 1)
                        tops = top[:, half * 2 * HALF:(half + 1) * 2 * HALF]
                        part, rest = top_parts[:, half], top_rest[:, half]
                        link(nc.vector.tensor_scalar(top_cut[:], tops, -1.0, None, ALU.mult))
                        link(nc.vector.tensor_copy(part[:, 0, :], top_cut[:]))
                        link(nc.vector.scalar_tensor_tensor(rest, tops, -1.0, part[:, 0, :], ALU.mult, ALU.subtract))
                        link(nc.vector.tensor_copy(top_cut[:], rest))
                        link(nc.vector.tensor_copy(part[:, 1, :], top_cut[:]))
                        nc.vector.tensor_tensor(part[:, 2, :], rest, part[:, 1, :], ALU.subtract).then_inc(parts_cut, 1)

        @block.scalar
        def _(act):
            def keep_rows(b, half):
                act.wait_ge(rows_turned, 2 * b + half + 1)
                if b >= 1:
                    act.wait_ge(rows_placed[half], 16 * PARTS * b)
                nc.scalar.activation(top_rows[half][:], ps_rows[0:PARTS * 2 * HALF, :], ACT.Copy).then_inc(rows_kept, 1)

            def keep_out(b, pair):
                act.wait_ge(weighted, 4 * b + 2 * pair + 2)
                if b >= 2:
                    act.wait_ge(stored[b % 2], 16 * (b // 2))
                nc.scalar.activation(out[b % 2][:, 2 * pair:2 * pair + 2, :], ps_out[pair][:], ACT.Copy).then_inc(out_kept, 1)

            keep_rows(0, 0)
            keep_rows(0, 1)
            for b in range(B):
                for h in range(H):
                    at = b * H + h
                    act.wait_ge(scored, at + 1)
                    if at >= RING:
                        act.wait_ge(weighted, (at - RING) // 4 + 1)
                    nc.scalar.activation(prob[at % RING][:], ps_score[at % 3][:], ACT.Exp, scale=scale).then_inc(prob_ready, 1)
                    if h == 4 and b >= 1:
                        keep_out(b - 1, 1)
                    if h == 11:
                        keep_out(b, 0)
                    if h == HALF + 3 and b + 1 < B:
                        keep_rows(b + 1, 0)
                if b + 1 < B:
                    keep_rows(b + 1, 1)
            keep_out(B - 1, 1)


class Kept:

    def __init__(self, s, layer):
        E, n = layer.experts, layer.name
        self.rank = s.sbuf(n + "rank", [P, B, E], F32)
        self.index = s.sbuf(n + "index", [P, B, 8], F32)
        self.weight = s.sbuf(n + "weight", [P, B, 8], F32)
        self.before = s.sbuf(n + "before", [P, E], BF16)
        self.first_row = s.sbuf(n + "first_row", [P, E], F32)


class Consts:

    def __init__(self, s):
        self.identity = s.sbuf("identity", [P, P], F32)
        self.earlier = s.sbuf("earlier", [P, P], BF16)
        self.ones = s.sbuf("ones", [P, P], BF16)
        self.ramp = s.sbuf("ramp", [P, P], F32)
        self.number = s.sbuf("number", [P, 1], F32)
        self.token = s.sbuf("token", [P, B], I32)


class Routing:

    def __init__(self, nc, s, layer, kept, consts, gate, gate_bias, table, normed_dram):
        self.nc, self.layer, self.kept, self.consts, self.gate, self.gate_bias = nc, layer, kept, consts, gate, gate_bias
        self.table, self.normed_dram = table, normed_dram
        E = layer.experts
        self.spare = 8 - layer.chosen
        self.stats = s.sbuf("r_stats", [P, 6], F32)
        self.mean_var = s.sbuf("r_mean_var", [P, 2], F32)
        self.root = s.sbuf("r_root", [P, 2], F32)
        self.x_norm = [s.sbuf(f"r_norm{n}", [P, D], F32) for n in range(2)]
        self.x_turned = s.sbuf("r_turned_sb", [P, 2, P], F32)
        self.logits = s.sbuf("r_logits", [P, E], F32)
        self.top = s.sbuf("r_top", [P, 8], F32)
        self.minus_top = s.sbuf("r_minus_top", [P, 1], F32)
        self.expo = s.sbuf("r_expo", [P, E], F32)
        self.total = s.sbuf("r_total", [P, 1], F32)
        self.share = s.sbuf("r_share", [P, 1], F32)
        self.probs = s.sbuf("r_probs", [P, E + self.spare], F32)
        self.taken = s.sbuf("r_taken", [P, E + self.spare], F32)
        self.best = s.sbuf("r_best", [P, 8], F32)
        self.picks = s.sbuf("r_picks", [P, 8], F32)
        self.index = s.sbuf("r_index", [P, 8], U32)
        self.mask = s.sbuf("r_mask", [P, E], BF16)
        self.junk = s.sbuf("r_junk", [P, E], F32)
        self.place = s.sbuf("r_place", [P, 8], F32)
        self.place_int = s.sbuf("r_place_int", [P, 8], I32)
        self.column = s.sbuf("r_column", [P, 8], I32)
        self.address = [s.sbuf(f"r_address{n}", [P, 8], I32) for n in range(2)]
        self.ps_turned = s.psum("r_ps_turned", [P, 2, P])
        self.ps_logits = s.psum("r_ps_logits", [P, E])
        self.ps_rank = s.psum("r_ps_rank", [P, E])
        self.normed = s.sem("r_normed")
        self.stored = [s.sem(f"r_stored{n}") for n in range(2)]
        self.turned = s.sem("r_turned")
        self.turned_kept = s.sem("r_turned_kept")
        self.scored = s.sem("r_scored")
        self.top_known = s.sem("r_top_known")
        self.expo_ready = s.sem("r_expo_ready")
        self.mask_ready = s.sem("r_mask_ready")
        self.ranked = s.sem("r_ranked")
        self.rank_kept = s.sem("r_rank_kept")
        self.places_ready = s.sem("r_places_ready")
        self.scattered = [s.sem(f"r_scattered{n}") for n in range(2)]

    def dve_normalise(self, dve, link, b, x):
        nc, n = self.nc, b % 2
        normalise_stats(nc, link, x, self.stats, self.mean_var)
        reciprocal_root(nc, link, self.mean_var, self.root)
        if b >= 2:
            dve.wait_ge(self.stored[n], 16 * (b // 2))
            dve.wait_ge(self.turned, b - 1)
        nc.vector.tensor_scalar(self.x_norm[n][:], x, self.mean_var[:, 0:1], self.root[:, 0:1],
                                ALU.subtract, ALU.mult).then_inc(self.normed, 1)

    def sp_store(self, sp, b):
        sp.wait_ge(self.normed, b + 1)
        sp.dma_start(self.normed_dram[b * P:(b + 1) * P, :], self.x_norm[b % 2][:]).then_inc(self.stored[b % 2], 16)

    def sp_finish(self, sp):
        for n in range(2):
            sp.wait_ge(self.stored[n], 16 * (B // 2))

    def pe_turn(self, pe, b):
        pe.wait_ge(self.normed, b + 1)
        if b >= 1:
            pe.wait_ge(self.turned_kept, b)
        for k in range(2):
            last = self.nc.tensor.transpose(self.ps_turned[:, k, :], self.x_norm[b % 2][:, k * P:(k + 1) * P],
                                            self.consts.identity[:])
        last.then_inc(self.turned, 1)

    def act_keep_turned(self, act, b):
        act.wait_ge(self.turned, b + 1)
        if b >= 1:
            act.wait_ge(self.scored, b)
        self.nc.scalar.activation(self.x_turned[:], self.ps_turned[:], ACT.Copy).then_inc(self.turned_kept, 1)

    def pe_score(self, pe, b):
        pe.wait_ge(self.turned_kept, b + 1)
        if b >= 1:
            pe.wait_ge(self.top_known, b)
        for k in range(2):
            last = self.nc.tensor.matmul(self.ps_logits[:], self.x_turned[:, k, :], self.gate[:, k, :],
                                         start=k == 0, stop=k == 1)
        last.then_inc(self.scored, 1)

    def dve_softmax_top(self, dve, link, b):
        nc = self.nc
        dve.wait_ge(self.scored, b + 1)
        if self.gate_bias is None:
            link(nc.vector.tensor_copy(self.logits[:], self.ps_logits[:]))
        else:
            link(nc.vector.tensor_tensor(self.logits[:], self.ps_logits[:], self.gate_bias[:], ALU.add))
        link(nc.vector.max(self.top[:], self.logits[:]))
        nc.vector.tensor_scalar(self.minus_top[:], self.top[:, 0:1], -1.0, None, ALU.mult).then_inc(self.top_known, 1)

    def act_exponentials(self, act, b):
        act.wait_ge(self.top_known, b + 1)
        self.nc.scalar.activation(self.expo[:], self.logits[:], ACT.Exp, bias=self.minus_top[:, 0:1],
                                  accum_out=self.total[:, 0:1]).then_inc(self.expo_ready, 1)

    def dve_choose(self, dve, link, b):
        nc, E, chosen = self.nc, self.layer.experts, self.layer.chosen
        weight = self.kept.weight
        if b == 0 and self.spare:
            link(nc.vector.memset(self.probs[:, E:], -1.0))
            link(nc.vector.memset(self.picks[:, chosen:], -1.0))
        dve.wait_ge(self.expo_ready, b + 1)
        link(nc.vector.reciprocal(self.share[:], self.total[:]))
        link(nc.vector.tensor_scalar(self.probs[:, 0:E], self.expo[:], self.share[:, 0:1], None, ALU.mult))
        link(nc.vector.max(self.best[:], self.probs[:, 0:E]))
        link(nc.vector.max_index(self.index[:], self.best[:], self.probs[:, 0:E]))
        link(nc.vector.tensor_copy(self.kept.index[:, b, :], self.index[:]))
        link(nc.vector.tensor_copy(self.picks[:, 0:chosen], self.best[:, 0:chosen]))
        link(nc.vector.match_replace(self.taken[:], self.picks[:], self.probs[:], -2.0))
        if b >= 1:
            dve.wait_ge(self.ranked, b)
        nc.vector.tensor_scalar(self.mask[:], self.taken[:, 0:E], -1.5, None, ALU.is_lt).then_inc(self.mask_ready, 1)
        if self.spare:
            link(nc.vector.reduce_sum(self.total[:], self.best[:, 0:chosen], AX_X))
            link(nc.vector.reciprocal(self.share[:], self.total[:]))
            link(nc.vector.tensor_scalar(weight[:, b, :], self.best[:], self.share[:, 0:1], None, ALU.mult))
        else:
            link(nc.vector.tensor_copy(weight[:, b, :], self.best[:]))

    def pe_rank(self, pe, b):
        pe.wait_ge(self.mask_ready, b + 1)
        if b >= 1:
            pe.wait_ge(self.rank_kept, 2 * b)
        last = self.nc.tensor.matmul(self.ps_rank[:], self.consts.earlier[:], self.mask[:], start=True, stop=b == 0)
        if b >= 1:
            last = self.nc.tensor.matmul(self.ps_rank[:], self.consts.ones[:], self.kept.before[:], start=False, stop=True)
        last.then_inc(self.ranked, 1)

    def dve_places(self, dve, link, b):
        nc, kept = self.nc, self.kept
        rank, index = kept.rank[:, b, :], kept.index[:, b, :]
        address = self.address[b % 2]
        dve.wait_ge(self.ranked, b + 1)
        nc.vector.tensor_copy(rank, self.ps_rank[:]).then_inc(self.rank_kept, 1)
        if b == 0:
            nc.vector.tensor_copy(kept.before[:], self.mask[:]).then_inc(self.rank_kept, 1)
        else:
            nc.vector.tensor_tensor(kept.before[:], kept.before[:], self.mask[:], ALU.add).then_inc(self.rank_kept, 1)
        dve.wait_ge(self.rank_kept, 2 * b + 2)
        own_rank(nc, link, self.layer, self.consts.ramp, index, rank, self.junk, self.place)
        link(nc.vector.scalar_tensor_tensor(self.place[:], index, float(TOKENS), self.place[:], ALU.mult, ALU.add))
        link(nc.vector.tensor_copy(self.place_int[:], self.place[:]))
        link(nc.vector.tensor_scalar(self.column[:], self.place_int[:], P.bit_length() - 1, None, ALU.logical_shift_right))
        link(nc.vector.tensor_scalar(self.place_int[:], self.place_int[:], P - 1, self.layer.columns.bit_length() - 1,
                                     ALU.bitwise_and, ALU.logical_shift_left))
        if b >= 2:
            dve.wait_ge(self.scattered[b % 2], 16 * self.layer.chosen * (b // 2))
        nc.vector.tensor_tensor(address[:], self.place_int[:], self.column[:], ALU.bitwise_or).then_inc(self.places_ready, 1)

    def pool_scatter(self, pool, b):
        pool.wait_ge(self.places_ready, b + 1)
        for k in range(self.layer.chosen):
            to = bass.IndirectOffsetOnAxis(ap=self.address[b % 2][:, k:k + 1], axis=0)
            self.nc.gpsimd.indirect_dma_start(self.table, to, self.consts.token[:, b:b + 1], None)\
                .then_inc(self.scattered[b % 2], 16)

    def pool_finish(self, pool):
        for n in range(2):
            pool.wait_ge(self.scattered[n], 16 * self.layer.chosen * (B // 2))


def own_rank(nc, link, layer, ramp, index, rank, junk, place):
    for k in range(8):
        if k < layer.chosen:
            nc_op = nc.vector.scalar_tensor_tensor(junk[:], ramp[:, 0:layer.experts], index[:, k:k + 1], rank,
                                                   ALU.is_equal, ALU.mult, accum_out=place[:, k:k + 1])
            link(nc_op)
    if layer.chosen < 8:
        link(nc.vector.memset(place[:, layer.chosen:], 0.0))


def setup_phase(nc, consts, consts_f, token_numbers, tables):
    with ExitStack() as stack:
        s = Space(nc, stack, "su_")
        loaded = s.sbuf("loaded", [P, 3, P], F32)
        zeros = s.sbuf("zeros", [P, LAYER0.columns], I32)
        arrived, made, zeroed = s.sem("arrived"), s.sem("made"), s.sem("zeroed")
        block = stack.enter_context(nc.Block())

        @block.sync
        def _(sp):
            sp.dma_start(loaded[:], consts_f).then_inc(arrived, 16)
            sp.dma_start(consts.token[:], token_numbers).then_inc(arrived, 16)
            sp.wait_ge(made, 1)
            for layer, table in tables:
                sp.dma_start(table.rearrange("(p c) a -> p (c a)", p=P), zeros[:, 0:layer.columns]).then_inc(zeroed, 16)
            sp.wait_ge(zeroed, 16 * len(tables))

        @block.vector
        def _(dve):
            nc.vector.memset(zeros[:], 0).then_inc(made, 1)
            dve.wait_ge(arrived, 32)
            nc.vector.tensor_copy(consts.identity[:], loaded[:, 0, :]).then_inc(made, 1)
            nc.vector.tensor_copy(consts.earlier[:], loaded[:, 1, :]).then_inc(made, 1)
            nc.vector.tensor_copy(consts.ramp[:], loaded[:, 2, :]).then_inc(made, 1)
            nc.vector.memset(consts.ones[:], 1.0).then_inc(made, 1)
            nc.vector.reduce_sum(consts.number[:], loaded[:, 1, :], AX_X).then_inc(made, 1)
            dve.wait_ge(made, 6)
            nc.vector.tensor_scalar(consts.number[:], consts.number[:], -1.0, float(P - 1), ALU.mult, ALU.add).then_inc(made, 1)
            dve.wait_ge(made, 7)


def merge_phase(nc, consts, kept, x, weights, biases, attended, gate_dram, x_out, table, normed_dram):
    layer = LAYER0
    with ExitStack() as stack:
        s = Space(nc, stack, "mg_")
        w = s.sbuf("w", [P, P], F32)
        bias = s.sbuf("bias", [P, 7], F32)
        gate = s.sbuf("gate", [P, 2, layer.experts], F32)
        sums_in = [s.sbuf(f"sums_in{n}", [P, 4, D], F32) for n in range(2)]
        x_in = [s.sbuf(f"x_in{n}", [P, D], F32) for n in range(2)]
        share = s.sbuf("share", [P, 2, 4, 4], F32)
        heads = s.sbuf("heads", [P, 2, P], F32)
        merged = s.sbuf("merged", [P, D], F32)
        x_new = [s.sbuf(f"x_new{n}", [P, D], F32) for n in range(2)]
        ps_sums = [s.psum(f"ps_sums{n}", [P, 4, P]) for n in range(2)]
        ps_heads = s.psum("ps_heads", [P, 2, P])
        ps_merged = s.psum("ps_merged", [P, D])
        routing = Routing(nc, s, layer, kept, consts, gate, None, table, normed_dram)
        weights_loaded, link_v = s.sem("weights_loaded"), s.sem("link_v")
        in_loaded = [s.sem(f"in_loaded{n}") for n in range(2)]
        x_stored = [s.sem(f"x_stored{n}") for n in range(2)]
        sums_turned, heads_ready, heads_turned, heads_kept, merged_ready, x_ready = (
            s.sem(n) for n in ("sums_turned", "heads_ready", "heads_turned", "heads_kept", "merged_ready", "x_ready"))
        block = stack.enter_context(nc.Block())

        @block.sync
        def _(sp):
            def load(b):
                n = b % 2
                if b >= 2:
                    sp.wait_ge(sums_turned, b - 1)
                sp.dma_start(sums_in[n][:], attended[b]).then_inc(in_loaded[n], 16)
                if b >= 2:
                    sp.wait_ge(x_ready, b - 1)
                sp.dma_start(x_in[n][:], x[b]).then_inc(in_loaded[n], 16)

            load(0)
            sp.dma_start(w[:], weights[:, 3, :]).then_inc(weights_loaded, 16)
            sp.dma_start(bias[:], biases).then_inc(weights_loaded, 16)
            sp.dma_start(gate[:], gate_dram).then_inc(weights_loaded, 16)
            load(1)
            for b in range(B + 1):
                if b < B:
                    sp.wait_ge(x_ready, b + 1)
                    sp.dma_start(x_out[b], x_new[b % 2][:]).then_inc(x_stored[b % 2], 16)
                    if b + 2 < B:
                        load(b + 2)
                if b >= 1:
                    routing.sp_store(sp, b - 1)
            for n in range(2):
                sp.wait_ge(x_stored[n], 16 * (B // 2))
            routing.sp_finish(sp)

        @block.tensor
        def _(pe):
            pe.wait_ge(weights_loaded, 48)
            for b in range(B + 1):
                n = b % 2
                if b < B:
                    pe.wait_ge(in_loaded[n], 32 * (b // 2 + 1))
                    if b >= 1:
                        pe.wait_ge(heads_ready, b)
                    for half in range(2):
                        for g in range(4):
                            last = nc.tensor.transpose(ps_sums[half][:, g, :], sums_in[n][:, g, half * P:(half + 1) * P],
                                                       consts.identity[:])
                    last.then_inc(sums_turned, 1)
                if b >= 1:
                    routing.pe_turn(pe, b - 1)
                if b < B:
                    pe.wait_ge(heads_ready, b + 1)
                    for half in range(2):
                        last = nc.tensor.transpose(ps_heads[:, half, :], heads[:, half, :], consts.identity[:])
                    last.then_inc(heads_turned, 1)
                if b >= 1:
                    routing.pe_score(pe, b - 1)
                if b < B:
                    pe.wait_ge(heads_kept, b + 1)
                    if b >= 1:
                        pe.wait_ge(x_ready, b)
                    nc.tensor.matmul(ps_merged[:], w[:], merged[:], start=True, stop=True).then_inc(merged_ready, 1)
                if b >= 1:
                    routing.pe_rank(pe, b - 1)

        @block.scalar
        def _(act):
            act.wait_ge(weights_loaded, 48)
            for b in range(B + 1):
                if b >= 1:
                    routing.act_keep_turned(act, b - 1)
                if b < B:
                    act.wait_ge(heads_turned, b + 1)
                    if b >= 1:
                        act.wait_ge(merged_ready, b)
                    nc.scalar.activation(merged[:], ps_heads[:].rearrange("p a n -> p (a n)"), ACT.Identity,
                                         bias=bias[:, 2:3]).then_inc(heads_kept, 1)
                if b >= 1:
                    routing.act_exponentials(act, b - 1)

        @block.vector
        def _(dve):
            link = Link(dve, link_v)
            dve.wait_ge(weights_loaded, 48)
            for b in range(B + 1):
                n = b % 2
                if b >= 1:
                    dve.wait_ge(x_ready, b)
                    routing.dve_normalise(dve, link, b - 1, x_new[(b - 1) % 2][:])
                if b < B:
                    dve.wait_ge(sums_turned, b + 1)
                    sums = [ps_sums[half][:].rearrange("p g (j v) -> p g j v", v=VW) for half in range(2)]
                    for half in range(2):
                        link(nc.vector.reciprocal(share[:, half], sums[half][:, :, :, HD]))
                    if b >= 1:
                        dve.wait_ge(heads_turned, b)
                    for half in range(2):
                        to = heads[:, half, :].rearrange("p (d g j) -> p g j d", g=4, j=4)
                        last = nc.vector.tensor_tensor(to, sums[half][:, :, :, 0:HD],
                                                       share[:, half].unsqueeze(3).broadcast_to([P, 4, 4, HD]), ALU.mult)
                    last.then_inc(heads_ready, 1)
                if b >= 1:
                    routing.dve_softmax_top(dve, link, b - 1)
                if b < B:
                    dve.wait_ge(merged_ready, b + 1)
                    dve.wait_ge(in_loaded[n], 32 * (b // 2 + 1))
                    if b >= 2:
                        dve.wait_ge(x_stored[n], 16 * (b // 2))
                    nc.vector.scalar_tensor_tensor(x_new[n][:], ps_merged[:], bias[:, 3:4], x_in[n][:],
                                                   ALU.add, ALU.add).then_inc(x_ready, 1)
                if b >= 1:
                    routing.dve_choose(dve, link, b - 1)
                    routing.dve_places(dve, link, b - 1)

        @block.gpsimd
        def _(pool):
            for b in range(B):
                routing.pool_scatter(pool, b)
            routing.pool_finish(pool)


def tiles_phase(nc, layer, consts, kept, table, normed_dram, up_dram, down_dram, rows_out):
    with ExitStack() as stack:
        s = Space(nc, stack, layer.name)
        E, U, C, W = layer.experts, layer.unroll, layer.chunks, layer.width
        lists = s.sbuf("lists", [P, layer.columns], I32)
        tile_column = s.sbuf("tile_column", [1, P], I32)
        tile_expert = s.sbuf("tile_expert", [1, P], I32)
        last_group_at = s.sbuf("last_group_at", [1, 1], I32)
        lists_loaded = s.sem("lists_loaded")
        plan_tiles(nc, s, layer, consts, kept, table, lists, lists_loaded, tile_column, tile_expert, last_group_at)

        up_w = [s.sbuf(f"up_w{u}", [P, 2, 2 * layer.inter], F32) for u in range(U)]
        down_w = [s.sbuf(f"down_w{u}", [W, C, D], F32) for u in range(U)]
        column = [s.sbuf(f"column{u}", [P, 1], I32) for u in range(U)]
        rows = [s.sbuf(f"rows{u}", [P, D], F32) for u in range(U)]
        out = [s.sbuf(f"out{u}", [P, D], F32) for u in range(U)]
        x_turned = [s.sbuf(f"x_turned{n}", [P, 2, P], F32) for n in range(2)]
        silu = [s.sbuf(f"silu{n}", [W, C * P], F32) for n in range(2)]
        inner = [s.sbuf(f"inner{n}", [W, C * P], F32) for n in range(2)]
        ps_x = [s.psum(f"ps_x{n}", [P, 2, P]) for n in range(2)]
        ps_up = [s.psum(f"ps_up{n}", [W, 2, C * P]) for n in range(2)]
        ps_out = [s.psum(f"ps_out{n}", [P, D]) for n in range(2)]
        weights_loaded = [s.sem(f"weights_loaded{u}") for u in range(U)]
        gathered = [s.sem(f"gathered{u}") for u in range(U)]
        stored = [s.sem(f"stored{u}") for u in range(U)]
        column_copied, parted, turned, turned_kept, up_done, silu_done, inner_ready, down_done, out_kept = (
            s.sem(n) for n in ("column_copied", "parted", "turned", "turned_kept", "up_done", "silu_done",
                               "inner_ready", "down_done", "out_kept"))
        block = stack.enter_context(nc.Block())
        most_groups = layer.tiles // U

        def groups(engine):
            return engine.value_load(last_group_at[0:1, 0:1], min_val=1, max_val=most_groups - 1)

        def apart(engine):
            engine.sem_inc(parted, 1)

        @block.sync
        def _(sp):
            last = groups(sp)

            def load(i, u):
                e = sp.value_load(tile_expert[0:1, bass.ds(i * U + u, 1)], min_val=0, max_val=E - 1)
                sp.dma_start(up_w[u][:], up_dram[bass.ds(e, 1)].rearrange("a p k n -> (a p) k n")).then_inc(weights_loaded[u], 16)
                sp.dma_start(down_w[u][:], down_dram[bass.ds(e, 1)].rearrange("a p k n -> (a p) k n")).then_inc(weights_loaded[u], 16)

            for u in range(U):
                load(0, u)
            with sp.Fori(1, last + 1) as i:
                for u in range(U):
                    sp.wait_ge(down_done, i * U + u - U + 1)
                    load(i, u)

        @block.gpsimd
        def _(pool):
            last = groups(pool)

            def gather(i, u):
                c = pool.value_load(tile_column[0:1, bass.ds(i * U + u, 1)], min_val=0, max_val=layer.columns - 1)
                nc.gpsimd.tensor_copy(column[u][:], lists[:, bass.ds(c, 1)]).then_inc(column_copied, 1)
                pool.wait_ge(column_copied, i * U + u + 1)
                apart(pool)
                nc.gpsimd.indirect_dma_start(rows[u][:], None, normed_dram, bass.IndirectOffsetOnAxis(ap=column[u][:], axis=0))\
                    .then_inc(gathered[u], 16)

            for u in range(U):
                gather(0, u)
            with pool.Fori(1, last + 1) as i:
                for u in range(U):
                    pool.wait_ge(turned, i * U + u - U + 1)
                    gather(i, u)

        @block.tensor
        def _(pe):
            last = groups(pe)

            def down(t, u):
                pe.wait_ge(inner_ready, t + 1)
                for c in range(C):
                    op = nc.tensor.matmul(ps_out[u % 2][:], inner[u % 2][:, c * P:(c + 1) * P], down_w[u][:, c, :],
                                          start=c == 0, stop=c == C - 1)
                op.then_inc(down_done, 1)

            def step(i, u, first=False):
                t = i * U + u
                pe.wait_ge(gathered[u], i * 16 + 16)
                for k in range(2):
                    op = nc.tensor.transpose(ps_x[u % 2][:, k, :], rows[u][:, k * P:(k + 1) * P], consts.identity[:])
                op.then_inc(turned, 1)
                if not (first and u < 2):
                    down(t - 2, (u - 2) % U)
                pe.wait_ge(turned_kept, t + 1)
                pe.wait_ge(weights_loaded[u], i * 32 + 32)
                for part in range(2):
                    for c in range(C):
                        at = (part * C + c) * W
                        for k in range(2):
                            op = nc.tensor.matmul(ps_up[u % 2][:, part, c * P:(c + 1) * P], up_w[u][:, k, at:at + W],
                                                  x_turned[u % 2][:, k, :], start=k == 0, stop=k == 1)
                op.then_inc(up_done, 1)

            for u in range(U):
                step(0, u, True)
            with pe.Fori(1, last + 1) as i:
                for u in range(U):
                    step(i, u)
            down(last * U + U - 2, U - 2)
            down(last * U + U - 1, U - 1)

        @block.scalar
        def _(act):
            last = groups(act)

            def store(i, u):
                act.wait_ge(out_kept, i * U + u + 1)
                act.dma_start(rows_out[bass.ds(i * U + u, 1)].rearrange("a p n -> (a p) n"), out[u][:]).then_inc(stored[u], 16)

            def step(i, u, first=False):
                t = i * U + u
                act.wait_ge(turned, t + 1)
                nc.scalar.activation(x_turned[u % 2][:], ps_x[u % 2][:], ACT.Copy).then_inc(turned_kept, 1)
                act.wait_ge(up_done, t + 1)
                nc.scalar.activation(silu[u % 2][:], ps_up[u % 2][:, 0, :], ACT.Silu).then_inc(silu_done, 1)
                if not (first and u < 2):
                    store(i if u >= 2 else i - 1, (u - 2) % U)

            for u in range(U):
                step(0, u, True)
            with act.Fori(1, last + 1) as i:
                for u in range(U):
                    step(i, u)
            store(last, U - 2)
            store(last, U - 1)
            for u in range(U):
                act.wait_ge(stored[u], last * 16 + 32)
                apart(act)

        @block.vector
        def _(dve):
            last = groups(dve)
            for u in range(U):
                dve.sem_inc(stored[u], 16)

            def keep(i, u):
                dve.wait_ge(stored[u], i * 16 + 16)
                dve.wait_ge(down_done, i * U + u + 1)
                nc.vector.tensor_copy(out[u][:], ps_out[u % 2][:]).then_inc(out_kept, 1)

            def step(i, u, first=False):
                if not (first and u < 2):
                    keep(i if u >= 2 else i - 1, (u - 2) % U)
                dve.wait_ge(silu_done, i * U + u + 1)
                nc.vector.tensor_tensor(inner[u % 2][:], silu[u % 2][:], ps_up[u % 2][:, 1, :], ALU.mult).then_inc(inner_ready, 1)

            for u in range(U):
                step(0, u, True)
            with dve.Fori(1, last + 1) as i:
                for u in range(U):
                    step(i, u)
            keep(last, U - 2)
            keep(last, U - 1)


def plan_tiles(nc, s, layer, consts, kept, table, lists, lists_loaded, tile_column, tile_expert, last_group_at):
    with ExitStack() as stack:
        s = Space(nc, stack, layer.name + "plan_")
        E, U = layer.experts, layer.unroll
        count = s.sbuf("count", [P, E], I32)
        tiles = s.sbuf("tiles", [P, E], F32)
        ends = [s.sbuf(f"ends{n}", [P, E], F32) for n in range(2)]
        junk = s.sbuf("junk", [P, E], F32)
        groups = s.sbuf("groups", [P, P], F32)
        own = s.sbuf("own", [P, 8], F32)
        done_experts, done_tiles, expert, col = own[:, 0:1], own[:, 1:2], own[:, 2:3], own[:, 3:4]
        last_group = own[:, 4:5]
        ps_count = s.psum("ps_count", [P, E])
        ps_row = s.psum("ps_row", [P, 2, P])
        counted, own_ready, rows_ready, link_v = (s.sem(n) for n in ("counted", "own_ready", "rows_ready", "link_v"))
        block = stack.enter_context(nc.Block())

        @block.sync
        def _(sp):
            sp.dma_start(lists[:], table.rearrange("(p c) a -> p (c a)", p=P)).then_inc(lists_loaded, 16)
            sp.wait_ge(lists_loaded, 16)

        @block.tensor
        def _(pe):
            nc.tensor.matmul(ps_count[:], consts.ones[:], kept.before[:], start=True, stop=True).then_inc(counted, 1)
            pe.wait_ge(own_ready, 1)
            nc.tensor.transpose(ps_row[0:1, 0, :], col, consts.identity[:])
            nc.tensor.transpose(ps_row[0:1, 1, :], expert, consts.identity[:]).then_inc(rows_ready, 1)

        @block.vector
        def _(dve):
            link = Link(dve, link_v)
            dve.wait_ge(counted, 1)
            link(nc.vector.tensor_scalar(count[:], ps_count[:], float(P - 1), None, ALU.add))
            link(nc.vector.tensor_scalar(count[:], count[:], P.bit_length() - 1, None, ALU.logical_shift_right))
            link(nc.vector.tensor_copy(tiles[:], count[:]))
            link(nc.vector.tensor_copy(ends[0][:], tiles[:]))
            n, step = 0, 1
            while step < E:
                link(nc.vector.tensor_copy(ends[1 - n][:, 0:step], ends[n][:, 0:step]))
                link(nc.vector.tensor_tensor(ends[1 - n][:, step:], ends[n][:, step:], ends[n][:, 0:E - step], ALU.add))
                n, step = 1 - n, 2 * step
            end = ends[n]
            link(nc.vector.tensor_tensor(kept.first_row[:], end[:], tiles[:], ALU.subtract))
            link(nc.vector.tensor_scalar(kept.first_row[:], kept.first_row[:], float(P), None, ALU.mult))
            link(nc.vector.tensor_scalar(junk[:], end[:], consts.number[:, 0:1], None, ALU.is_le, ALU.add,
                                         accum_out=done_experts))
            link(nc.vector.scalar_tensor_tensor(junk[:], end[:], consts.number[:, 0:1], tiles[:], ALU.is_le, ALU.mult,
                                                accum_out=done_tiles))
            link(nc.vector.tensor_scalar(expert, done_experts, float(E - 1), None, ALU.min))
            link(nc.vector.scalar_tensor_tensor(col, expert, float(layer.lists), consts.number[:, 0:1], ALU.mult, ALU.add))
            link(nc.vector.tensor_tensor(col, col, done_tiles, ALU.subtract))
            link(nc.vector.tensor_scalar(col, col, float(layer.columns - 1), None, ALU.min))
            nc.vector.engine_nop().then_inc(own_ready, 1)
            most = layer.tiles // U
            link(nc.vector.tensor_scalar(groups[:, 0:most], consts.ramp[:, 0:most], float(U), float(U + 1), ALU.mult, ALU.add))
            link(nc.vector.tensor_scalar(junk[:, 0:most], groups[:, 0:most], end[:, E - 1:E], None, ALU.is_le, ALU.add,
                                         accum_out=last_group))
            link(nc.vector.tensor_copy(last_group_at[:], last_group[0:1, :]))
            dve.wait_ge(rows_ready, 1)
            link(nc.vector.tensor_copy(tile_column[:], ps_row[0:1, 0, :]))
            link(nc.vector.tensor_copy(tile_expert[:], ps_row[0:1, 1, :]))


class Gather:

    def __init__(self, nc, s, layer, kept, consts, rows_dram):
        self.nc, self.layer, self.kept, self.consts = nc, layer, kept, consts
        self.rows_dram = rows_dram.rearrange("t p n -> (t p) n")
        E = layer.experts
        self.rank = s.sbuf("g_rank", [P, E], F32)
        self.junk = s.sbuf("g_junk", [P, E], F32)
        self.place = s.sbuf("g_place", [P, 8], F32)
        self.row = [s.sbuf(f"g_row{n}", [P, 8], I32) for n in range(2)]
        self.rows = [s.sbuf(f"g_rows{n}", [P, layer.chosen, D], F32) for n in range(2)]
        self.rows_known = s.sem("g_rows_known")
        self.gathered = [s.sem(f"g_gathered{n}") for n in range(2)]
        self.summed = s.sem("g_summed")

    def dve_rows(self, dve, link, b):
        nc, n, kept = self.nc, b % 2, self.kept
        link(nc.vector.tensor_tensor(self.rank[:], kept.rank[:, b, :], kept.first_row[:], ALU.add))
        own_rank(nc, link, self.layer, self.consts.ramp, kept.index[:, b, :], self.rank[:], self.junk, self.place)
        if b >= 2:
            dve.wait_ge(self.gathered[n], 16 * self.layer.chosen * (b // 2))
        nc.vector.tensor_copy(self.row[n][:], self.place[:]).then_inc(self.rows_known, 1)

    def pool_gather(self, pool, b):
        n = b % 2
        pool.wait_ge(self.rows_known, b + 1)
        if b >= 2:
            pool.wait_ge(self.summed, b - 1)
        for k in range(self.layer.chosen):
            of = bass.IndirectOffsetOnAxis(ap=self.row[n][:, k:k + 1], axis=0)
            self.nc.gpsimd.indirect_dma_start(self.rows[n][:, k, :], None, self.rows_dram, of)\
                .then_inc(self.gathered[n], 16)

    def dve_sum(self, dve, link, b, x, out):
        nc, n, last = self.nc, b % 2, self.layer.chosen - 1
        dve.wait_ge(self.gathered[n], 16 * self.layer.chosen * (b // 2 + 1))
        for k in range(last + 1):
            op = nc.vector.scalar_tensor_tensor(out, self.rows[n][:, k, :], self.kept.weight[:, b, k:k + 1], x if k == 0 else out,
                                                ALU.mult, ALU.add)
            if k < last:
                link(op)
        op.then_inc(self.summed, 1)


def features_phase(nc, consts, kept0, kept1, x, ctx, ctx_turned, rows_dram, gate_dram, gate_bias_dram, x_out, table, normed_dram):
    layer = LAYER1
    scale = 1.0 / float(np.sqrt(D))
    with ExitStack() as stack:
        s = Space(nc, stack, "ft_")
        gate = s.sbuf("gate", [P, 2, layer.experts], F32)
        gate_bias = s.sbuf("gate_bias", [P, layer.experts], F32)
        x_in = [s.sbuf(f"x_in{n}", [P, D], F32) for n in range(2)]
        keys = [s.sbuf(f"keys{n}", [P, D], F32) for n in range(2)]
        vals = [s.sbuf(f"vals{n}", [P, 2, P], F32) for n in range(2)]
        x_sum = [s.sbuf(f"x_sum{n}", [P, D], F32) for n in range(2)]
        stats = s.sbuf("stats", [P, 6], F32)
        mean_var = s.sbuf("mean_var", [P, 2], F32)
        root = s.sbuf("root", [P, 2], F32)
        x_norm = s.sbuf("x_norm", [P, D], F32)
        top = s.sbuf("top", [P, 2], F32)
        minus_top = s.sbuf("minus_top", [P, 2], F32)
        expo = s.sbuf("expo", [P, 2, D], F32)
        total = s.sbuf("total", [P, 2], F32)
        share = s.sbuf("share", [P, 2], F32)
        vals_shared = s.sbuf("vals_shared", [P, 2, P], F32)
        x_new = [s.sbuf(f"x_new{n}", [P, D], F32) for n in range(2)]
        ps_scores = s.psum("ps_scores", [P, 2, D])
        ps_out = s.psum("ps_out", [P, D])
        gather = Gather(nc, s, LAYER0, kept0, consts, rows_dram)
        routing = Routing(nc, s, layer, kept1, consts, gate, gate_bias, table, normed_dram)
        gates_loaded, link_v = s.sem("gates_loaded"), s.sem("link_v")
        in_loaded = [s.sem(f"in_loaded{n}") for n in range(2)]
        x_stored = [s.sem(f"x_stored{n}") for n in range(2)]
        normed, scored, top_known, expo_ready, vals_ready, attended, x_ready = (
            s.sem(n) for n in ("normed", "scored", "top_known", "expo_ready", "vals_ready", "attended", "x_ready"))
        block = stack.enter_context(nc.Block())

        @block.sync
        def _(sp):
            def load(b):
                n = b % 2
                if b >= 2:
                    sp.wait_ge(attended, b - 1)
                sp.dma_start(x_in[n][:], x[b]).then_inc(in_loaded[n], 16)
                sp.dma_start(keys[n][:], ctx[b]).then_inc(in_loaded[n], 16)
                sp.dma_start(vals[n][:], ctx_turned[b]).then_inc(in_loaded[n], 16)

            sp.dma_start(gate[:], gate_dram).then_inc(gates_loaded, 16)
            sp.dma_start(gate_bias[:], gate_bias_dram).then_inc(gates_loaded, 16)
            load(0)
            load(1)
            for b in range(B + 1):
                if b < B:
                    sp.wait_ge(x_ready, b + 1)
                    sp.dma_start(x_out[b], x_new[b % 2][:]).then_inc(x_stored[b % 2], 16)
                    if b + 2 < B:
                        load(b + 2)
                if b >= 1:
                    routing.sp_store(sp, b - 1)
            for n in range(2):
                sp.wait_ge(x_stored[n], 16 * (B // 2))
            routing.sp_finish(sp)

        @block.gpsimd
        def _(pool):
            gather.pool_gather(pool, 0)
            gather.pool_gather(pool, 1)
            for b in range(B):
                if b + 2 < B:
                    gather.pool_gather(pool, b + 2)
                routing.pool_scatter(pool, b)
            routing.pool_finish(pool)

        @block.tensor
        def _(pe):
            pe.wait_ge(gates_loaded, 32)
            for b in range(B + 1):
                n = b % 2
                if b < B:
                    pe.wait_ge(in_loaded[n], 48 * (b // 2 + 1))
                    pe.wait_ge(normed, b + 1)
                    if b >= 1:
                        pe.wait_ge(expo_ready, b)
                    for c in range(2):
                        op = nc.tensor.matmul(ps_scores[:, c, :], keys[n][:, c * P:(c + 1) * P], x_norm[:], start=True, stop=True)
                    op.then_inc(scored, 1)
                if b >= 1:
                    routing.pe_turn(pe, b - 1)
                    routing.pe_score(pe, b - 1)
                if b < B:
                    pe.wait_ge(vals_ready, b + 1)
                    if b >= 1:
                        pe.wait_ge(x_ready, b)
                    for c in range(2):
                        op = nc.tensor.matmul(ps_out[:], vals_shared[:, c, :], expo[:, c, :], start=c == 0, stop=c == 1)
                    op.then_inc(attended, 1)
                if b >= 1:
                    routing.pe_rank(pe, b - 1)

        @block.scalar
        def _(act):
            for b in range(B + 1):
                if b >= 1:
                    routing.act_keep_turned(act, b - 1)
                if b < B:
                    act.wait_ge(top_known, b + 1)
                    if b >= 1:
                        act.wait_ge(attended, b)
                    for c in range(2):
                        op = nc.scalar.activation(expo[:, c, :], ps_scores[:, c, :], ACT.Exp, bias=minus_top[:, c:c + 1],
                                                  scale=scale, accum_out=total[:, c:c + 1])
                    op.then_inc(expo_ready, 1)
                if b >= 1:
                    routing.act_exponentials(act, b - 1)

        @block.vector
        def _(dve):
            link = Link(dve, link_v)
            dve.wait_ge(gates_loaded, 32)
            gather.dve_rows(dve, link, 0)
            gather.dve_rows(dve, link, 1)
            for b in range(B + 1):
                n = b % 2
                if b < B:
                    dve.wait_ge(in_loaded[n], 48 * (b // 2 + 1))
                    if b >= 2:
                        dve.wait_ge(x_ready, b - 1)
                    gather.dve_sum(dve, link, b, x_in[n][:], x_sum[n][:])
                    dve.wait_ge(gather.summed, b + 1)
                    normalise_stats(nc, link, x_sum[n][:], stats, mean_var)
                    reciprocal_root(nc, link, mean_var, root)
                    if b >= 1:
                        dve.wait_ge(scored, b)
                    nc.vector.tensor_scalar(x_norm[:], x_sum[n][:], mean_var[:, 0:1], root[:, 0:1],
                                            ALU.subtract, ALU.mult).then_inc(normed, 1)
                if b >= 1:
                    dve.wait_ge(x_ready, b)
                    routing.dve_normalise(dve, link, b - 1, x_new[(b - 1) % 2][:])
                if b < B:
                    dve.wait_ge(scored, b + 1)
                    link(nc.vector.reduce_max(top[:], ps_scores[:], AX_X))
                    nc.vector.tensor_scalar(minus_top[:], top[:], -scale, None, ALU.mult).then_inc(top_known, 1)
                if b >= 1:
                    routing.dve_softmax_top(dve, link, b - 1)
                if b < B:
                    dve.wait_ge(expo_ready, b + 1)
                    link(nc.vector.reciprocal(share[:], total[:]))
                    for c in range(2):
                        op = nc.vector.tensor_scalar(vals_shared[:, c, :], vals[n][:, c, :], share[:, c:c + 1], None, ALU.mult)
                    op.then_inc(vals_ready, 1)
                if b >= 1:
                    routing.dve_choose(dve, link, b - 1)
                if b < B:
                    dve.wait_ge(attended, b + 1)
                    if b >= 2:
                        dve.wait_ge(x_stored[n], 16 * (b // 2))
                    nc.vector.tensor_tensor(x_new[n][:], x_sum[n][:], ps_out[:], ALU.add).then_inc(x_ready, 1)
                if b >= 1:
                    routing.dve_places(dve, link, b - 1)
                if b + 2 < B:
                    gather.dve_rows(dve, link, b + 2)


def last_phase(nc, consts, kept, x, rows_dram, out):
    with ExitStack() as stack:
        s = Space(nc, stack, "ls_")
        x_in = [s.sbuf(f"x_in{n}", [P, D], F32) for n in range(2)]
        x_sum = [s.sbuf(f"x_sum{n}", [P, D], F32) for n in range(2)]
        gather = Gather(nc, s, LAYER1, kept, consts, rows_dram)
        link_v = s.sem("link_v")
        in_loaded = [s.sem(f"in_loaded{n}") for n in range(2)]
        stored = [s.sem(f"stored{n}") for n in range(2)]
        block = stack.enter_context(nc.Block())

        @block.sync
        def _(sp):
            for b in range(2):
                sp.dma_start(x_in[b][:], x[b]).then_inc(in_loaded[b], 16)
            for b in range(B):
                n = b % 2
                sp.wait_ge(gather.summed, b + 1)
                sp.dma_start(out[b], x_sum[n][:]).then_inc(stored[n], 16)
                if b + 2 < B:
                    sp.dma_start(x_in[n][:], x[b + 2]).then_inc(in_loaded[n], 16)
            for n in range(2):
                sp.wait_ge(stored[n], 16 * (B // 2))

        @block.gpsimd
        def _(pool):
            for b in range(B):
                gather.pool_gather(pool, b)

        @block.vector
        def _(dve):
            link = Link(dve, link_v)
            gather.dve_rows(dve, link, 0)
            gather.dve_rows(dve, link, 1)
            for b in range(B):
                n = b % 2
                dve.wait_ge(in_loaded[n], 16 * (b // 2 + 1))
                if b >= 2:
                    dve.wait_ge(stored[n], 16 * (b // 2))
                gather.dve_sum(dve, link, b, x_in[n][:], x_sum[n][:])
                if b + 2 < B:
                    gather.dve_rows(dve, link, b + 2)


def two_layers(nc, x, ctx, ctx_turned, consts_f, token_numbers, weights, biases, rotary, gate0, up0, down0,
               gate1, gate1_bias, up1, down1, out):
    def scratch(name, shape, dtype=F32):
        return nc.dram_tensor(name, shape, dtype, kind="Internal").ap()

    q_stack = scratch("q_stack", [B, TERMS, P, D], BF16)
    k_stack = scratch("k_stack", [B, TERMS, P, D], BF16)
    values = scratch("values", [B, P, 2, H, VW])
    attended = scratch("attended", [B, P, 4, D])
    x_mid = [scratch(f"x_mid{n}", [B, P, D]) for n in range(2)]
    normed = [scratch(f"normed{n}", [TOKENS, D]) for n in range(2)]
    tables = [scratch(f"table{n}", [P * layer.columns, 1], I32) for n, layer in enumerate((LAYER0, LAYER1))]
    rows = [scratch(f"rows{n}", [layer.tiles, P, D]) for n, layer in enumerate((LAYER0, LAYER1))]
    with ExitStack() as stack:
        s = Space(nc, stack, "")
        consts, kept0, kept1 = Consts(s), Kept(s, LAYER0), Kept(s, LAYER1)
        setup_phase(nc, consts, consts_f, token_numbers, [(LAYER0, tables[0]), (LAYER1, tables[1])])
        project_phase(nc, x, ctx, weights, biases, rotary, q_stack, k_stack, values)
        attend_phase(nc, consts.identity, q_stack, k_stack, values, attended,
                     [to[layer.least:] for layer, to in zip((LAYER0, LAYER1), rows)])
        merge_phase(nc, consts, kept0, x, weights, biases, attended, gate0, x_mid[0], tables[0], normed[0])
        tiles_phase(nc, LAYER0, consts, kept0, tables[0], normed[0], up0, down0, rows[0])
        features_phase(nc, consts, kept0, kept1, x_mid[0], ctx, ctx_turned, rows[0], gate1, gate1_bias, x_mid[1],
                       tables[1], normed[1])
        tiles_phase(nc, LAYER1, consts, kept1, tables[1], normed[1], up1, down1, rows[1])
        last_phase(nc, consts, kept1, x_mid[1], rows[1], out)


def laid_out(x, ctx_2048, L0_xattn_encoding, L0_xattn_Wq, L0_xattn_bq, L0_xattn_Wk, L0_xattn_bk, L0_xattn_Wv,
             L0_xattn_bv, L0_xattn_Wm, L0_xattn_bm, L0_ffn_gate_w, L0_ffn_w13, L0_ffn_w2, L1_ffn_router_w,
             L1_ffn_expert_bias, L1_ffn_gate_proj, L1_ffn_up_proj, L1_ffn_down_proj):
    at = np.arange(P)
    identity = np.eye(P, dtype=np.float32)
    earlier = (at[:, None] < at[None, :]).astype(np.float32)
    ramp = np.broadcast_to(at.astype(np.float32), (P, P))
    sign = np.where(at // H % 2 == 0, -1.0, 1.0).astype(np.float32)
    swap = at ^ H
    bq, bk = L0_xattn_bq, L0_xattn_bk
    rotary = np.repeat(L0_xattn_encoding[:, 0, 0].transpose(2, 0, 1), H, axis=0)

    def by_contraction(w):
        return w.reshape(w.shape[0], 2, P, -1).transpose(0, 2, 1, 3)

    def gates(w):
        return w.T.reshape(2, P, -1).transpose(1, 0, 2)

    up1 = np.concatenate([L1_ffn_gate_proj, L1_ffn_up_proj], axis=2)
    return {
        "x": x,
        "ctx": ctx_2048,
        "ctx_turned": ctx_2048.transpose(0, 2, 1).reshape(B, 2, P, P).transpose(0, 2, 1, 3),
        "consts_f": np.stack([identity, earlier, ramp], axis=1),
        "token_numbers": (at[:, None] + P * np.arange(B)[None, :]).astype(np.int32),
        "weights": np.stack([w.T for w in (L0_xattn_Wq, L0_xattn_Wk, L0_xattn_Wv, L0_xattn_Wm)], axis=1),
        "biases": np.stack([bq, bk, L0_xattn_bv, L0_xattn_bm, bq[swap], bk[swap], sign], axis=1),
        "rotary": rotary,
        "gate0": gates(L0_ffn_gate_w),
        "up0": by_contraction(L0_ffn_w13.transpose(0, 2, 1)),
        "down0": L0_ffn_w2.transpose(0, 2, 1).reshape(LAYER0.experts, 1, P, D).transpose(0, 2, 1, 3),
        "gate1": gates(L1_ffn_router_w),
        "gate1_bias": np.broadcast_to(L1_ffn_expert_bias, (P, LAYER1.experts)),
        "up1": by_contraction(up1),
        "down1": L1_ffn_down_proj.reshape(LAYER1.experts, LAYER1.chunks, LAYER1.width, D).transpose(0, 2, 1, 3),
    }


def kernel(**inputs):
    import concourse.bacc as bacc
    from concourse.bass_utils import run_bass_kernel_spmd

    nc = bacc.Bacc("TRN2", target_bir_lowering=False, num_devices=1)
    arrays, args = {}, []
    for name, a in laid_out(**{k: np.asarray(v) for k, v in inputs.items()}).items():
        a = np.ascontiguousarray(a)
        arrays["in_" + name] = a
        args.append(nc.dram_tensor("in_" + name, a.shape, mybir.dt.from_np(a.dtype), kind="ExternalInput").ap())
    out = nc.dram_tensor("out", (B, P, D), F32, kind="ExternalOutput").ap()
    two_layers(nc, *args, out)
    result = run_bass_kernel_spmd(nc, [arrays], core_ids=[0])
    return result.results[0]["out"]
```

```python
from contextlib import ExitStack

import numpy as np

import concourse.bass as bass
from concourse import mybir

P = 128
B = 8
D = 256
TOKENS = B * P
H = 16
HD = P // H
EPS = 1e-5
NEWTON = 3
GROUPS = ((0, 1), (2, 3, 4), (5, 6, 7))
MOST = max(len(g) for g in GROUPS)
WARM_UP = 24
PARTS = 3
TERMS = 6
STACK = TERMS * HD
TOP = 96
ROWS = TOP + PARTS
DEEP = 4
ONES_PAIR = float(np.array([0x3F803F80], np.uint32).view(np.float32)[0])
VW = 32

F32 = mybir.dt.float32
BF16 = mybir.dt.bfloat16
I32 = mybir.dt.int32
U32 = mybir.dt.uint32
ALU = mybir.AluOpType
ACT = mybir.ActivationFunctionType
AX_X = mybir.AxisListType.X


class Layer:

    def __init__(self, name, experts, chosen, inter, unroll):
        self.name, self.experts, self.chosen, self.inter, self.unroll = name, experts, chosen, inter, unroll
        self.chunks = -(-inter // P)
        self.width = inter // self.chunks
        self.lists = TOKENS // P
        self.columns = experts * self.lists
        most = TOKENS * chosen // P + experts - 1
        self.tiles = -(-most // unroll) * unroll
        self.least = TOKENS * chosen // P
        assert self.width * self.chunks == inter and self.tiles <= P


LAYER0 = Layer("l0_", 64, 8, 128, 8)
LAYER1 = Layer("l1_", 16, 4, 224, 6)


class Link:

    def __init__(self, engine, semaphore):
        self.engine, self.semaphore, self.count = engine, semaphore, 0

    def free(self, instruction):
        self.count += 1
        instruction.then_inc(self.semaphore, 1)

    def __call__(self, instruction):
        self.free(instruction)
        self.engine.wait_ge(self.semaphore, self.count)


class Space:

    def __init__(self, nc, stack, prefix):
        self.nc, self.stack, self.prefix = nc, stack, prefix
        self.semaphores = []
        stack.callback(self.clear)

    def sbuf(self, name, shape, dtype):
        return self.stack.enter_context(self.nc.sbuf_tensor(self.prefix + name, shape, dtype))

    def psum(self, name, shape, dtype=F32):
        return self.stack.enter_context(self.nc.psum_tensor(self.prefix + name, shape, dtype))

    def sem(self, name):
        self.semaphores.append(self.nc.alloc_semaphore(self.prefix + name))
        return self.semaphores[-1]

    def clear(self):
        if self.semaphores:
            self.nc.clear_and_free_semaphores(self.semaphores)
            self.nc.all_engine_barrier()


def normalise_stats(nc, link, x, stats, mean_var):
    link(nc.vector.bn_stats(stats[:], x))
    link(nc.vector.bn_aggr(mean_var[:, 0:2], stats[:]))
    link(nc.vector.tensor_scalar(mean_var[:, 1:2], mean_var[:, 1:2], EPS, None, ALU.add))


def reciprocal_root(nc, link, mean_var, work):
    bits, magic = work[:, 0:1].bitcast(I32), float(0x5F3759DF)
    link(nc.vector.tensor_scalar(work[:, 1:2].bitcast(I32), mean_var[:, 1:2].bitcast(I32), 1, None,
                                 ALU.logical_shift_right))
    link(nc.vector.tensor_scalar(bits, work[:, 1:2].bitcast(I32), -1.0, magic, ALU.mult, ALU.add))
    for _ in range(NEWTON):
        link(nc.vector.scalar_tensor_tensor(work[:, 1:2], work[:, 0:1], mean_var[:, 1:2], work[:, 0:1],
                                            ALU.mult, ALU.mult))
        link(nc.vector.tensor_scalar(work[:, 1:2], work[:, 1:2], -0.5, 1.5, ALU.mult, ALU.add))
        link(nc.vector.tensor_tensor(work[:, 0:1], work[:, 0:1], work[:, 1:2], ALU.mult))


class Operands:

    def __init__(self, s, q_stack, k_stack, values):
        self.q_stack, self.k_stack, self.values = q_stack, k_stack, values
        self.q = [s.sbuf(f"q_in{n}", [ROWS, H * D], BF16) for n in range(DEEP)]
        self.k = [s.sbuf(f"k_in{n}", [ROWS, H * D], BF16) for n in range(DEEP)]
        self.v = [s.sbuf(f"v_in{n}", [P, 2, H, VW], F32) for n in range(DEEP)]
        self.loaded = [s.sem(f"loaded{n}") for n in range(DEEP)]
        self.rows_set = s.sem("rows_set")

    def set_rows(self, nc, pool, n):
        nc.gpsimd.memset(self.k[n][0:TOP].bitcast(F32), 0.0)
        nc.gpsimd.memset(self.q[n][0:TOP].bitcast(F32), 0.0).then_inc(self.rows_set, 1)
        pool.wait_ge(self.rows_set, 2 * n + 1)
        nc.gpsimd.memset(self.k[n][TOP:ROWS].bitcast(F32), ONES_PAIR).then_inc(self.rows_set, 1)
        pool.wait_ge(self.rows_set, 2 * n + 2)

    def load(self, engine, b):
        n = b % DEEP
        for to, stack in ((self.q, self.q_stack), (self.k, self.k_stack)):
            engine.dma_start(to[n][0:STACK, :], stack[b].rearrange("t (d h) n -> (t d) (h n)", h=H)).then_inc(self.loaded[n], 16)
        engine.dma_start(self.v[n][:], self.values[b]).then_inc(self.loaded[n], 16)


def project_phase(nc, x, ctx, weights, biases, rotary, operands):
    q_stack, k_stack, values = operands.q_stack, operands.k_stack, operands.values
    with ExitStack() as stack:
        s = Space(nc, stack, "pj_")
        w = s.sbuf("w", [P, 4, P], F32)
        w_turned = s.sbuf("w_turned", [P, 2, P], F32)
        bias = s.sbuf("bias", [P, 7], F32)
        bias_turned = s.sbuf("bias_turned", [P, 2], F32)
        rot = s.sbuf("rot", [P, 2, D], F32)
        x_in = [s.sbuf(f"x_in{n}", [P, D], F32) for n in range(2)]
        c_in = [s.sbuf(f"c_in{n}", [P, D], F32) for n in range(2)]
        x_norm = [s.sbuf(f"x_norm{n}", [P, D], F32) for n in range(2)]
        stats = s.sbuf("stats", [P, 6], F32)
        mean_var = s.sbuf("mean_var", [P, 2], F32)
        root = s.sbuf("root", [P, 2], F32)
        straight = s.sbuf("straight", [P, 2, D], F32)
        turned = s.sbuf("turned", [P, 2, D], F32)
        full = [s.sbuf(f"full{n}", [P, 2, D], F32) for n in range(2)]
        rest = [s.sbuf(f"rest{n}", [P, 2, D], F32) for n in range(2)]
        parts = [s.sbuf(f"parts{n}", [P, 2, PARTS, D], BF16) for n in range(2)]
        v_out = [s.sbuf(f"v_out{n}", [P, 2, H, VW], F32) for n in range(2)]
        ps_qk = [s.psum(f"ps_qk{n}", [P, 2, 2, D]) for n in range(2)]
        ps_v = [s.psum(f"ps_v{n}", [P, 2, P]) for n in range(2)]
        consts_loaded, link_v = s.sem("consts_loaded"), s.sem("link_v")
        x_loaded = [s.sem(f"x_loaded{n}") for n in range(2)]
        c_loaded = [s.sem(f"c_loaded{n}") for n in range(2)]
        stored = [s.sem(f"stored{n}") for n in range(2)]
        w_ready, normed, projected, roped = s.sem("w_ready"), s.sem("normed"), s.sem("projected"), s.sem("roped")
        summed, high_cut, rest_ready, mid_cut, low_cut = (
            s.sem(n) for n in ("summed", "high_cut", "rest_ready", "mid_cut", "low_cut"))
        ones_set, v_kept = s.sem("ones_set"), s.sem("v_kept")
        block = stack.enter_context(nc.Block())

        @block.sync
        def _(sp):
            def load(b):
                if b >= 2:
                    sp.wait_ge(normed, b - 1)
                sp.dma_start(x_in[b % 2][:], x[b]).then_inc(x_loaded[b % 2], 16)
                if b >= 2:
                    sp.wait_ge(projected, b - 1)
                sp.dma_start(c_in[b % 2][:], ctx[b]).then_inc(c_loaded[b % 2], 16)

            sp.dma_start(x_in[0][:], x[0]).then_inc(x_loaded[0], 16)
            sp.dma_start(w[:], weights).then_inc(consts_loaded, 16)
            sp.dma_start(bias[:], biases).then_inc(consts_loaded, 16)
            sp.dma_start(c_in[0][:], ctx[0]).then_inc(c_loaded[0], 16)
            sp.dma_start(rot[:], rotary).then_inc(consts_loaded, 16)
            load(1)
            for b in range(B):
                n = b % 2
                if b + 2 < B:
                    load(b + 2)
                sp.wait_ge(v_kept, b + 1)
                sp.dma_start(values[b], v_out[n][:]).then_inc(stored[n], 16)
                sp.wait_ge(low_cut, b + 1)
                row = 0
                for i in range(PARTS):
                    m = PARTS - i
                    q_to = q_stack[b, row:row + m].rearrange("j p n -> p j n")
                    k_to = k_stack[b, row:row + m].rearrange("j p n -> p j n")
                    q_from = parts[n][:, 0, i:i + 1, :].broadcast_to([P, m, D])
                    sp.dma_start(q_to, q_from).then_inc(stored[n], 16)
                    sp.dma_start(k_to, parts[n][:, 1, 0:m, :]).then_inc(stored[n], 16)
                    row += m
            for n in range(2):
                sp.wait_ge(stored[n], 16 * 7 * (B // 2))

        @block.tensor
        def _(pe):
            pe.wait_ge(w_ready, 1)
            for b in range(B):
                n = b % 2
                if b >= 2:
                    pe.wait_ge(roped, b - 1)
                    pe.wait_ge(v_kept, b - 1)
                pe.wait_ge(normed, b + 1)
                nc.tensor.matmul(ps_qk[n][:, 0, 0, :], w[:, 0, :], x_norm[n][:], start=True, stop=True)
                nc.tensor.matmul(ps_qk[n][:, 0, 1, :], w_turned[:, 0, :], x_norm[n][:], start=True, stop=True)
                pe.wait_ge(c_loaded[n], 16 * (b // 2 + 1))
                nc.tensor.matmul(ps_qk[n][:, 1, 0, :], w[:, 1, :], c_in[n][:], start=True, stop=True)
                nc.tensor.matmul(ps_qk[n][:, 1, 1, :], w_turned[:, 1, :], c_in[n][:], start=True, stop=True)
                for m in range(2):
                    last = nc.tensor.matmul(ps_v[n][:, m, :], c_in[n][:, m * P:(m + 1) * P], w[:, 2, :],
                                            start=True, stop=True)
                last.then_inc(projected, 1)

        @block.vector
        def _(dve):
            link = Link(dve, link_v)

            def normalise(b):
                n = b % 2
                dve.wait_ge(x_loaded[n], 16 * (b // 2 + 1))
                normalise_stats(nc, link, x_in[n][:], stats, mean_var)
                reciprocal_root(nc, link, mean_var, root)
                if b >= 2:
                    dve.wait_ge(projected, b - 1)
                nc.vector.tensor_scalar(x_norm[n][:], x_in[n][:], mean_var[:, 0:1], root[:, 0:1],
                                        ALU.subtract, ALU.mult).then_inc(normed, 1)

            normalise(0)
            dve.wait_ge(consts_loaded, 48)
            for t in range(2):
                to = w_turned[:, t, :].rearrange("p (j s h) -> p j s h", s=2, h=H)
                of = w[:, t, :].rearrange("p (j s h) -> p j s h", s=2, h=H)
                nc.vector.tensor_scalar(to[:, :, 0, :], of[:, :, 1, :], -1.0, None, ALU.mult)
                last = nc.vector.tensor_copy(to[:, :, 1, :], of[:, :, 0, :])
            last.then_inc(w_ready, 1)
            link(nc.vector.tensor_scalar(bias_turned[:], bias[:, 4:6], bias[:, 6:7], None, ALU.mult))
            for b in range(B):
                n = b % 2
                if b + 1 < B:
                    normalise(b + 1)
                dve.wait_ge(projected, b + 1)
                if b >= 1:
                    dve.wait_ge(summed, b)
                for t in range(2):
                    nc.vector.scalar_tensor_tensor(straight[:, t, :], ps_qk[n][:, t, 0, :], bias[:, t:t + 1],
                                                   rot[:, 0, :], ALU.add, ALU.mult)
                    last = nc.vector.scalar_tensor_tensor(turned[:, t, :], ps_qk[n][:, t, 1, :],
                                                          bias_turned[:, t:t + 1], rot[:, 1, :], ALU.add, ALU.mult)
                last.then_inc(roped, 1)

        @block.gpsimd
        def _(pool):
            for n in range(2):
                last = nc.gpsimd.memset(v_out[n][:], 1.0)
            last.then_inc(ones_set, 1)
            operands.set_rows(nc, pool, 0)
            for b in range(B):
                n = b % 2
                pool.wait_ge(roped, b + 1)
                if b >= 2:
                    pool.wait_ge(low_cut, b - 1)
                nc.gpsimd.tensor_tensor(full[n][:], straight[:], turned[:], ALU.add).then_inc(summed, 1)
                pool.wait_ge(high_cut, b + 1)
                nc.gpsimd.tensor_tensor(rest[n][:], full[n][:], parts[n][:, :, 0, :], ALU.subtract).then_inc(rest_ready, 1)
                pool.wait_ge(mid_cut, b + 1)
                pool.wait_ge(rest_ready, b + 1)
                nc.gpsimd.tensor_tensor(parts[n][:, :, 2, :], rest[n][:], parts[n][:, :, 1, :],
                                        ALU.subtract).then_inc(low_cut, 1)
                if 1 <= b < DEEP:
                    operands.set_rows(nc, pool, b)

        @block.scalar
        def _(act):
            act.wait_ge(ones_set, 1)
            for b in range(B):
                n = b % 2
                act.wait_ge(projected, b + 1)
                if b >= 2:
                    act.wait_ge(stored[n], 16 * 7 * (b // 2))
                    if b - 2 < DEEP:
                        act.wait_ge(operands.rows_set, 2 * (b - 1))
                        operands.load(act, b - 2)
                nc.scalar.activation(v_out[n][:, :, :, 0:HD], ps_v[n][:].rearrange("p m (d h) -> p m h d", h=H),
                                     ACT.Copy).then_inc(v_kept, 1)
                act.wait_ge(summed, b + 1)
                nc.scalar.activation(parts[n][:, :, 0, :], full[n][:], ACT.Copy).then_inc(high_cut, 1)
                act.wait_ge(rest_ready, b + 1)
                nc.scalar.activation(parts[n][:, :, 1, :], rest[n][:], ACT.Copy).then_inc(mid_cut, 1)


def attend_phase(nc, identity, operands, attended, tails):
    scale = 1.0 / float(np.sqrt(HD))
    HALF = H // 2
    HALVES = 2 * B
    LEAD = H + 4
    q_in, k_in, v_in, loaded = operands.q, operands.k, operands.v, operands.loaded
    with ExitStack() as stack:
        s = Space(nc, stack, "at_")
        top = s.sbuf("top", [P, 2 * H], F32)
        top_rest = s.sbuf("top_rest", [P, 2, 2 * HALF], F32)
        top_parts = s.sbuf("top_parts", [P, 2, PARTS, 2 * HALF], F32)
        top_cut = s.sbuf("top_cut", [P, 2 * HALF], BF16)
        top_rows = [s.sbuf(f"top_rows{n}", [PARTS * 2 * HALF, P], BF16) for n in range(2)]
        RING, TOPS, SCORES = 12, 2, 3
        prob = [s.sbuf(f"prob{n}", [P, 2, D], F32) for n in range(RING)]
        out = [s.sbuf(f"out{n}", [P, 4, D], F32) for n in range(2)]
        ps_top = [s.psum(f"ps_top{n}", [P, 2, D]) for n in range(TOPS)]
        ps_score = [s.psum(f"ps_score{n}", [P, 2, D]) for n in range(SCORES)]
        ps_out = [s.psum(f"ps_out{n}", [P, 2, D]) for n in range(2)]
        ps_rows = s.psum("ps_rows", [P, P])
        zeros = s.sbuf("zeros", [P, D], F32)
        zeros_set, tails_zeroed, link_g = s.sem("zeros_set"), s.sem("tails_zeroed"), s.sem("link_g")
        top_scored, top_found, parts_cut, rows_turned, rows_kept = (
            s.sem(n) for n in ("top_scored", "top_found", "parts_cut", "rows_turned", "rows_kept"))
        rows_placed = [s.sem(f"rows_placed{n}") for n in range(2)]
        scored, prob_ready, weighted, out_kept, link_v = (
            s.sem(n) for n in ("scored", "prob_ready", "weighted", "out_kept", "link_v"))
        stored = [s.sem(f"stored{n}") for n in range(2)]
        block = stack.enter_context(nc.Block())

        def columns(at, half=None):
            first = at % H * D + (half or 0) * P
            return slice(first, first + (D if half is None else P))

        @block.sync
        def _(sp):
            def place(hh):
                b, half = hh // 2, hh % 2
                sp.wait_ge(rows_kept, hh + 1)
                for i in range(PARTS):
                    to = q_in[b % DEEP][TOP + i:TOP + i + 1, half * HALF * D:(half + 1) * HALF * D]
                    sp.dma_start(to.rearrange("a (r n) -> a r n", n=P),
                                 top_rows[half][i * 2 * HALF:(i + 1) * 2 * HALF, :]).then_inc(rows_placed[half], 16)

            for hh in range(3):
                place(hh)
            for b in range(B):
                if 2 * b + 3 < HALVES:
                    place(2 * b + 3)
                if b + DEEP < B:
                    sp.wait_ge(weighted, 4 * (b + 1))
                    operands.load(sp, b + DEEP)
                sp.wait_ge(out_kept, 2 * b + 2)
                sp.dma_start(attended[b], out[b % 2][:]).then_inc(stored[b % 2], 16)
                if 2 * b + 4 < HALVES:
                    place(2 * b + 4)
            for n in range(2):
                sp.wait_ge(stored[n], 16 * (B // 2))

        @block.gpsimd
        def _(pool):
            nc.gpsimd.memset(zeros[:], 0.0).then_inc(zeros_set, 1)
            pool.wait_ge(zeros_set, 1)
            link, pieces = Link(pool, link_g), 0
            for hh in range(HALVES):
                half = hh % 2
                if hh >= 4:
                    for tail in tails:
                        share = -(-tail.shape[0] // (HALVES - 4))
                        first, end = (hh - 4) * share, min((hh - 3) * share, tail.shape[0])
                        if first < end:
                            pool.dma_start(tail[first:end].rearrange("t p n -> p t n"), zeros[:].unsqueeze(1)
                                           .broadcast_to([P, end - first, D])).then_inc(tails_zeroed, 16)
                            pieces += 1
                pool.wait_ge(top_found, (hh + 1) * HALF)
                if hh >= 2:
                    pool.wait_ge(rows_turned, hh - 1)
                tops = top[:, half * 2 * HALF:(half + 1) * 2 * HALF]
                part, rest = top_parts[:, half], top_rest[:, half]
                link(nc.gpsimd.tensor_scalar(top_cut[:], tops, -1.0, None, ALU.mult))
                link(nc.gpsimd.tensor_copy(part[:, 0, :], top_cut[:]))
                link(nc.gpsimd.tensor_tensor(rest, tops, part[:, 0, :], ALU.add))
                link(nc.gpsimd.tensor_scalar(top_cut[:], rest, -1.0, None, ALU.mult))
                link(nc.gpsimd.tensor_copy(part[:, 1, :], top_cut[:]))
                link(nc.gpsimd.tensor_tensor(rest, rest, part[:, 1, :], ALU.add))
                nc.gpsimd.tensor_scalar(part[:, 2, :], rest, -1.0, None, ALU.mult).then_inc(parts_cut, 1)
            pool.wait_ge(tails_zeroed, 16 * pieces)

        @block.tensor
        def _(pe):
            def score_for_top(at):
                n = at // H % DEEP
                if at % H == 0:
                    pe.wait_ge(loaded[n], 48 * (at // H // DEEP + 1))
                if at >= TOPS:
                    pe.wait_ge(top_found, at - TOPS + 1)
                for half in range(2):
                    last = nc.tensor.matmul(ps_top[at % TOPS][:, half, :], q_in[n][0:TOP, columns(at, half)],
                                            k_in[n][0:TOP, columns(at)], start=True, stop=True)
                last.then_inc(top_scored, 1)

            def turn_tops(hh):
                pe.wait_ge(parts_cut, hh + 1)
                if hh >= 1:
                    pe.wait_ge(rows_kept, hh)
                nc.tensor.transpose(ps_rows[0:PARTS * 2 * HALF, :], top_parts[:, hh % 2].rearrange("p i c -> p (i c)"),
                                    identity[:]).then_inc(rows_turned, 1)

            def score(at):
                n = at // H % DEEP
                if at % HALF == 0:
                    pe.wait_ge(rows_placed[at // HALF % 2], 16 * PARTS * (at // H + 1))
                if at >= SCORES:
                    pe.wait_ge(prob_ready, at - SCORES + 1)
                for half in range(2):
                    last = nc.tensor.matmul(ps_score[at % SCORES][:, half, :], k_in[n][0:ROWS, columns(at, half)],
                                            q_in[n][0:ROWS, columns(at)], start=True, stop=True)
                last.then_inc(scored, 1)

            def weigh(group, half):
                b, g = group // 4, group % 4
                if half == 0:
                    pe.wait_ge(prob_ready, 4 * group + 4)
                    if b >= 1 and g % 2 == 0:
                        pe.wait_ge(out_kept, 2 * (b - 1) + g // 2 + 1)
                for j in range(4):
                    last = nc.tensor.matmul(ps_out[g // 2][32 * j:32 * j + VW, g % 2, :], v_in[b % DEEP][:, half, 4 * g + j, :],
                                            prob[(4 * group + j) % RING][:, half, :], start=half == 0, stop=half == 1,
                                            skip_group_check=True)
                if half == 1:
                    last.then_inc(weighted, 1)

            for at in range(-LEAD, B * H + 4):
                if 0 <= at < B * H:
                    score(at)
                if at + LEAD < B * H:
                    score_for_top(at + LEAD)
                if at >= 4 and at % 4 == 1:
                    weigh(at // 4 - 1, 0)
                if at >= 4 and at % 4 == 3:
                    weigh(at // 4 - 1, 1)
                hh, late = divmod(at + LEAD - 4, HALF)
                if late == HALF - 1 and 0 <= hh < HALVES:
                    turn_tops(hh)
                if at == -1:
                    for _ in range(WARM_UP):
                        nc.tensor.matmul(ps_score[0][:, 0, :], k_in[0][0:TOP, 0:P], k_in[0][0:TOP, 0:D], start=True, stop=True)

        @block.vector
        def _(dve):
            for at in range(B * H):
                dve.wait_ge(top_scored, at + 1)
                if at >= H and at % HALF == 0:
                    dve.wait_ge(parts_cut, at // HALF - 1)
                h = at % H
                nc.vector.reduce_max(top[:, 2 * h:2 * h + 2], ps_top[at % TOPS][:], AX_X).then_inc(top_found, 1)

        @block.scalar
        def _(act):
            def keep_rows(hh):
                act.wait_ge(rows_turned, hh + 1)
                if hh >= 2:
                    act.wait_ge(rows_placed[hh % 2], 16 * PARTS * (hh // 2))
                nc.scalar.activation(top_rows[hh % 2][:], ps_rows[0:PARTS * 2 * HALF, :], ACT.Copy).then_inc(rows_kept, 1)

            def keep_out(pair):
                b = pair // 2
                act.wait_ge(weighted, 2 * pair + 2)
                if b >= 2:
                    act.wait_ge(stored[b % 2], 16 * (b // 2))
                nc.scalar.activation(out[b % 2][:, 2 * (pair % 2):2 * (pair % 2) + 2, :], ps_out[pair % 2][:],
                                     ACT.Copy).then_inc(out_kept, 1)

            for at in range(-LEAD, B * H + 5):
                if 0 <= at < B * H:
                    act.wait_ge(scored, at + 1)
                    if at >= RING:
                        act.wait_ge(weighted, (at - RING) // 4 + 1)
                    nc.scalar.activation(prob[at % RING][:], ps_score[at % SCORES][:], ACT.Exp, scale=scale).then_inc(prob_ready, 1)
                hh, late = divmod(at + LEAD - 5, HALF)
                if late == HALF - 1 and 0 <= hh < HALVES:
                    keep_rows(hh)
                if at >= HALF + 4 and at % HALF == 4:
                    keep_out(at // HALF - 1)


class Kept:

    def __init__(self, s, layer):
        E, n = layer.experts, layer.name
        self.rank = s.sbuf(n + "rank", [P, B, E], F32)
        self.index = s.sbuf(n + "index", [P, B, 8], F32)
        self.weight = s.sbuf(n + "weight", [P, B, 8], F32)
        self.mask = s.sbuf(n + "mask", [P, B, E], BF16)
        self.row = s.sbuf(n + "row", [P, B, 8], I32)
        self.tile_column = s.sbuf(n + "tile_column", [1, P], I32)
        self.tile_expert = s.sbuf(n + "tile_expert", [1, P], I32)
        self.last_group_at = s.sbuf(n + "last_group_at", [1, 1], I32)


class Consts:

    def __init__(self, s):
        self.identity = s.sbuf("identity", [P, P], F32)
        self.earlier = s.sbuf("earlier", [P, P], BF16)
        self.ones = s.sbuf("ones", [P, P], BF16)
        self.ramp = s.sbuf("ramp", [P, P], F32)
        self.number = s.sbuf("number", [P, 1], F32)
        self.token = s.sbuf("token", [P, B], I32)


def span(group):
    return slice(group[0], group[-1] + 1)


class Norm:

    def __init__(self, nc, s, name):
        self.nc = nc
        self.stats = s.sbuf(name + "stats", [P, MOST, 6], F32)
        self.mean_var = s.sbuf(name + "mean_var", [P, MOST, 2], F32)
        self.root = s.sbuf(name + "root", [P, 2, MOST], F32)

    def __call__(self, link, group, x, x_norm, normed):
        nc, n = self.nc, len(group)
        for j, b in enumerate(group):
            link.free(nc.vector.bn_stats(self.stats[:, j, :], x[:, b, :]))
        link.engine.wait_ge(link.semaphore, link.count)
        for j in range(n):
            link.free(nc.vector.bn_aggr(self.mean_var[:, j, :], self.stats[:, j, :]))
        link.engine.wait_ge(link.semaphore, link.count)
        variance, root, work = self.mean_var[:, 0:n, 1], self.root[:, 0, 0:n], self.root[:, 1, 0:n]
        link(nc.vector.tensor_scalar(variance, variance, EPS, None, ALU.add))
        link(nc.vector.tensor_scalar(work.bitcast(I32), variance.bitcast(I32), 1, None, ALU.logical_shift_right))
        link(nc.vector.tensor_scalar(root.bitcast(I32), work.bitcast(I32), -1.0, float(0x5F3759DF), ALU.mult, ALU.add))
        for _ in range(NEWTON):
            link(nc.vector.tensor_tensor(work, root, root, ALU.mult))
            link(nc.vector.tensor_tensor(work, work, variance, ALU.mult))
            link(nc.vector.tensor_scalar(work, work, -0.5, 1.5, ALU.mult, ALU.add))
            link(nc.vector.tensor_tensor(root, root, work, ALU.mult))
        for j, b in enumerate(group):
            nc.vector.tensor_scalar(x_norm[:, b, :], x[:, b, :], self.mean_var[:, j, 0:1], self.root[:, 0, j:j + 1],
                                    ALU.subtract, ALU.mult).then_inc(normed, 1)


class Routing:

    def __init__(self, nc, s, layer, kept, consts, gate, gate_bias, table, normed_dram):
        self.nc, self.layer, self.kept, self.consts, self.gate, self.gate_bias = nc, layer, kept, consts, gate, gate_bias
        self.table, self.normed_dram = table, normed_dram
        E = layer.experts
        self.spare = 8 - layer.chosen
        self.norm = Norm(nc, s, "r_")
        self.x_norm = s.sbuf("r_norm", [P, B, D], F32)
        self.x_turned = [s.sbuf(f"r_turned_sb{n}", [P, 2, P], F32) for n in range(2)]
        self.logits = s.sbuf("r_logits", [P, MOST, E], F32)
        self.top = s.sbuf("r_top", [P, MOST], F32)
        self.expo = s.sbuf("r_expo", [P, MOST, E], F32)
        self.total = s.sbuf("r_total", [P, MOST], F32)
        self.share = s.sbuf("r_share", [P, MOST], F32)
        self.probs = s.sbuf("r_probs", [P, MOST, E + self.spare], F32)
        self.taken = s.sbuf("r_taken", [P, MOST, E + self.spare], F32)
        self.best = s.sbuf("r_best", [P, MOST, 8], F32)
        self.picks = s.sbuf("r_picks", [P, MOST, 8], F32)
        self.index = s.sbuf("r_index", [P, MOST, 8], U32)
        self.junk = s.sbuf("r_junk", [P, 8, E], F32)
        self.place = s.sbuf("r_place", [P, MOST, 8], F32)
        self.place_int = s.sbuf("r_place_int", [P, MOST, 8], I32)
        self.column = s.sbuf("r_column", [P, MOST, 8], I32)
        self.address = s.sbuf("r_address", [P, B, 8], I32)
        self.ps_turned = s.psum("r_ps_turned", [P, 2, P])
        narrow = s.psum("r_ps_narrow", [P, 2 * MOST + 1, E])
        self.ps_logits, self.ps_rank, self.ps_count = narrow[:, 0:MOST], narrow[:, MOST:2 * MOST], narrow[:, 2 * MOST]
        (self.normed, self.stored, self.turned, self.turned_kept, self.scored, self.logits_ready, self.expo_ready,
         self.mask_ready, self.ranked, self.rank_kept, self.places_ready, self.scattered) = (
            s.sem("r_" + n) for n in ("normed", "stored", "turned", "turned_kept", "scored", "logits_ready",
                                      "expo_ready", "mask_ready", "ranked", "rank_kept", "places_ready", "scattered"))

    def dve_start(self, link):
        if self.spare:
            link.free(self.nc.vector.memset(self.probs[:, :, self.layer.experts:], -1.0))
            link.free(self.nc.vector.memset(self.picks[:, :, self.layer.chosen:], -1.0))
            link.free(self.nc.vector.memset(self.place[:, :, self.layer.chosen:], 0.0))

    def dve_normalise(self, link, i, x):
        self.norm(link, GROUPS[i], x, self.x_norm, self.normed)

    def sp_store(self, sp, i):
        group = GROUPS[i]
        sp.wait_ge(self.normed, group[-1] + 1)
        sp.dma_start(self.normed_dram.rearrange("(b p) n -> p b n", p=P)[:, span(group), :],
                     self.x_norm[:, span(group), :]).then_inc(self.stored, 16)

    def sp_finish(self, sp):
        sp.wait_ge(self.stored, 16 * len(GROUPS))

    def pe_turn(self, pe, b):
        pe.wait_ge(self.normed, b + 1)
        if b >= 1:
            pe.wait_ge(self.turned_kept, b)
        for k in range(2):
            last = self.nc.tensor.transpose(self.ps_turned[:, k, :], self.x_norm[:, b, k * P:(k + 1) * P],
                                            self.consts.identity[:])
        last.then_inc(self.turned, 1)

    def act_keep_turned(self, act, b):
        act.wait_ge(self.turned, b + 1)
        if b >= 2:
            act.wait_ge(self.scored, b - 1)
        self.nc.scalar.activation(self.x_turned[b % 2][:], self.ps_turned[:], ACT.Copy).then_inc(self.turned_kept, 1)

    def pe_score(self, pe, i, b):
        pe.wait_ge(self.turned_kept, b + 1)
        if i >= 1 and b == GROUPS[i][0]:
            pe.wait_ge(self.rank_kept, i)
        for k in range(2):
            last = self.nc.tensor.matmul(self.ps_logits[:, b - GROUPS[i][0], :], self.x_turned[b % 2][:, k, :],
                                         self.gate[:, k, :], start=k == 0, stop=k == 1)
        last.then_inc(self.scored, 1)

    def pe_turn_and_score(self, pe, i):
        group = GROUPS[i]
        self.pe_turn(pe, group[0])
        for b in group:
            if b != group[-1]:
                self.pe_turn(pe, b + 1)
            self.pe_score(pe, i, b)

    def dve_logits(self, dve, link, i):
        nc, n, E = self.nc, len(GROUPS[i]), self.layer.experts
        logits, top = self.logits[:, 0:n, :], self.top[:, 0:n]
        dve.wait_ge(self.scored, GROUPS[i][-1] + 1)
        scores = self.ps_logits[:, 0:n, :]
        if self.gate_bias is not None:
            link(nc.vector.tensor_tensor(logits, scores, self.gate_bias[:].unsqueeze(1).broadcast_to([P, n, E]), ALU.add))
            scores = logits
        link(nc.vector.reduce_max(top, scores, AX_X))
        nc.vector.tensor_tensor(logits, scores, top.unsqueeze(2).broadcast_to([P, n, E]),
                                ALU.subtract).then_inc(self.logits_ready, 1)

    def act_exponentials(self, act, i):
        n = len(GROUPS[i])
        act.wait_ge(self.logits_ready, i + 1)
        self.nc.scalar.activation(self.expo[:, 0:n, :], self.logits[:, 0:n, :], ACT.Exp).then_inc(self.expo_ready, 1)

    def dve_choose(self, dve, link, i):
        nc, E, chosen, n, batches = self.nc, self.layer.experts, self.layer.chosen, len(GROUPS[i]), span(GROUPS[i])
        expo, total, share, best = self.expo[:, 0:n, :], self.total[:, 0:n], self.share[:, 0:n], self.best[:, 0:n, :]
        weight, picks = self.kept.weight[:, batches, :], self.picks if self.spare else self.best
        dve.wait_ge(self.expo_ready, i + 1)
        link(nc.vector.reduce_sum(total, expo, AX_X))
        link(nc.vector.reciprocal(share, total))
        link(nc.vector.tensor_tensor(self.probs[:, 0:n, 0:E], expo, share.unsqueeze(2).broadcast_to([P, n, E]), ALU.mult))
        for j in range(n):
            link.free(nc.vector.max(self.best[:, j, :], self.probs[:, j, 0:E]))
        dve.wait_ge(link.semaphore, link.count)
        for j in range(n):
            link.free(nc.vector.max_index(self.index[:, j, :], self.best[:, j, :], self.probs[:, j, 0:E]))
        if self.spare:
            link.free(nc.vector.tensor_copy(self.picks[:, 0:n, 0:chosen], self.best[:, 0:n, 0:chosen]))
        dve.wait_ge(link.semaphore, link.count)
        for j in range(n):
            link.free(nc.vector.match_replace(self.taken[:, j, :], picks[:, j, :], self.probs[:, j, :], -2.0))
        dve.wait_ge(link.semaphore, link.count)
        nc.vector.tensor_scalar(self.kept.mask[:, batches, :], self.taken[:, 0:n, 0:E], -1.5, None,
                                ALU.is_lt).then_inc(self.mask_ready, 1)
        link.free(nc.vector.tensor_copy(self.kept.index[:, batches, :], self.index[:, 0:n, :]))
        if self.spare:
            link(nc.vector.reduce_sum(total, best[:, :, 0:chosen], AX_X))
            link(nc.vector.reciprocal(share, total))
            link(nc.vector.tensor_tensor(weight, best, share.unsqueeze(2).broadcast_to([P, n, 8]), ALU.mult))
        else:
            link(nc.vector.tensor_copy(weight, best))

    def pe_rank(self, pe, i):
        mask = self.kept.mask
        pe.wait_ge(self.mask_ready, i + 1)
        if i >= 1:
            pe.wait_ge(self.rank_kept, i)
        for j, b in enumerate(GROUPS[i]):
            last = self.nc.tensor.matmul(self.ps_rank[:, j, :], self.consts.earlier[:], mask[:, b, :], start=True, stop=b == 0)
            for before in range(b):
                last = self.nc.tensor.matmul(self.ps_rank[:, j, :], self.consts.ones[:], mask[:, before, :],
                                             start=False, stop=before == b - 1)
        last.then_inc(self.ranked, 1)

    def dve_places(self, dve, link, i):
        nc, kept, layer, n, batches = self.nc, self.kept, self.layer, len(GROUPS[i]), span(GROUPS[i])
        place, place_int, column = self.place[:, 0:n, :], self.place_int[:, 0:n, :], self.column[:, 0:n, :]
        dve.wait_ge(self.ranked, i + 1)
        nc.vector.tensor_copy(kept.rank[:, batches, :], self.ps_rank[:, 0:n, :]).then_inc(self.rank_kept, 1)
        dve.wait_ge(self.rank_kept, i + 1)
        for j, b in enumerate(GROUPS[i]):
            look_up(nc, link, layer, self.consts.ramp, kept.index[:, b, :], kept.rank[:, b, :], self.junk, self.place[:, j, :])
        link(nc.vector.scalar_tensor_tensor(place, kept.index[:, batches, :], float(TOKENS), place, ALU.mult, ALU.add))
        link(nc.vector.tensor_copy(place_int, place))
        link(nc.vector.tensor_scalar(column, place_int, P.bit_length() - 1, None, ALU.logical_shift_right))
        link(nc.vector.tensor_scalar(place_int, place_int, P - 1, layer.columns.bit_length() - 1,
                                     ALU.bitwise_and, ALU.logical_shift_left))
        nc.vector.tensor_tensor(self.address[:, batches, :], place_int, column, ALU.bitwise_or).then_inc(self.places_ready, 1)

    def pool_scatter(self, pool, i):
        pool.wait_ge(self.places_ready, i + 1)
        for b in GROUPS[i]:
            for k in range(self.layer.chosen):
                to = bass.IndirectOffsetOnAxis(ap=self.address[:, b, k:k + 1], axis=0)
                self.nc.gpsimd.indirect_dma_start(self.table, to, self.consts.token[:, b:b + 1], None)\
                    .then_inc(self.scattered, 16)

    def pool_finish(self, pool):
        pool.wait_ge(self.scattered, 16 * self.layer.chosen * B)


def look_up(nc, link, layer, ramp, index, values, junk, found):
    for k in range(layer.chosen):
        link.free(nc.vector.scalar_tensor_tensor(junk[:, k, :], ramp[:, 0:layer.experts], index[:, k:k + 1], values,
                                                 ALU.is_equal, ALU.mult, accum_out=found[:, k:k + 1]))
    link.engine.wait_ge(link.semaphore, link.count)


def setup_phase(nc, consts, consts_f, token_numbers, tables):
    with ExitStack() as stack:
        s = Space(nc, stack, "su_")
        loaded = s.sbuf("loaded", [P, 3, P], F32)
        zeros = s.sbuf("zeros", [P, LAYER0.columns], I32)
        arrived, made, zeroed = s.sem("arrived"), s.sem("made"), s.sem("zeroed")
        block = stack.enter_context(nc.Block())

        @block.sync
        def _(sp):
            sp.dma_start(loaded[:], consts_f).then_inc(arrived, 16)
            sp.dma_start(consts.token[:], token_numbers).then_inc(arrived, 16)
            sp.wait_ge(made, 1)
            for layer, table in tables:
                sp.dma_start(table.rearrange("(p c) a -> p (c a)", p=P), zeros[:, 0:layer.columns]).then_inc(zeroed, 16)
            sp.wait_ge(zeroed, 16 * len(tables))

        @block.vector
        def _(dve):
            nc.vector.memset(zeros[:], 0).then_inc(made, 1)
            dve.wait_ge(arrived, 32)
            nc.vector.tensor_copy(consts.identity[:], loaded[:, 0, :]).then_inc(made, 1)
            nc.vector.tensor_copy(consts.earlier[:], loaded[:, 1, :]).then_inc(made, 1)
            nc.vector.tensor_copy(consts.ramp[:], loaded[:, 2, :]).then_inc(made, 1)
            nc.vector.memset(consts.ones[:], 1.0).then_inc(made, 1)
            nc.vector.reduce_sum(consts.number[:], loaded[:, 1, :], AX_X).then_inc(made, 1)
            dve.wait_ge(made, 6)
            nc.vector.tensor_scalar(consts.number[:], consts.number[:], -1.0, float(P - 1), ALU.mult, ALU.add).then_inc(made, 1)
            dve.wait_ge(made, 7)


def merge_phase(nc, consts, kept, x_all, x, weights, biases, attended, gate_dram, table, normed_dram):
    layer = LAYER0
    with ExitStack() as stack:
        s = Space(nc, stack, "mg_")
        w = s.sbuf("w", [P, P], F32)
        bias = s.sbuf("bias", [P, 7], F32)
        gate = s.sbuf("gate", [P, 2, layer.experts], F32)
        sums_in = [s.sbuf(f"sums_in{n}", [P, 4, D], F32) for n in range(3)]
        x_in = s.sbuf("x_in", [P, B, D], F32)
        share = s.sbuf("share", [P, MOST, 2, 4, 4], F32)
        heads = [s.sbuf(f"heads{n}", [P, 2, P], F32) for n in range(2)]
        merged = [s.sbuf(f"merged{n}", [P, D], F32) for n in range(2)]
        ps_sums = [s.psum(f"ps_sums{n}", [P, 2, 4, P]) for n in range(2)]
        ps_heads = s.psum("ps_heads", [P, 2, P])
        ps_merged = s.psum("ps_merged", [P, D])
        routing = Routing(nc, s, layer, kept, consts, gate, None, table, normed_dram)
        plan = Plan(nc, s, layer, consts, kept, routing)
        weights_loaded, x_loaded, link_v = s.sem("weights_loaded"), s.sem("x_loaded"), s.sem("link_v")
        in_loaded = [s.sem(f"in_loaded{n}") for n in range(3)]
        sums_turned, heads_ready, heads_turned, heads_kept, merged_ready, x_ready = (
            s.sem(n) for n in ("sums_turned", "heads_ready", "heads_turned", "heads_kept", "merged_ready", "x_ready"))
        block = stack.enter_context(nc.Block())

        @block.sync
        def _(sp):
            def load(b):
                if b >= 3:
                    sp.wait_ge(sums_turned, b - 2)
                sp.dma_start(sums_in[b % 3][:], attended[b]).then_inc(in_loaded[b % 3], 16)

            load(0)
            sp.dma_start(w[:], weights[:, 3, :]).then_inc(weights_loaded, 16)
            sp.dma_start(bias[:], biases).then_inc(weights_loaded, 16)
            sp.dma_start(gate[:], gate_dram).then_inc(weights_loaded, 16)
            load(1)
            sp.dma_start(x_in[:], x.rearrange("b p n -> p b n")).then_inc(x_loaded, 16)
            for b in range(2, B):
                load(b)
            for i in range(len(GROUPS)):
                routing.sp_store(sp, i)
            routing.sp_finish(sp)

        @block.tensor
        def _(pe):
            def turn_sums(b):
                pe.wait_ge(in_loaded[b % 3], 16 * (b // 3 + 1))
                if b >= 2:
                    pe.wait_ge(heads_ready, b - 1)
                for half in range(2):
                    for g in range(4):
                        last = nc.tensor.transpose(ps_sums[b % 2][:, half, g, :],
                                                   sums_in[b % 3][:, g, half * P:(half + 1) * P], consts.identity[:])
                last.then_inc(sums_turned, 1)

            pe.wait_ge(weights_loaded, 48)
            turn_sums(0)
            turn_sums(1)
            for i in range(len(GROUPS) + 1):
                for b in GROUPS[i] if i < len(GROUPS) else ():
                    pe.wait_ge(heads_ready, b + 1)
                    if b >= 1:
                        pe.wait_ge(heads_kept, b)
                    for half in range(2):
                        last = nc.tensor.transpose(ps_heads[:, half, :], heads[b % 2][:, half, :], consts.identity[:])
                    last.then_inc(heads_turned, 1)
                    if b + 2 < B:
                        turn_sums(b + 2)
                    pe.wait_ge(heads_kept, b + 1)
                    if b >= 1:
                        pe.wait_ge(x_ready, b)
                    nc.tensor.matmul(ps_merged[:], w[:], merged[b % 2][:], start=True, stop=True).then_inc(merged_ready, 1)
                if i >= 1:
                    routing.pe_rank(pe, i - 1)
                if i < len(GROUPS):
                    routing.pe_turn_and_score(pe, i)
            plan.pe_count(pe)
            plan.pe_rows(pe)

        @block.scalar
        def _(act):
            act.wait_ge(weights_loaded, 48)
            for i in range(len(GROUPS) + 1):
                for b in GROUPS[i] if i < len(GROUPS) else ():
                    act.wait_ge(heads_turned, b + 1)
                    if b >= 2:
                        act.wait_ge(merged_ready, b - 1)
                    nc.scalar.activation(merged[b % 2][:], ps_heads[:].rearrange("p a n -> p (a n)"), ACT.Identity,
                                         bias=bias[:, 2:3]).then_inc(heads_kept, 1)
                if i >= 1:
                    routing.act_exponentials(act, i - 1)
                for b in GROUPS[i] if i < len(GROUPS) else ():
                    routing.act_keep_turned(act, b)

        @block.vector
        def _(dve):
            link = Link(dve, link_v)

            def divide(b, j):
                dve.wait_ge(sums_turned, b + 1)
                sums = ps_sums[b % 2][:].rearrange("p a g (j v) -> p a g j v", v=VW)
                for half in range(2):
                    link.free(nc.vector.reciprocal(share[:, j, half], sums[:, half, :, :, HD]))
                dve.wait_ge(link_v, link.count)
                if b >= 2:
                    dve.wait_ge(heads_turned, b - 1)
                for half in range(2):
                    to = heads[b % 2][:, half, :].rearrange("p (d g j) -> p g j d", g=4, j=4)
                    last = nc.vector.tensor_tensor(to, sums[:, half, :, :, 0:HD],
                                                   share[:, j, half].unsqueeze(3).broadcast_to([P, 4, 4, HD]), ALU.mult)
                last.then_inc(heads_ready, 1)

            def add(b):
                dve.wait_ge(merged_ready, b + 1)
                nc.vector.scalar_tensor_tensor(x_all[:, b, :], ps_merged[:], bias[:, 3:4], x_in[:, b, :],
                                               ALU.add, ALU.add).then_inc(x_ready, 1)

            dve.wait_ge(weights_loaded, 48)
            dve.wait_ge(x_loaded, 16)
            routing.dve_start(link)
            for i in range(len(GROUPS) + 1):
                group = GROUPS[i] if i < len(GROUPS) else ()
                for j, b in enumerate(group):
                    divide(b, j)
                    if j >= 1:
                        add(b - 1)
                if i >= 1:
                    routing.dve_logits(dve, link, i - 1)
                if group:
                    add(group[-1])
                    dve.wait_ge(x_ready, group[-1] + 1)
                if i >= 1:
                    routing.dve_choose(dve, link, i - 1)
                if group:
                    routing.dve_normalise(link, i, x_all)
                if i >= 1:
                    routing.dve_places(dve, link, i - 1)
            plan.dve_plan(dve, link)

        @block.gpsimd
        def _(pool):
            for i in range(len(GROUPS)):
                routing.pool_scatter(pool, i)
            routing.pool_finish(pool)


def tiles_phase(nc, layer, consts, kept, table, normed_dram, up_dram, down_dram, rows_out):
    with ExitStack() as stack:
        s = Space(nc, stack, layer.name)
        E, U, C, W = layer.experts, layer.unroll, layer.chunks, layer.width
        lists = s.sbuf("lists", [P, layer.columns], I32)
        tile_column, tile_expert, last_group_at = kept.tile_column, kept.tile_expert, kept.last_group_at
        lists_loaded = s.sem("lists_loaded")
        up_w = [s.sbuf(f"up_w{u}", [P, 2, 2 * layer.inter], F32) for u in range(U)]
        down_w = [s.sbuf(f"down_w{u}", [W, C, D], F32) for u in range(U)]
        column = [s.sbuf(f"column{u}", [P, 1], I32) for u in range(U)]
        rows = [s.sbuf(f"rows{u}", [P, D], F32) for u in range(U)]
        out = [s.sbuf(f"out{u}", [P, D], F32) for u in range(U)]
        x_turned = [s.sbuf(f"x_turned{n}", [P, 2, P], F32) for n in range(2)]
        silu = [s.sbuf(f"silu{n}", [W, C * P], F32) for n in range(2)]
        inner = [s.sbuf(f"inner{n}", [W, C * P], F32) for n in range(2)]
        ps_x = [s.psum(f"ps_x{n}", [P, 2, P]) for n in range(2)]
        ps_up = [s.psum(f"ps_up{n}", [W, 2, C * P]) for n in range(2)]
        ps_out = [s.psum(f"ps_out{n}", [P, D]) for n in range(2)]
        weights_loaded = [s.sem(f"weights_loaded{u}") for u in range(U)]
        gathered = [s.sem(f"gathered{u}") for u in range(U)]
        stored = [s.sem(f"stored{u}") for u in range(U)]
        column_copied, parted, turned, turned_kept, up_done, silu_done, inner_ready, down_done, out_kept = (
            s.sem(n) for n in ("column_copied", "parted", "turned", "turned_kept", "up_done", "silu_done",
                               "inner_ready", "down_done", "out_kept"))
        block = stack.enter_context(nc.Block())
        most_groups = layer.tiles // U

        def groups(engine):
            return engine.value_load(last_group_at[0:1, 0:1], min_val=1, max_val=most_groups - 1)

        def apart(engine):
            engine.sem_inc(parted, 1)

        @block.sync
        def _(sp):
            sp.dma_start(lists[:], table.rearrange("(p c) a -> p (c a)", p=P)).then_inc(lists_loaded, 16)
            last = groups(sp)

            def load(i, u):
                e = sp.value_load(tile_expert[0:1, bass.ds(i * U + u, 1)], min_val=0, max_val=E - 1)
                sp.dma_start(up_w[u][:], up_dram[bass.ds(e, 1)].rearrange("a p k n -> (a p) k n")).then_inc(weights_loaded[u], 16)
                sp.dma_start(down_w[u][:], down_dram[bass.ds(e, 1)].rearrange("a p k n -> (a p) k n")).then_inc(weights_loaded[u], 16)

            for u in range(U):
                load(0, u)
            with sp.Fori(1, last + 1) as i:
                for u in range(U):
                    sp.wait_ge(down_done, i * U + u - U + 1)
                    load(i, u)

        @block.gpsimd
        def _(pool):
            last = groups(pool)
            pool.wait_ge(lists_loaded, 16)
            apart(pool)

            def gather(i, u):
                c = pool.value_load(tile_column[0:1, bass.ds(i * U + u, 1)], min_val=0, max_val=layer.columns - 1)
                nc.gpsimd.tensor_copy(column[u][:], lists[:, bass.ds(c, 1)]).then_inc(column_copied, 1)
                pool.wait_ge(column_copied, i * U + u + 1)
                apart(pool)
                nc.gpsimd.indirect_dma_start(rows[u][:], None, normed_dram, bass.IndirectOffsetOnAxis(ap=column[u][:], axis=0))\
                    .then_inc(gathered[u], 16)

            for u in range(U):
                gather(0, u)
            with pool.Fori(1, last + 1) as i:
                for u in range(U):
                    pool.wait_ge(turned, i * U + u - U + 1)
                    gather(i, u)

        @block.tensor
        def _(pe):
            last = groups(pe)

            def down(t, u):
                pe.wait_ge(inner_ready, t + 1)
                for c in range(C):
                    op = nc.tensor.matmul(ps_out[u % 2][:], inner[u % 2][:, c * P:(c + 1) * P], down_w[u][:, c, :],
                                          start=c == 0, stop=c == C - 1)
                op.then_inc(down_done, 1)

            def step(i, u, first=False):
                t = i * U + u
                pe.wait_ge(gathered[u], i * 16 + 16)
                for k in range(2):
                    op = nc.tensor.transpose(ps_x[u % 2][:, k, :], rows[u][:, k * P:(k + 1) * P], consts.identity[:])
                op.then_inc(turned, 1)
                if not (first and u < 2):
                    down(t - 2, (u - 2) % U)
                pe.wait_ge(turned_kept, t + 1)
                pe.wait_ge(weights_loaded[u], i * 32 + 32)
                for part in range(2):
                    for c in range(C):
                        at = (part * C + c) * W
                        for k in range(2):
                            op = nc.tensor.matmul(ps_up[u % 2][:, part, c * P:(c + 1) * P], up_w[u][:, k, at:at + W],
                                                  x_turned[u % 2][:, k, :], start=k == 0, stop=k == 1)
                op.then_inc(up_done, 1)

            for u in range(U):
                step(0, u, True)
            with pe.Fori(1, last + 1) as i:
                for u in range(U):
                    step(i, u)
            down(last * U + U - 2, U - 2)
            down(last * U + U - 1, U - 1)

        @block.scalar
        def _(act):
            last = groups(act)

            def store(i, u):
                act.wait_ge(out_kept, i * U + u + 1)
                act.dma_start(rows_out[bass.ds(i * U + u, 1)].rearrange("a p n -> (a p) n"), out[u][:]).then_inc(stored[u], 16)

            def step(i, u, first=False):
                t = i * U + u
                act.wait_ge(turned, t + 1)
                nc.scalar.activation(x_turned[u % 2][:], ps_x[u % 2][:], ACT.Copy).then_inc(turned_kept, 1)
                act.wait_ge(up_done, t + 1)
                nc.scalar.activation(silu[u % 2][:], ps_up[u % 2][:, 0, :], ACT.Silu).then_inc(silu_done, 1)
                if not (first and u < 2):
                    store(i if u >= 2 else i - 1, (u - 2) % U)

            for u in range(U):
                step(0, u, True)
            with act.Fori(1, last + 1) as i:
                for u in range(U):
                    step(i, u)
            store(last, U - 2)
            store(last, U - 1)
            for u in range(U):
                act.wait_ge(stored[u], last * 16 + 32)
                apart(act)

        @block.vector
        def _(dve):
            last = groups(dve)
            for u in range(U):
                dve.sem_inc(stored[u], 16)

            def keep(i, u):
                dve.wait_ge(stored[u], i * 16 + 16)
                dve.wait_ge(down_done, i * U + u + 1)
                nc.vector.tensor_copy(out[u][:], ps_out[u % 2][:]).then_inc(out_kept, 1)

            def step(i, u, first=False):
                if not (first and u < 2):
                    keep(i if u >= 2 else i - 1, (u - 2) % U)
                dve.wait_ge(silu_done, i * U + u + 1)
                nc.vector.tensor_tensor(inner[u % 2][:], silu[u % 2][:], ps_up[u % 2][:, 1, :], ALU.mult).then_inc(inner_ready, 1)

            for u in range(U):
                step(0, u, True)
            with dve.Fori(1, last + 1) as i:
                for u in range(U):
                    step(i, u)
            keep(last, U - 2)
            keep(last, U - 1)


class Plan:

    def __init__(self, nc, s, layer, consts, kept, routing):
        self.nc, self.layer, self.consts, self.kept, self.routing = nc, layer, consts, kept, routing
        E = layer.experts
        self.count = s.sbuf("p_count", [P, E], I32)
        self.tiles = s.sbuf("p_tiles", [P, E], F32)
        self.ends = [s.sbuf(f"p_ends{n}", [P, E], F32) for n in range(2)]
        self.first_row = s.sbuf("p_first_row", [P, E], F32)
        self.rank = s.sbuf("p_rank", [P, B, E], F32)
        self.junk = s.sbuf("p_junk", [P, 8, P], F32)
        self.groups = s.sbuf("p_groups", [P, P], F32)
        self.own = s.sbuf("p_own", [P, 8], F32)
        self.place = s.sbuf("p_place", [P, B, 8], F32)
        self.ps_count, self.ps_row = routing.ps_count, routing.ps_turned
        self.counted, self.own_ready, self.rows_ready = (s.sem("p_" + n) for n in ("counted", "own_ready", "rows_ready"))

    def pe_count(self, pe):
        pe.wait_ge(self.routing.rank_kept, len(GROUPS))
        for b in range(B):
            last = self.nc.tensor.matmul(self.ps_count, self.consts.ones[:], self.kept.mask[:, b, :],
                                         start=b == 0, stop=b == B - 1)
        last.then_inc(self.counted, 1)

    def pe_rows(self, pe):
        pe.wait_ge(self.own_ready, 1)
        for n in range(2):
            last = self.nc.tensor.transpose(self.ps_row[0:1, n, :], self.own[:, n:n + 1], self.consts.identity[:])
        last.then_inc(self.rows_ready, 1)

    def dve_plan(self, dve, link):
        nc, layer, consts, kept = self.nc, self.layer, self.consts, self.kept
        E, U = layer.experts, layer.unroll
        count, tiles, ends, junk, groups = self.count, self.tiles, self.ends, self.junk, self.groups
        expert, col, done_experts, done_tiles, last_group = (self.own[:, n:n + 1] for n in range(5))
        dve.wait_ge(self.counted, 1)
        link(nc.vector.tensor_scalar(count[:], self.ps_count, float(P - 1), None, ALU.add))
        link(nc.vector.tensor_scalar(count[:], count[:], P.bit_length() - 1, None, ALU.logical_shift_right))
        link(nc.vector.tensor_copy(tiles[:], count[:]))
        link(nc.vector.tensor_copy(ends[0][:], tiles[:]))
        n, step = 0, 1
        while step < E:
            link.free(nc.vector.tensor_copy(ends[1 - n][:, 0:step], ends[n][:, 0:step]))
            link(nc.vector.tensor_tensor(ends[1 - n][:, step:], ends[n][:, step:], ends[n][:, 0:E - step], ALU.add))
            n, step = 1 - n, 2 * step
        end = ends[n]
        link.free(nc.vector.tensor_scalar(junk[:, 0, 0:E], end[:], consts.number[:, 0:1], None, ALU.is_le, ALU.add,
                                          accum_out=done_experts))
        link(nc.vector.scalar_tensor_tensor(junk[:, 1, 0:E], end[:], consts.number[:, 0:1], tiles[:], ALU.is_le, ALU.mult,
                                            accum_out=done_tiles))
        link(nc.vector.tensor_scalar(expert, done_experts, float(E - 1), None, ALU.min))
        link(nc.vector.scalar_tensor_tensor(col, expert, float(layer.lists), consts.number[:, 0:1], ALU.mult, ALU.add))
        link(nc.vector.tensor_tensor(col, col, done_tiles, ALU.subtract))
        link(nc.vector.tensor_scalar(col, col, float(layer.columns - 1), None, ALU.min))
        nc.vector.engine_nop().then_inc(self.own_ready, 1)
        most = layer.tiles // U
        link(nc.vector.tensor_scalar(groups[:, 0:most], consts.ramp[:, 0:most], float(U), float(U + 1), ALU.mult, ALU.add))
        link(nc.vector.tensor_scalar(junk[:, 2, 0:most], groups[:, 0:most], end[:, E - 1:E], None, ALU.is_le, ALU.add,
                                     accum_out=last_group))
        link(nc.vector.tensor_copy(kept.last_group_at[:], last_group[0:1, :]))
        link(nc.vector.tensor_tensor(self.first_row[:], end[:], tiles[:], ALU.subtract))
        link(nc.vector.tensor_scalar(self.first_row[:], self.first_row[:], float(P), None, ALU.mult))
        link(nc.vector.tensor_tensor(self.rank[:], kept.rank[:], self.first_row[:].unsqueeze(1).broadcast_to([P, B, E]), ALU.add))
        link(nc.vector.memset(self.place[:], 0.0))
        for b in range(B):
            look_up(nc, link, layer, consts.ramp, kept.index[:, b, :], self.rank[:, b, :], junk[:, :, 0:E], self.place[:, b, :])
        link(nc.vector.tensor_copy(kept.row[:], self.place[:]))
        dve.wait_ge(self.rows_ready, 1)
        link(nc.vector.tensor_copy(kept.tile_expert[:], self.ps_row[0:1, 0, :]))
        link(nc.vector.tensor_copy(kept.tile_column[:], self.ps_row[0:1, 1, :]))


class Gather:

    DEEP = 3

    def __init__(self, nc, s, layer, kept, rows_dram):
        self.nc, self.layer, self.kept = nc, layer, kept
        self.rows_dram = rows_dram.rearrange("t p n -> (t p) n")
        self.rows = [s.sbuf(f"g_rows{n}", [P, layer.chosen, D], F32) for n in range(self.DEEP)]
        self.gathered = [s.sem(f"g_gathered{n}") for n in range(self.DEEP)]
        self.summed = s.sem("g_summed")

    def pool_gather(self, pool, b):
        n = b % self.DEEP
        if b >= self.DEEP:
            pool.wait_ge(self.summed, b - self.DEEP + 1)
        for k in range(self.layer.chosen):
            of = bass.IndirectOffsetOnAxis(ap=self.kept.row[:, b, k:k + 1], axis=0)
            self.nc.gpsimd.indirect_dma_start(self.rows[n][:, k, :], None, self.rows_dram, of)\
                .then_inc(self.gathered[n], 16)

    def dve_sum(self, dve, link, b, x, out):
        nc, n, last = self.nc, b % self.DEEP, self.layer.chosen - 1
        dve.wait_ge(self.gathered[n], 16 * self.layer.chosen * (b // self.DEEP + 1))
        for k in range(last + 1):
            op = nc.vector.scalar_tensor_tensor(out, self.rows[n][:, k, :], self.kept.weight[:, b, k:k + 1], x if k == 0 else out,
                                                ALU.mult, ALU.add)
            if k < last:
                link(op)
        op.then_inc(self.summed, 1)


def features_phase(nc, consts, kept0, kept1, x_all, ctx, ctx_turned, rows_dram, gate_dram, gate_bias_dram, table, normed_dram):
    layer = LAYER1
    scale = 1.0 / float(np.sqrt(D))
    with ExitStack() as stack:
        s = Space(nc, stack, "ft_")
        gate = s.sbuf("gate", [P, 2, layer.experts], F32)
        gate_bias = s.sbuf("gate_bias", [P, layer.experts], F32)
        keys = s.sbuf("keys", [P, B, D], F32)
        vals = s.sbuf("vals", [P, B, 2, P], F32)
        x_sum = s.sbuf("x_sum", [P, B, D], F32)
        norm = Norm(nc, s, "")
        x_norm = s.sbuf("x_norm", [P, B, D], F32)
        top = s.sbuf("top", [P, MOST, 2], F32)
        minus_top = s.sbuf("minus_top", [P, MOST, 2], F32)
        expo = s.sbuf("expo", [P, MOST, 2, D], F32)
        total = s.sbuf("total", [P, MOST, 2], F32)
        share = s.sbuf("share", [P, MOST, 2], F32)
        vals_shared = s.sbuf("vals_shared", [P, MOST, 2, P], F32)
        ps_scores = [s.psum(f"ps_scores{n}", [P, 2, D]) for n in range(MOST)]
        ps_out = [s.psum(f"ps_out{n}", [P, D]) for n in range(2)]
        gather = Gather(nc, s, LAYER0, kept0, rows_dram)
        routing = Routing(nc, s, layer, kept1, consts, gate, gate_bias, table, normed_dram)
        plan = Plan(nc, s, layer, consts, kept1, routing)
        inputs_loaded, link_v = s.sem("inputs_loaded"), s.sem("link_v")
        normed, scored, top_known, expo_ready, vals_ready, attended, x_ready = (
            s.sem(n) for n in ("normed", "scored", "top_known", "expo_ready", "vals_ready", "attended", "x_ready"))
        block = stack.enter_context(nc.Block())
        STEPS = range(len(GROUPS) + 1)

        def of(i):
            return list(enumerate(GROUPS[i])) if i < len(GROUPS) else []

        @block.sync
        def _(sp):
            sp.dma_start(keys[:], ctx.rearrange("b p n -> p b n")).then_inc(inputs_loaded, 16)
            sp.dma_start(vals[:], ctx_turned.rearrange("b p k n -> p b k n")).then_inc(inputs_loaded, 16)
            sp.dma_start(gate[:], gate_dram).then_inc(inputs_loaded, 16)
            sp.dma_start(gate_bias[:], gate_bias_dram).then_inc(inputs_loaded, 16)
            for i in range(len(GROUPS)):
                routing.sp_store(sp, i)
            routing.sp_finish(sp)

        @block.gpsimd
        def _(pool):
            ahead = Gather.DEEP
            for b in range(ahead):
                gather.pool_gather(pool, b)
            for i in range(len(GROUPS)):
                for b in GROUPS[i + 1] if i + 1 < len(GROUPS) else ():
                    if b >= ahead:
                        gather.pool_gather(pool, b)
                routing.pool_scatter(pool, i)
            routing.pool_finish(pool)

        @block.tensor
        def _(pe):
            pe.wait_ge(inputs_loaded, 64)
            for i in STEPS:
                for j, b in of(i):
                    pe.wait_ge(normed, b + 1)
                    if i >= 1:
                        pe.wait_ge(expo_ready, b - j)
                    for c in range(2):
                        op = nc.tensor.matmul(ps_scores[j][:, c, :], keys[:, b, c * P:(c + 1) * P], x_norm[:, b, :], start=True, stop=True)
                    op.then_inc(scored, 1)
                if i >= 1:
                    routing.pe_rank(pe, i - 1)
                for j, b in of(i):
                    pe.wait_ge(vals_ready, b + 1)
                    if b >= 2:
                        pe.wait_ge(x_ready, b - 1)
                    for c in range(2):
                        op = nc.tensor.matmul(ps_out[b % 2][:], vals_shared[:, j, c, :], expo[:, j, c, :], start=c == 0, stop=c == 1)
                    op.then_inc(attended, 1)
                if of(i):
                    routing.pe_turn_and_score(pe, i)
            plan.pe_count(pe)
            plan.pe_rows(pe)

        @block.scalar
        def _(act):
            for i in STEPS:
                if i >= 1:
                    routing.act_exponentials(act, i - 1)
                for j, b in of(i):
                    act.wait_ge(top_known, b + 1)
                    if i >= 1:
                        act.wait_ge(attended, b - j)
                    for c in range(2):
                        op = nc.scalar.activation(expo[:, j, c, :], ps_scores[j][:, c, :], ACT.Exp, bias=minus_top[:, j, c:c + 1],
                                                  scale=scale, accum_out=total[:, j, c:c + 1])
                    op.then_inc(expo_ready, 1)
                for j, b in of(i):
                    routing.act_keep_turned(act, b)

        @block.vector
        def _(dve):
            link = Link(dve, link_v)
            routing.dve_start(link)
            for i in STEPS:
                for j, b in of(i):
                    gather.dve_sum(dve, link, b, x_all[:, b, :], x_sum[:, b, :])
                if of(i):
                    dve.wait_ge(gather.summed, GROUPS[i][-1] + 1)
                    norm(link, GROUPS[i], x_sum, x_norm, normed)
                if i >= 1:
                    if i == 1:
                        dve.wait_ge(inputs_loaded, 64)
                    routing.dve_logits(dve, link, i - 1)
                for j, b in of(i):
                    dve.wait_ge(scored, b + 1)
                    link(nc.vector.reduce_max(top[:, j, :], ps_scores[j][:], AX_X))
                    nc.vector.tensor_scalar(minus_top[:, j, :], top[:, j, :], -scale, None, ALU.mult).then_inc(top_known, 1)
                if i >= 1:
                    routing.dve_choose(dve, link, i - 1)
                for j, b in of(i):
                    dve.wait_ge(expo_ready, b + 1)
                    link(nc.vector.reciprocal(share[:, j, :], total[:, j, :]))
                    for c in range(2):
                        op = nc.vector.tensor_scalar(vals_shared[:, j, c, :], vals[:, b, c, :], share[:, j, c:c + 1], None, ALU.mult)
                    op.then_inc(vals_ready, 1)
                if i >= 1:
                    routing.dve_places(dve, link, i - 1)
                for j, b in of(i):
                    dve.wait_ge(attended, b + 1)
                    nc.vector.tensor_tensor(x_all[:, b, :], x_sum[:, b, :], ps_out[b % 2][:], ALU.add).then_inc(x_ready, 1)
                if of(i):
                    dve.wait_ge(x_ready, GROUPS[i][-1] + 1)
                    routing.dve_normalise(link, i, x_all)
            plan.dve_plan(dve, link)


def last_phase(nc, kept, x_all, rows_dram, out):
    with ExitStack() as stack:
        s = Space(nc, stack, "ls_")
        x_sum = s.sbuf("x_sum", [P, B, D], F32)
        gather = Gather(nc, s, LAYER1, kept, rows_dram)
        link_v, stored = s.sem("link_v"), s.sem("stored")
        block = stack.enter_context(nc.Block())

        @block.sync
        def _(sp):
            for b in range(B):
                sp.wait_ge(gather.summed, b + 1)
                sp.dma_start(out[b], x_sum[:, b, :]).then_inc(stored, 16)
            sp.wait_ge(stored, 16 * B)

        @block.gpsimd
        def _(pool):
            for b in range(B):
                gather.pool_gather(pool, b)

        @block.vector
        def _(dve):
            link = Link(dve, link_v)
            for b in range(B):
                gather.dve_sum(dve, link, b, x_all[:, b, :], x_sum[:, b, :])


def two_layers(nc, x, ctx, ctx_turned, consts_f, token_numbers, weights, biases, rotary, gate0, up0, down0,
               gate1, gate1_bias, up1, down1, out):
    def scratch(name, shape, dtype=F32):
        return nc.dram_tensor(name, shape, dtype, kind="Internal").ap()

    q_stack = scratch("q_stack", [B, TERMS, P, D], BF16)
    k_stack = scratch("k_stack", [B, TERMS, P, D], BF16)
    values = scratch("values", [B, P, 2, H, VW])
    attended = scratch("attended", [B, P, 4, D])
    normed = [scratch(f"normed{n}", [TOKENS, D]) for n in range(2)]
    tables = [scratch(f"table{n}", [P * layer.columns, 1], I32) for n, layer in enumerate((LAYER0, LAYER1))]
    rows = [scratch(f"rows{n}", [layer.tiles, P, D]) for n, layer in enumerate((LAYER0, LAYER1))]
    with ExitStack() as stack:
        s = Space(nc, stack, "")
        consts, kept0, kept1 = Consts(s), Kept(s, LAYER0), Kept(s, LAYER1)
        setup_phase(nc, consts, consts_f, token_numbers, [(LAYER0, tables[0]), (LAYER1, tables[1])])
        with ExitStack() as attention:
            operands = Operands(Space(nc, attention, "op_"), q_stack, k_stack, values)
            project_phase(nc, x, ctx, weights, biases, rotary, operands)
            attend_phase(nc, consts.identity, operands, attended,
                         [to[layer.least:] for layer, to in zip((LAYER0, LAYER1), rows)])
        x_all = s.sbuf("x_all", [P, B, D], F32)
        merge_phase(nc, consts, kept0, x_all, x, weights, biases, attended, gate0, tables[0], normed[0])
        tiles_phase(nc, LAYER0, consts, kept0, tables[0], normed[0], up0, down0, rows[0])
        features_phase(nc, consts, kept0, kept1, x_all, ctx, ctx_turned, rows[0], gate1, gate1_bias, tables[1], normed[1])
        tiles_phase(nc, LAYER1, consts, kept1, tables[1], normed[1], up1, down1, rows[1])
        last_phase(nc, kept1, x_all, rows[1], out)


def laid_out(x, ctx_2048, L0_xattn_encoding, L0_xattn_Wq, L0_xattn_bq, L0_xattn_Wk, L0_xattn_bk, L0_xattn_Wv,
             L0_xattn_bv, L0_xattn_Wm, L0_xattn_bm, L0_ffn_gate_w, L0_ffn_w13, L0_ffn_w2, L1_ffn_router_w,
             L1_ffn_expert_bias, L1_ffn_gate_proj, L1_ffn_up_proj, L1_ffn_down_proj):
    at = np.arange(P)
    identity = np.eye(P, dtype=np.float32)
    earlier = (at[:, None] < at[None, :]).astype(np.float32)
    ramp = np.broadcast_to(at.astype(np.float32), (P, P))
    sign = np.where(at // H % 2 == 0, -1.0, 1.0).astype(np.float32)
    swap = at ^ H
    bq, bk = L0_xattn_bq, L0_xattn_bk
    rotary = np.repeat(L0_xattn_encoding[:, 0, 0].transpose(2, 0, 1), H, axis=0)

    def by_contraction(w):
        return w.reshape(w.shape[0], 2, P, -1).transpose(0, 2, 1, 3)

    def gates(w):
        return w.T.reshape(2, P, -1).transpose(1, 0, 2)

    up1 = np.concatenate([L1_ffn_gate_proj, L1_ffn_up_proj], axis=2)
    return {
        "x": x,
        "ctx": ctx_2048,
        "ctx_turned": ctx_2048.transpose(0, 2, 1).reshape(B, 2, P, P).transpose(0, 2, 1, 3),
        "consts_f": np.stack([identity, earlier, ramp], axis=1),
        "token_numbers": (at[:, None] + P * np.arange(B)[None, :]).astype(np.int32),
        "weights": np.stack([w.T for w in (L0_xattn_Wq, L0_xattn_Wk, L0_xattn_Wv, L0_xattn_Wm)], axis=1),
        "biases": np.stack([bq, bk, L0_xattn_bv, L0_xattn_bm, bq[swap], bk[swap], sign], axis=1),
        "rotary": rotary,
        "gate0": gates(L0_ffn_gate_w),
        "up0": by_contraction(L0_ffn_w13.transpose(0, 2, 1)),
        "down0": L0_ffn_w2.transpose(0, 2, 1).reshape(LAYER0.experts, 1, P, D).transpose(0, 2, 1, 3),
        "gate1": gates(L1_ffn_router_w),
        "gate1_bias": np.broadcast_to(L1_ffn_expert_bias, (P, LAYER1.experts)),
        "up1": by_contraction(up1),
        "down1": L1_ffn_down_proj.reshape(LAYER1.experts, LAYER1.chunks, LAYER1.width, D).transpose(0, 2, 1, 3),
    }


def kernel(**inputs):
    import concourse.bacc as bacc
    from concourse.bass_utils import run_bass_kernel_spmd

    nc = bacc.Bacc("TRN2", target_bir_lowering=False, num_devices=1)
    arrays, args = {}, []
    for name, a in laid_out(**{k: np.asarray(v) for k, v in inputs.items()}).items():
        a = np.ascontiguousarray(a)
        arrays["in_" + name] = a
        args.append(nc.dram_tensor("in_" + name, a.shape, mybir.dt.from_np(a.dtype), kind="ExternalInput").ap())
    out = nc.dram_tensor("out", (B, P, D), F32, kind="ExternalOutput").ap()
    two_layers(nc, *args, out)
    result = run_bass_kernel_spmd(nc, [arrays], core_ids=[0])
    return result.results[0]["out"]
```

```python
from contextlib import ExitStack

import numpy as np

import concourse.bass as bass
from concourse import mybir

P = 128
B = 8
D = 256
TOKENS = B * P
H = 16
HD = P // H
EPS = 1e-5
NEWTON = 3
MOST = 3
WARM_UP = 24
PARTS = 3
TERMS = 6
STACK = TERMS * HD
TOP = 96
ROWS = TOP + PARTS
DEEP = 4
ONES_PAIR = float(np.array([0x3F803F80], np.uint32).view(np.float32)[0])
VW = 32

F32 = mybir.dt.float32
BF16 = mybir.dt.bfloat16
I32 = mybir.dt.int32
U32 = mybir.dt.uint32
ALU = mybir.AluOpType
ACT = mybir.ActivationFunctionType
AX_X = mybir.AxisListType.X


class Layer:

    def __init__(self, name, experts, chosen, inter, unroll, groups, by_token):
        self.groups = groups
        self.by_token = by_token
        self.name, self.experts, self.chosen, self.inter, self.unroll = name, experts, chosen, inter, unroll
        self.chunks = -(-inter // P)
        self.width = inter // self.chunks
        self.lists = TOKENS // P
        self.columns = experts * self.lists
        self.list_columns = self.columns + unroll
        most = TOKENS * chosen // P + experts - 1
        self.tiles = -(-most // unroll) * unroll
        self.least = TOKENS * chosen // P
        assert self.width * self.chunks == inter and self.tiles <= P


LAYER0 = Layer("l0_", 64, 8, 128, 8, ((0, 1), (2, 3), (4, 5, 6), (7,)), False)
LAYER1 = Layer("l1_", 16, 4, 224, 6, ((0, 1), (2, 3, 4), (5, 6, 7)), True)


class Link:

    def __init__(self, engine, semaphore):
        self.engine, self.semaphore, self.count = engine, semaphore, 0

    def free(self, instruction):
        self.count += 1
        instruction.then_inc(self.semaphore, 1)

    def __call__(self, instruction):
        self.free(instruction)
        self.engine.wait_ge(self.semaphore, self.count)


class Space:

    def __init__(self, nc, stack, prefix):
        self.nc, self.stack, self.prefix = nc, stack, prefix
        self.semaphores = []
        stack.callback(self.clear)

    def sbuf(self, name, shape, dtype):
        return self.stack.enter_context(self.nc.sbuf_tensor(self.prefix + name, shape, dtype))

    def psum(self, name, shape, dtype=F32):
        return self.stack.enter_context(self.nc.psum_tensor(self.prefix + name, shape, dtype))

    def sem(self, name):
        self.semaphores.append(self.nc.alloc_semaphore(self.prefix + name))
        return self.semaphores[-1]

    def clear(self):
        if self.semaphores:
            self.nc.clear_and_free_semaphores(self.semaphores)
            self.nc.all_engine_barrier()


def span(group):
    return slice(group[0], group[-1] + 1)


class Norm:

    def __init__(self, nc, s, name, most):
        self.nc = nc
        self.stats = s.sbuf(name + "stats", [P, most, 6], F32)
        self.mean_var = s.sbuf(name + "mean_var", [P, most, 2], F32)
        self.root = s.sbuf(name + "root", [P, 4, most], F32)

    def __call__(self, link, group, x, x_norm, normed):
        nc, n = self.nc, len(group)
        for j, b in enumerate(group):
            link.free(nc.vector.bn_stats(self.stats[:, j, :], x[:, b, :]))
        link.engine.wait_ge(link.semaphore, link.count)
        for j in range(n):
            link.free(nc.vector.bn_aggr(self.mean_var[:, j, :], self.stats[:, j, :]))
        link.engine.wait_ge(link.semaphore, link.count)
        variance = self.mean_var[:, 0:n, 1]
        root, work, half, full = (self.root[:, k, 0:n] for k in range(4))
        link.free(nc.vector.tensor_scalar(half, variance, EPS, -0.5, ALU.add, ALU.mult))
        link(nc.vector.tensor_scalar(full, variance, EPS, None, ALU.add))
        link(nc.vector.tensor_scalar(work.bitcast(I32), full.bitcast(I32), 1, None, ALU.logical_shift_right))
        link(nc.vector.tensor_scalar(root.bitcast(I32), work.bitcast(I32), -1.0, float(0x5F3759DF), ALU.mult, ALU.add))
        for _ in range(NEWTON):
            link(nc.vector.tensor_tensor(work, root, root, ALU.mult))
            link(nc.vector.tensor_tensor(work, work, half, ALU.mult))
            link(nc.vector.scalar_tensor_tensor(root, work, 1.5, root, ALU.add, ALU.mult))
        for j, b in enumerate(group):
            nc.vector.tensor_scalar(x_norm[:, b, :], x[:, b, :], self.mean_var[:, j, 0:1], self.root[:, 0, j:j + 1],
                                    ALU.subtract, ALU.mult).then_inc(normed, 1)


class Operands:

    SLOTS = TERMS + PARTS
    FIRST, MIDDLE, LOW = slice(0, 7, 6), slice(3, 8, 4), slice(5, 9, 3)
    LOADS = PARTS + 1
    OUT = 4

    def __init__(self, s, parts_dram):
        self.parts_dram = parts_dram
        self.q = [s.sbuf(f"q_in{n}", [ROWS, H * D], BF16) for n in range(DEEP)]
        self.k = [s.sbuf(f"k_in{n}", [ROWS, H * D], BF16) for n in range(DEEP)]
        self.v = s.sbuf("v_in", [P, B, 2, H, VW], F32)
        self.parts = [s.sbuf(f"parts{n}", [P, self.SLOTS, D], BF16) for n in range(self.OUT)]
        self.stored = [s.sem(f"stored{n}") for n in range(self.OUT)]
        self.loaded = [s.sem(f"loaded{n}") for n in range(DEEP)]
        self.rows_set = s.sem("rows_set")

    def set_rows(self, nc, pool, n):
        nc.gpsimd.memset(self.k[n][0:TOP].bitcast(F32), 0.0)
        nc.gpsimd.memset(self.q[n][0:TOP].bitcast(F32), 0.0).then_inc(self.rows_set, 1)
        pool.wait_ge(self.rows_set, 2 * n + 1)
        nc.gpsimd.memset(self.k[n][TOP:ROWS].bitcast(F32), ONES_PAIR).then_inc(self.rows_set, 1)
        pool.wait_ge(self.rows_set, 2 * n + 2)

    def load(self, engine, b):
        n = b % DEEP
        if b < DEEP:
            engine.wait_ge(self.rows_set, 2 * (b + 1))
        engine.wait_ge(self.stored[b % self.OUT], 16 * (b // self.OUT + 1))
        q_from = self.parts_dram[b, 0:TERMS].rearrange("t (d h) n -> (t d) (h n)", h=H)
        engine.dma_start(self.q[n][0:STACK, :], q_from).then_inc(self.loaded[n], 16)
        row = 0
        for i in range(PARTS):
            m = PARTS - i
            k_from = self.parts_dram[b, TERMS:TERMS + m].rearrange("t (d h) n -> (t d) (h n)", h=H)
            engine.dma_start(self.k[n][row:row + m * HD, :], k_from).then_inc(self.loaded[n], 16)
            row += m * HD


class Setup:

    def __init__(self, nc, s, consts, consts_f, token_numbers, choice_numbers, spare_rows, table0, table1):
        self.nc, self.consts, self.consts_f, self.spare_rows = nc, consts, consts_f, spare_rows
        self.token_numbers, self.choice_numbers, self.table0, self.table1 = token_numbers, choice_numbers, table0, table1
        self.loaded = s.sbuf("loaded", [P, 3, P], F32)
        self.zeros = s.sbuf("zeros", [P, LAYER0.columns], I32)
        self.arrived, self.zeros_set, self.zeroed = s.sem("consts_arrived"), s.sem("zeros_set"), s.sem("zeroed")

    def sp_load(self, sp):
        sp.dma_start(self.loaded[:], self.consts_f).then_inc(self.arrived, 16)
        sp.dma_start(self.consts.token[:], self.token_numbers).then_inc(self.arrived, 16)
        sp.dma_start(self.consts.choice[:], self.choice_numbers).then_inc(self.arrived, 16)

    def sp_zero(self, sp):
        sp.wait_ge(self.zeros_set, 1)
        sp.dma_start(self.table0.rearrange("(p c) a -> p (c a)", p=P), self.zeros[:]).then_inc(self.zeroed, 16)
        sp.dma_start(self.table1.rearrange("(p c) a -> p (c a)", p=P), self.spare_rows[:, 0:LAYER1.columns]).then_inc(self.zeroed, 16)

    def sp_finish(self, sp):
        sp.wait_ge(self.zeroed, 32)

    def dve_consts(self, dve, link):
        nc, consts, loaded = self.nc, self.consts, self.loaded
        nc.vector.memset(consts.ones[:], 1.0)
        dve.wait_ge(self.arrived, 48)
        nc.vector.tensor_copy(consts.identity[:], loaded[:, 0, :])
        nc.vector.tensor_copy(consts.earlier[:], loaded[:, 1, :])
        nc.vector.tensor_copy(consts.ramp[:], loaded[:, 2, :])
        link(nc.vector.reduce_sum(consts.number[:], loaded[:, 1, :], AX_X))
        link(nc.vector.tensor_scalar(consts.number[:], consts.number[:], -1.0, float(P - 1), ALU.mult, ALU.add))


def project_phase(nc, x, x_all, ctx, weights, biases, rotary, operands, *constants):
    parts_dram, parts, stored = operands.parts_dram, operands.parts, operands.stored
    OUT = operands.OUT
    with ExitStack() as stack:
        s = Space(nc, stack, "pj_")
        w = s.sbuf("w", [P, 4, P], F32)
        setup = Setup(nc, s, *constants)
        w_turned = s.sbuf("w_turned", [P, 2, P], F32)
        bias = s.sbuf("bias", [P, 7], F32)
        bias_turned = s.sbuf("bias_turned", [P, 2], F32)
        rot = s.sbuf("rot", [P, 2, D], F32)
        c_in = s.sbuf("c_in", [P, B, D], F32)
        x_norm = s.sbuf("x_norm", [P, B, D], F32)
        norm = Norm(nc, s, "", B - 1)
        straight = s.sbuf("straight", [P, 2, D], F32)
        turned = s.sbuf("turned", [P, 2, D], F32)
        full = [s.sbuf(f"full{n}", [P, 2, D], F32) for n in range(3)]
        rest = [s.sbuf(f"rest{n}", [P, 2, D], F32) for n in range(2)]
        ps_qk = [s.psum(f"ps_qk{n}", [P, 2, 2, D]) for n in range(2)]
        ps_v = [s.psum(f"ps_v{n}", [P, 2, P]) for n in range(2)]
        consts_loaded, link_v, x_loaded, c_loaded = (s.sem(n) for n in ("consts_loaded", "link_v", "x_loaded", "c_loaded"))
        first_x_loaded, first_c_loaded = s.sem("first_x_loaded"), s.sem("first_c_loaded")
        w_ready, normed, projected, roped = s.sem("w_ready"), s.sem("normed"), s.sem("projected"), s.sem("roped")
        summed, high_cut, rest_ready, mid_cut, low_cut = (
            s.sem(n) for n in ("summed", "high_cut", "rest_ready", "mid_cut", "low_cut"))
        ones_set, v_kept = s.sem("ones_set"), s.sem("v_kept")
        block = stack.enter_context(nc.Block())

        @block.sync
        def _(sp):
            sp.dma_start(x_all[:, 0, :], x[0]).then_inc(first_x_loaded, 16)
            sp.dma_start(w[:], weights).then_inc(consts_loaded, 16)
            sp.dma_start(c_in[:, 0, :], ctx[0]).then_inc(first_c_loaded, 16)
            sp.dma_start(bias[:], biases).then_inc(consts_loaded, 16)
            sp.dma_start(rot[:], rotary).then_inc(consts_loaded, 16)
            sp.dma_start(x_all[:, 1:, :], x[1:].rearrange("b p n -> p b n")).then_inc(x_loaded, 16)
            sp.dma_start(c_in[:, 1:, :], ctx[1:].rearrange("b p n -> p b n")).then_inc(c_loaded, 16)
            setup.sp_load(sp)
            setup.sp_zero(sp)
            for b in range(B):
                n = b % OUT
                sp.wait_ge(low_cut, b + 1)
                sp.dma_start(parts_dram[b].rearrange("t p n -> p t n"), parts[n][:]).then_inc(stored[n], 16)
                if 2 <= b < DEEP + 1:
                    operands.load(sp, b - 2)
            setup.sp_finish(sp)

        @block.tensor
        def _(pe):
            pe.wait_ge(w_ready, 1)
            for b in range(B):
                n = b % 2
                if b >= 2:
                    pe.wait_ge(roped, b - 1)
                    pe.wait_ge(v_kept, b - 1)
                pe.wait_ge(normed, b + 1)
                nc.tensor.matmul(ps_qk[n][:, 0, 0, :], w[:, 0, :], x_norm[:, b, :], start=True, stop=True)
                nc.tensor.matmul(ps_qk[n][:, 0, 1, :], w_turned[:, 0, :], x_norm[:, b, :], start=True, stop=True)
                if b < 2:
                    pe.wait_ge(c_loaded if b else first_c_loaded, 16)
                nc.tensor.matmul(ps_qk[n][:, 1, 0, :], w[:, 1, :], c_in[:, b, :], start=True, stop=True)
                nc.tensor.matmul(ps_qk[n][:, 1, 1, :], w_turned[:, 1, :], c_in[:, b, :], start=True, stop=True)
                for m in range(2):
                    last = nc.tensor.matmul(ps_v[n][:, m, :], c_in[:, b, m * P:(m + 1) * P], w[:, 2, :],
                                            start=True, stop=True)
                last.then_inc(projected, 1)

        @block.vector
        def _(dve):
            link = Link(dve, link_v)
            nc.vector.memset(setup.zeros[:], 0).then_inc(setup.zeros_set, 1)
            dve.wait_ge(first_x_loaded, 16)
            norm(link, (0,), x_all, x_norm, normed)
            dve.wait_ge(consts_loaded, 48)
            for t in range(2):
                to = w_turned[:, t, :].rearrange("p (j s h) -> p j s h", s=2, h=H)
                of = w[:, t, :].rearrange("p (j s h) -> p j s h", s=2, h=H)
                nc.vector.tensor_scalar(to[:, :, 0, :], of[:, :, 1, :], -1.0, None, ALU.mult)
                last = nc.vector.tensor_copy(to[:, :, 1, :], of[:, :, 0, :])
            last.then_inc(w_ready, 1)
            link(nc.vector.tensor_scalar(bias_turned[:], bias[:, 4:6], bias[:, 6:7], None, ALU.mult))
            dve.wait_ge(x_loaded, 16)
            dve.wait_ge(normed, 1)
            norm(link, tuple(range(1, B)), x_all, x_norm, normed)
            for b in range(B):
                n = b % 2
                dve.wait_ge(projected, b + 1)
                if b >= 1:
                    dve.wait_ge(summed, b)
                for t in range(2):
                    nc.vector.scalar_tensor_tensor(straight[:, t, :], ps_qk[n][:, t, 0, :], bias[:, t:t + 1],
                                                   rot[:, 0, :], ALU.add, ALU.mult)
                    last = nc.vector.scalar_tensor_tensor(turned[:, t, :], ps_qk[n][:, t, 1, :],
                                                          bias_turned[:, t:t + 1], rot[:, 1, :], ALU.add, ALU.mult)
                last.then_inc(roped, 1)
                dve.wait_ge(roped, b + 1)
                if b >= 3:
                    dve.wait_ge(rest_ready, b - 2)
                nc.vector.tensor_tensor(full[b % 3][:], straight[:], turned[:], ALU.add).then_inc(summed, 1)
            setup.dve_consts(dve, link)

        @block.gpsimd
        def _(pool):
            def cut_low(b):
                pool.wait_ge(mid_cut, b + 1)
                nc.gpsimd.tensor_tensor(parts[b % OUT][:, Operands.LOW, :], rest[b % 2][:], parts[b % OUT][:, Operands.MIDDLE, :],
                                        ALU.subtract).then_inc(low_cut, 1)

            for b in range(B):
                nc.gpsimd.memset(operands.v[:, b], 1.0).then_inc(ones_set, 1)
            for n in range(2):
                operands.set_rows(nc, pool, n)
            for b in range(B):
                n = b % 3
                pool.wait_ge(high_cut, b + 1)
                if b >= 2:
                    pool.wait_ge(low_cut, b - 1)
                nc.gpsimd.tensor_tensor(rest[b % 2][:], full[n][:], parts[b % OUT][:, Operands.FIRST, :], ALU.subtract).then_inc(rest_ready, 1)
                if b >= 1:
                    cut_low(b - 1)
                if b == 3:
                    operands.set_rows(nc, pool, 2)
            cut_low(B - 1)

        @block.scalar
        def _(act):
            def cut(b, of, q_slot, times, k_slot):
                nc.scalar.activation(parts[b % OUT][:, q_slot:q_slot + times, :], of[:, 0:1, :].broadcast_to([P, times, D]), ACT.Copy)
                return nc.scalar.activation(parts[b % OUT][:, k_slot, :], of[:, 1, :], ACT.Copy)

            def cut_mid(b):
                act.wait_ge(rest_ready, b + 1)
                cut(b, rest[b % 2], TERMS - 3, 2, TERMS + 1).then_inc(mid_cut, 1)

            for b in range(B):
                n = b % 3
                act.wait_ge(ones_set, b + 1)
                act.wait_ge(projected, b + 1)
                nc.scalar.activation(operands.v[:, b, :, :, 0:HD], ps_v[b % 2][:].rearrange("p m (d h) -> p m h d", h=H),
                                     ACT.Copy).then_inc(v_kept, 1)
                act.wait_ge(summed, b + 1)
                if b >= OUT:
                    act.wait_ge(stored[b % OUT], 16 * (b // OUT))
                cut(b, full[n], 0, 3, TERMS).then_inc(high_cut, 1)
                if b >= 1:
                    cut_mid(b - 1)
            cut_mid(B - 1)


def attend_phase(nc, identity, operands, attended, tails, inputs):
    scale = 1.0 / float(np.sqrt(HD))
    HALF = H // 2
    HALVES = 2 * B
    LEAD = H + 4
    q_in, k_in, v_in, loaded = operands.q, operands.k, operands.v, operands.loaded
    with ExitStack() as stack:
        s = Space(nc, stack, "at_")
        top = s.sbuf("top", [P, 2 * H], F32)
        top_rest = s.sbuf("top_rest", [P, 2, 2 * HALF], F32)
        top_parts = s.sbuf("top_parts", [P, 2, PARTS, 2 * HALF], F32)
        top_cut = s.sbuf("top_cut", [P, 2 * HALF], BF16)
        top_rows = [s.sbuf(f"top_rows{n}", [PARTS * 2 * HALF, P], BF16) for n in range(2)]
        RING, TOPS, SCORES = 12, 2, 3
        prob = [s.sbuf(f"prob{n}", [P, 2, D], F32) for n in range(RING)]
        out = [s.sbuf(f"out{n}", [P, 4, D], F32) for n in range(2)]
        ps_top = [s.psum(f"ps_top{n}", [P, 2, D]) for n in range(TOPS)]
        ps_score = [s.psum(f"ps_score{n}", [P, 2, D]) for n in range(SCORES)]
        ps_out = [s.psum(f"ps_out{n}", [P, 2, D]) for n in range(2)]
        ps_rows = s.psum("ps_rows", [P, P])
        zeros = s.sbuf("zeros", [P, D], F32)
        zeros_set, tails_zeroed, link_g = s.sem("zeros_set"), s.sem("tails_zeroed"), s.sem("link_g")
        top_scored, top_found, parts_cut, rows_turned, rows_kept = (
            s.sem(n) for n in ("top_scored", "top_found", "parts_cut", "rows_turned", "rows_kept"))
        rows_placed = [s.sem(f"rows_placed{n}") for n in range(2)]
        scored, prob_ready, weighted, out_kept = (
            s.sem(n) for n in ("scored", "prob_ready", "weighted", "out_kept"))
        stored = [s.sem(f"stored{n}") for n in range(2)]
        block = stack.enter_context(nc.Block())

        def columns(at, half=None):
            first = at % H * D + (half or 0) * P
            return slice(first, first + (D if half is None else P))

        @block.sync
        def _(sp):
            def place(hh):
                b, half = hh // 2, hh % 2
                sp.wait_ge(rows_kept, hh + 1)
                for i in range(PARTS):
                    to = q_in[b % DEEP][TOP + i:TOP + i + 1, half * HALF * D:(half + 1) * HALF * D]
                    sp.dma_start(to.rearrange("a (r n) -> a r n", n=P),
                                 top_rows[half][i * 2 * HALF:(i + 1) * 2 * HALF, :]).then_inc(rows_placed[half], 16)

            operands.load(sp, DEEP - 1)
            for hh in range(3):
                place(hh)
            for b in range(B):
                if 2 * b + 3 < HALVES:
                    place(2 * b + 3)
                if b + DEEP < B:
                    sp.wait_ge(weighted, 4 * (b + 1))
                    operands.load(sp, b + DEEP)
                sp.wait_ge(out_kept, 2 * b + 2)
                sp.dma_start(attended[b], out[b % 2][:]).then_inc(stored[b % 2], 16)
                if 2 * b + 4 < HALVES:
                    place(2 * b + 4)
                if b == 1:
                    inputs.load_weights(sp)
                if 2 <= b < 2 + inputs.SUMS:
                    sp.wait_ge(stored[b % 2], 16 * (b // 2))
                    inputs.load_sums(sp, b - 2)
            for n in range(2):
                sp.wait_ge(stored[n], 16 * (B // 2))

        @block.gpsimd
        def _(pool):
            operands.set_rows(nc, pool, DEEP - 1)
            nc.gpsimd.memset(zeros[:], 0.0).then_inc(zeros_set, 1)
            pool.wait_ge(zeros_set, 1)
            link, pieces = Link(pool, link_g), 0
            for hh in range(HALVES):
                half = hh % 2
                if hh >= 4:
                    for tail in tails:
                        share = -(-tail.shape[0] // (HALVES - 4))
                        first, end = (hh - 4) * share, min((hh - 3) * share, tail.shape[0])
                        if first < end:
                            pool.dma_start(tail[first:end].rearrange("t p n -> p t n"), zeros[:].unsqueeze(1)
                                           .broadcast_to([P, end - first, D])).then_inc(tails_zeroed, 16)
                            pieces += 1
                pool.wait_ge(top_found, (hh + 1) * HALF)
                if hh >= 2:
                    pool.wait_ge(rows_turned, hh - 1)
                tops = top[:, half * 2 * HALF:(half + 1) * 2 * HALF]
                part, rest = top_parts[:, half], top_rest[:, half]
                link(nc.gpsimd.tensor_scalar(top_cut[:], tops, -1.0, None, ALU.mult))
                link(nc.gpsimd.tensor_copy(part[:, 0, :], top_cut[:]))
                link(nc.gpsimd.tensor_tensor(rest, tops, part[:, 0, :], ALU.add))
                link(nc.gpsimd.tensor_scalar(top_cut[:], rest, -1.0, None, ALU.mult))
                link(nc.gpsimd.tensor_copy(part[:, 1, :], top_cut[:]))
                link(nc.gpsimd.tensor_tensor(rest, rest, part[:, 1, :], ALU.add))
                nc.gpsimd.tensor_scalar(part[:, 2, :], rest, -1.0, None, ALU.mult).then_inc(parts_cut, 1)
            pool.wait_ge(tails_zeroed, 16 * pieces)

        @block.tensor
        def _(pe):
            def score_for_top(at):
                n = at // H % DEEP
                if at % H == 0:
                    pe.wait_ge(loaded[n], 16 * Operands.LOADS * (at // H // DEEP + 1))
                if at >= TOPS:
                    pe.wait_ge(top_found, at - TOPS + 1)
                for half in range(2):
                    last = nc.tensor.matmul(ps_top[at % TOPS][:, half, :], q_in[n][0:TOP, columns(at, half)],
                                            k_in[n][0:TOP, columns(at)], start=True, stop=True)
                last.then_inc(top_scored, 1)

            def turn_tops(hh):
                pe.wait_ge(parts_cut, hh + 1)
                if hh >= 1:
                    pe.wait_ge(rows_kept, hh)
                nc.tensor.transpose(ps_rows[0:PARTS * 2 * HALF, :], top_parts[:, hh % 2].rearrange("p i c -> p (i c)"),
                                    identity[:]).then_inc(rows_turned, 1)

            def score(at):
                n = at // H % DEEP
                if at % HALF == 0:
                    pe.wait_ge(rows_placed[at // HALF % 2], 16 * PARTS * (at // H + 1))
                if at >= SCORES:
                    pe.wait_ge(prob_ready, at - SCORES + 1)
                for half in range(2):
                    last = nc.tensor.matmul(ps_score[at % SCORES][:, half, :], k_in[n][0:ROWS, columns(at, half)],
                                            q_in[n][0:ROWS, columns(at)], start=True, stop=True)
                last.then_inc(scored, 1)

            def weigh(group, half):
                b, g = group // 4, group % 4
                if half == 0:
                    pe.wait_ge(prob_ready, 4 * group + 4)
                    if b >= 1 and g % 2 == 0:
                        pe.wait_ge(out_kept, 2 * (b - 1) + g // 2 + 1)
                for j in range(4):
                    last = nc.tensor.matmul(ps_out[g // 2][32 * j:32 * j + VW, g % 2, :], v_in[:, b, half, 4 * g + j, :],
                                            prob[(4 * group + j) % RING][:, half, :], start=half == 0, stop=half == 1,
                                            skip_group_check=True)
                if half == 1:
                    last.then_inc(weighted, 1)

            for at in range(-LEAD, B * H + 4):
                if 0 <= at < B * H:
                    score(at)
                if at + LEAD < B * H:
                    score_for_top(at + LEAD)
                if at >= 4 and at % 4 == 1:
                    weigh(at // 4 - 1, 0)
                if at >= 4 and at % 4 == 3:
                    weigh(at // 4 - 1, 1)
                hh, late = divmod(at + LEAD - 4, HALF)
                if late == HALF - 1 and 0 <= hh < HALVES:
                    turn_tops(hh)
                if at == -1:
                    for _ in range(WARM_UP):
                        nc.tensor.matmul(ps_score[0][:, 0, :], k_in[0][0:TOP, 0:P], k_in[0][0:TOP, 0:D], start=True, stop=True)

        @block.vector
        def _(dve):
            for at in range(B * H):
                dve.wait_ge(top_scored, at + 1)
                if at >= H and at % HALF == 0:
                    dve.wait_ge(parts_cut, at // HALF - 1)
                h = at % H
                nc.vector.reduce_max(top[:, 2 * h:2 * h + 2], ps_top[at % TOPS][:], AX_X).then_inc(top_found, 1)

        @block.scalar
        def _(act):
            def keep_rows(hh):
                act.wait_ge(rows_turned, hh + 1)
                if hh >= 2:
                    act.wait_ge(rows_placed[hh % 2], 16 * PARTS * (hh // 2))
                nc.scalar.activation(top_rows[hh % 2][:], ps_rows[0:PARTS * 2 * HALF, :], ACT.Copy).then_inc(rows_kept, 1)

            def keep_out(pair):
                b = pair // 2
                act.wait_ge(weighted, 2 * pair + 2)
                if b >= 2:
                    act.wait_ge(stored[b % 2], 16 * (b // 2))
                nc.scalar.activation(out[b % 2][:, 2 * (pair % 2):2 * (pair % 2) + 2, :], ps_out[pair % 2][:],
                                     ACT.Copy).then_inc(out_kept, 1)

            for at in range(-LEAD, B * H + 5):
                if 0 <= at < B * H:
                    act.wait_ge(scored, at + 1)
                    if at >= RING:
                        act.wait_ge(weighted, (at - RING) // 4 + 1)
                    nc.scalar.activation(prob[at % RING][:], ps_score[at % SCORES][:], ACT.Exp, scale=scale).then_inc(prob_ready, 1)
                hh, late = divmod(at + LEAD - 5, HALF)
                if late == HALF - 1 and 0 <= hh < HALVES:
                    keep_rows(hh)
                if at >= HALF + 4 and at % HALF == 4:
                    keep_out(at // HALF - 1)


class Kept:

    def __init__(self, s, layer):
        E, n = layer.experts, layer.name
        self.rank = s.sbuf(n + "rank", [P, B, E], F32)
        self.index = s.sbuf(n + "index", [P, B, 8], F32)
        self.weight = s.sbuf(n + "weight", [P, B, 8], F32)
        self.mask = s.sbuf(n + "mask", [P, B, E], BF16)
        self.row = s.sbuf(n + "row", [P, B, 8], I32)
        self.tile_column = s.sbuf(n + "tile_column", [1, P], I32)
        self.tile_expert = s.sbuf(n + "tile_expert", [1, P], I32)
        self.groups_between = s.sbuf(n + "groups_between", [1, 1], I32)


class Consts:

    def __init__(self, s):
        self.identity = s.sbuf("identity", [P, P], F32)
        self.earlier = s.sbuf("earlier", [P, P], BF16)
        self.ones = s.sbuf("ones", [P, P], BF16)
        self.ramp = s.sbuf("ramp", [P, P], F32)
        self.number = s.sbuf("number", [P, 1], F32)
        self.token = s.sbuf("token", [P, B], I32)
        self.choice = s.sbuf("choice", [P, B, LAYER1.chosen], I32)


class Experts:

    def __init__(self, s, layer, kept, up_dram, down_dram=None):
        self.layer, self.kept = layer, kept
        U = range(layer.unroll)
        if down_dram is None:
            both = [s.sbuf(f"w{u}", [P, 3, D], F32) for u in U]
            self.up, self.down = [w[:, 0:2, :] for w in both], [w[:, 2:3, :] for w in both]
            self.transfers = [(both, up_dram)]
        else:
            self.up = [s.sbuf(f"up_w{u}", [P, 2, 2 * layer.inter], F32) for u in U]
            self.down = [s.sbuf(f"down_w{u}", [layer.width, layer.chunks, D], F32) for u in U]
            self.transfers = [(self.up, up_dram), (self.down, down_dram)]
        self.loaded = [s.sem(f"weights_loaded{u}") for u in U]

    def load(self, sp, i, u):
        at = bass.ds(i * self.layer.unroll + u, 1)
        e = sp.value_load(self.kept.tile_expert[0:1, at], min_val=0, max_val=self.layer.experts - 1)
        for to, of in self.transfers:
            sp.dma_start(to[u][:], of[bass.ds(e, 1)].rearrange("a p k n -> (a p) k n")).then_inc(self.loaded[u], 16)

    def load_first(self, sp, planned):
        sp.wait_ge(planned, 1)
        sp.sem_inc(planned, 1)
        for u in range(self.layer.unroll):
            self.load(sp, 0, u)


class MergeInputs:

    SUMS = 3

    def __init__(self, s, attended, weights, biases, gate):
        self.attended, self.weights, self.biases, self.gate_dram = attended, weights, biases, gate
        self.w = s.sbuf("w", [P, P], F32)
        self.bias = s.sbuf("bias", [P, 7], F32)
        self.gate = s.sbuf("gate", [P, 2, LAYER0.experts], F32)
        self.sums = [s.sbuf(f"sums_in{n}", [P, 4, D], F32) for n in range(self.SUMS)]
        self.weights_loaded = s.sem("weights_loaded")
        self.sums_loaded = [s.sem(f"sums_loaded{n}") for n in range(self.SUMS)]

    def load_weights(self, sp):
        sp.dma_start(self.w[:], self.weights[:, 3, :]).then_inc(self.weights_loaded, 16)
        sp.dma_start(self.bias[:], self.biases).then_inc(self.weights_loaded, 16)
        sp.dma_start(self.gate[:], self.gate_dram).then_inc(self.weights_loaded, 16)

    def load_sums(self, sp, b):
        sp.dma_start(self.sums[b % self.SUMS][:], self.attended[b]).then_inc(self.sums_loaded[b % self.SUMS], 16)


class Routing:

    def __init__(self, nc, s, layer, kept, consts, gate, gate_bias, table, normed_dram):
        self.nc, self.layer, self.kept, self.consts, self.gate, self.gate_bias = nc, layer, kept, consts, gate, gate_bias
        self.table, self.normed_dram = table, normed_dram
        E = layer.experts
        self.spare = 8 - layer.chosen
        self.norm = Norm(nc, s, "r_", MOST)
        self.x_norm = s.sbuf("r_norm", [P, B, D], F32)
        self.x_turned = [s.sbuf(f"r_turned_sb{n}", [P, 2, P], F32) for n in range(2)]
        self.logits = s.sbuf("r_logits", [P, MOST, E], F32)
        self.top = s.sbuf("r_top", [P, MOST], F32)
        self.expo = s.sbuf("r_expo", [P, MOST, E], F32)
        self.total = s.sbuf("r_total", [P, MOST], F32)
        self.share = s.sbuf("r_share", [P, MOST], F32)
        self.probs = s.sbuf("r_probs", [P, MOST, E + self.spare], F32)
        self.taken = s.sbuf("r_taken", [P, MOST, E + self.spare], F32)
        self.best = s.sbuf("r_best", [P, MOST, 8], F32)
        self.picks = s.sbuf("r_picks", [P, MOST, 8], F32)
        self.index = s.sbuf("r_index", [P, MOST, 8], U32)
        self.junk = s.sbuf("r_junk", [P, 8, E], F32)
        self.place = s.sbuf("r_place", [P, MOST, 8], F32)
        self.place_int = s.sbuf("r_place_int", [P, MOST, 8], I32)
        self.column = s.sbuf("r_column", [P, MOST, 8], I32)
        self.address = s.sbuf("r_address", [P, B, 8], I32)
        self.ps_turned = s.psum("r_ps_turned", [P, 2, P])
        narrow = s.psum("r_ps_narrow", [P, 2 * MOST + 1, E])
        self.ps_logits, self.ps_rank, self.ps_count = narrow[:, 0:MOST], narrow[:, MOST:2 * MOST], narrow[:, 2 * MOST]
        (self.normed, self.stored, self.turned, self.turned_kept, self.scored, self.logits_ready, self.expo_ready,
         self.mask_ready, self.ranked, self.rank_kept, self.places_ready, self.scattered) = (
            s.sem("r_" + n) for n in ("normed", "stored", "turned", "turned_kept", "scored", "logits_ready",
                                      "expo_ready", "mask_ready", "ranked", "rank_kept", "places_ready", "scattered"))

    def dve_start(self, link):
        if self.spare:
            link.free(self.nc.vector.memset(self.probs[:, :, self.layer.experts:], -1.0))
            link.free(self.nc.vector.memset(self.picks[:, :, self.layer.chosen:], -1.0))
            link.free(self.nc.vector.memset(self.place[:, :, self.layer.chosen:], 0.0))

    def dve_normalise(self, link, i, x):
        self.norm(link, self.layer.groups[i], x, self.x_norm, self.normed)

    def sp_store(self, sp, i):
        group = self.layer.groups[i]
        sp.wait_ge(self.normed, group[-1] + 1)
        sp.dma_start(self.normed_dram.rearrange("(b p) n -> p b n", p=P)[:, span(group), :],
                     self.x_norm[:, span(group), :]).then_inc(self.stored, 16)

    def sp_finish(self, sp):
        sp.wait_ge(self.stored, 16 * len(self.layer.groups))

    def pe_turn(self, pe, b):
        pe.wait_ge(self.normed, b + 1)
        if b >= 1:
            pe.wait_ge(self.turned_kept, b)
        for k in range(2):
            last = self.nc.tensor.transpose(self.ps_turned[:, k, :], self.x_norm[:, b, k * P:(k + 1) * P],
                                            self.consts.identity[:])
        last.then_inc(self.turned, 1)

    def act_keep_turned(self, act, b):
        act.wait_ge(self.turned, b + 1)
        if b >= 2:
            act.wait_ge(self.scored, b - 1)
        self.nc.scalar.activation(self.x_turned[b % 2][:], self.ps_turned[:], ACT.Copy).then_inc(self.turned_kept, 1)

    def pe_score(self, pe, i, b):
        pe.wait_ge(self.turned_kept, b + 1)
        if i >= 1 and b == self.layer.groups[i][0]:
            pe.wait_ge(self.rank_kept, i)
        for k in range(2):
            last = self.nc.tensor.matmul(self.ps_logits[:, b - self.layer.groups[i][0], :], self.x_turned[b % 2][:, k, :],
                                         self.gate[:, k, :], start=k == 0, stop=k == 1)
        last.then_inc(self.scored, 1)

    def pe_turn_and_score(self, pe, i):
        group = self.layer.groups[i]
        self.pe_turn(pe, group[0])
        for b in group:
            if b != group[-1]:
                self.pe_turn(pe, b + 1)
            self.pe_score(pe, i, b)

    def dve_logits(self, dve, link, i):
        nc, n, E = self.nc, len(self.layer.groups[i]), self.layer.experts
        logits, top = self.logits[:, 0:n, :], self.top[:, 0:n]
        dve.wait_ge(self.scored, self.layer.groups[i][-1] + 1)
        scores = self.ps_logits[:, 0:n, :]
        if self.gate_bias is not None:
            link(nc.vector.tensor_tensor(logits, scores, self.gate_bias[:].unsqueeze(1).broadcast_to([P, n, E]), ALU.add))
            scores = logits
        link(nc.vector.reduce_max(top, scores, AX_X))
        nc.vector.tensor_tensor(logits, scores, top.unsqueeze(2).broadcast_to([P, n, E]),
                                ALU.subtract).then_inc(self.logits_ready, 1)

    def act_exponentials(self, act, i):
        n = len(self.layer.groups[i])
        act.wait_ge(self.logits_ready, i + 1)
        self.nc.scalar.activation(self.expo[:, 0:n, :], self.logits[:, 0:n, :], ACT.Exp).then_inc(self.expo_ready, 1)

    def dve_choose(self, dve, link, i):
        nc, E, chosen, n, batches = self.nc, self.layer.experts, self.layer.chosen, len(self.layer.groups[i]), span(self.layer.groups[i])
        expo, total, share, best = self.expo[:, 0:n, :], self.total[:, 0:n], self.share[:, 0:n], self.best[:, 0:n, :]
        weight, picks = self.kept.weight[:, batches, :], self.picks if self.spare else self.best
        dve.wait_ge(self.expo_ready, i + 1)
        link(nc.vector.reduce_sum(total, expo, AX_X))
        link(nc.vector.reciprocal(share, total))
        link(nc.vector.tensor_tensor(self.probs[:, 0:n, 0:E], expo, share.unsqueeze(2).broadcast_to([P, n, E]), ALU.mult))
        for j in range(n):
            link.free(nc.vector.max(self.best[:, j, :], self.probs[:, j, 0:E]))
        dve.wait_ge(link.semaphore, link.count)
        for j in range(n):
            link.free(nc.vector.max_index(self.index[:, j, :], self.best[:, j, :], self.probs[:, j, 0:E]))
        if self.spare:
            link.free(nc.vector.tensor_copy(self.picks[:, 0:n, 0:chosen], self.best[:, 0:n, 0:chosen]))
        dve.wait_ge(link.semaphore, link.count)
        for j in range(n):
            link.free(nc.vector.match_replace(self.taken[:, j, :], picks[:, j, :], self.probs[:, j, :], -2.0))
        dve.wait_ge(link.semaphore, link.count)
        nc.vector.tensor_scalar(self.kept.mask[:, batches, :], self.taken[:, 0:n, 0:E], -1.5, None,
                                ALU.is_lt).then_inc(self.mask_ready, 1)
        link.free(nc.vector.tensor_copy(self.kept.index[:, batches, :], self.index[:, 0:n, :]))
        if self.spare:
            link(nc.vector.reduce_sum(total, best[:, :, 0:chosen], AX_X))
            link(nc.vector.reciprocal(share, total))
            link(nc.vector.tensor_tensor(weight, best, share.unsqueeze(2).broadcast_to([P, n, 8]), ALU.mult))
        else:
            link(nc.vector.tensor_copy(weight, best))

    def pe_rank(self, pe, i):
        mask = self.kept.mask
        pe.wait_ge(self.mask_ready, i + 1)
        if i >= 1:
            pe.wait_ge(self.rank_kept, i)
        for j, b in enumerate(self.layer.groups[i]):
            last = self.nc.tensor.matmul(self.ps_rank[:, j, :], self.consts.earlier[:], mask[:, b, :], start=True, stop=b == 0)
            for before in range(b):
                last = self.nc.tensor.matmul(self.ps_rank[:, j, :], self.consts.ones[:], mask[:, before, :],
                                             start=False, stop=before == b - 1)
        last.then_inc(self.ranked, 1)

    def dve_places(self, dve, link, i):
        nc, kept, layer, n, batches = self.nc, self.kept, self.layer, len(self.layer.groups[i]), span(self.layer.groups[i])
        place, place_int, column = self.place[:, 0:n, :], self.place_int[:, 0:n, :], self.column[:, 0:n, :]
        dve.wait_ge(self.ranked, i + 1)
        nc.vector.tensor_copy(kept.rank[:, batches, :], self.ps_rank[:, 0:n, :]).then_inc(self.rank_kept, 1)
        dve.wait_ge(self.rank_kept, i + 1)
        for j, b in enumerate(self.layer.groups[i]):
            look_up(nc, link, layer, self.consts.ramp, kept.index[:, b, :], kept.rank[:, b, :], self.junk, self.place[:, j, :])
        link(nc.vector.scalar_tensor_tensor(place, kept.index[:, batches, :], float(TOKENS), place, ALU.mult, ALU.add))
        link(nc.vector.tensor_copy(place_int, place))
        link(nc.vector.tensor_scalar(column, place_int, P.bit_length() - 1, None, ALU.logical_shift_right))
        link(nc.vector.tensor_scalar(place_int, place_int, P - 1, layer.columns.bit_length() - 1,
                                     ALU.bitwise_and, ALU.logical_shift_left))
        nc.vector.tensor_tensor(self.address[:, batches, :], place_int, column, ALU.bitwise_or).then_inc(self.places_ready, 1)

    def pool_scatter(self, pool, i):
        pool.wait_ge(self.places_ready, i + 1)
        for b in self.layer.groups[i]:
            for k in range(self.layer.chosen):
                to = bass.IndirectOffsetOnAxis(ap=self.address[:, b, k:k + 1], axis=0)
                number = self.consts.choice[:, b, k:k + 1] if self.layer.by_token else self.consts.token[:, b:b + 1]
                self.nc.gpsimd.indirect_dma_start(self.table, to, number, None)\
                    .then_inc(self.scattered, 16)

    def pool_finish(self, pool):
        pool.wait_ge(self.scattered, 16 * self.layer.chosen * B)


def look_up(nc, link, layer, ramp, index, values, junk, found):
    for k in range(layer.chosen):
        link.free(nc.vector.scalar_tensor_tensor(junk[:, k, :], ramp[:, 0:layer.experts], index[:, k:k + 1], values,
                                                 ALU.is_equal, ALU.mult, accum_out=found[:, k:k + 1]))
    link.engine.wait_ge(link.semaphore, link.count)


def merge_phase(nc, consts, kept, x_all, inputs, table, normed_dram, experts):
    layer, w, bias, sums_in = LAYER0, inputs.w, inputs.bias, inputs.sums
    with ExitStack() as stack:
        s = Space(nc, stack, "mg_")
        share = s.sbuf("share", [P, MOST, 2, 4, 4], F32)
        heads = [s.sbuf(f"heads{n}", [P, 2, P], F32) for n in range(MOST)]
        merged = [s.sbuf(f"merged{n}", [P, D], F32) for n in range(MOST)]
        ps_sums = [s.psum(f"ps_sums{n}", [P, 2, 4, P]) for n in range(2)]
        ps_heads = s.psum("ps_heads", [P, 2, P])
        ps_merged = s.psum("ps_merged", [P, D])
        routing = Routing(nc, s, layer, kept, consts, inputs.gate, None, table, normed_dram)
        plan = Plan(nc, s, layer, consts, kept, routing)
        link_v = s.sem("link_v")
        sums_turned, heads_ready, heads_turned, heads_kept, merged_ready, x_ready = (
            s.sem(n) for n in ("sums_turned", "heads_ready", "heads_turned", "heads_kept", "merged_ready", "x_ready"))
        block = stack.enter_context(nc.Block())

        def of(i):
            return layer.groups[i] if 0 <= i < len(layer.groups) else ()

        @block.sync
        def _(sp):
            for b in range(inputs.SUMS, B):
                sp.wait_ge(sums_turned, b - inputs.SUMS + 1)
                inputs.load_sums(sp, b)
            for i in range(len(layer.groups)):
                routing.sp_store(sp, i)
            experts.load_first(sp, plan.planned)
            routing.sp_finish(sp)

        @block.tensor
        def _(pe):
            def turn_sums(b):
                n = b % inputs.SUMS
                pe.wait_ge(inputs.sums_loaded[n], 16 * (b // inputs.SUMS + 1))
                if b >= 2:
                    pe.wait_ge(heads_ready, b - 1)
                for half in range(2):
                    for g in range(4):
                        last = nc.tensor.transpose(ps_sums[b % 2][:, half, g, :], sums_in[n][:, g, half * P:(half + 1) * P],
                                                   consts.identity[:])
                last.then_inc(sums_turned, 1)

            def turn_heads(b):
                pe.wait_ge(heads_ready, b + 1)
                if b >= 1:
                    pe.wait_ge(heads_kept, b)
                for half in range(2):
                    last = nc.tensor.transpose(ps_heads[:, half, :], heads[b % MOST][:, half, :], consts.identity[:])
                last.then_inc(heads_turned, 1)

            def merge(b):
                pe.wait_ge(heads_kept, b + 1)
                if b >= 1:
                    pe.wait_ge(x_ready, b)
                nc.tensor.matmul(ps_merged[:], w[:], merged[b % MOST][:], start=True, stop=True).then_inc(merged_ready, 1)

            pe.wait_ge(inputs.weights_loaded, 48)
            turn_sums(0)
            turn_sums(1)
            for i in range(len(layer.groups) + 1):
                if i >= 1:
                    routing.pe_turn_and_score(pe, i - 1)
                for b in of(i):
                    turn_heads(b)
                    if b + 2 < B:
                        turn_sums(b + 2)
                for b in of(i):
                    merge(b)
                if i >= 1:
                    routing.pe_rank(pe, i - 1)
            plan.pe_count(pe)
            plan.pe_rows(pe)

        @block.scalar
        def _(act):
            act.wait_ge(inputs.weights_loaded, 48)
            for i in range(len(layer.groups) + 1):
                for b in of(i - 1):
                    routing.act_keep_turned(act, b)
                for b in of(i):
                    act.wait_ge(heads_turned, b + 1)
                    if b >= MOST:
                        act.wait_ge(merged_ready, b - MOST + 1)
                    nc.scalar.activation(merged[b % MOST][:], ps_heads[:].rearrange("p a n -> p (a n)"), ACT.Identity,
                                         bias=bias[:, 2:3]).then_inc(heads_kept, 1)
                if i >= 1:
                    routing.act_exponentials(act, i - 1)

        @block.vector
        def _(dve):
            link = Link(dve, link_v)

            def divide(b, j):
                dve.wait_ge(sums_turned, b + 1)
                sums = ps_sums[b % 2][:].rearrange("p a g (j v) -> p a g j v", v=VW)
                for half in range(2):
                    link.free(nc.vector.reciprocal(share[:, j, half], sums[:, half, :, :, HD]))
                dve.wait_ge(link_v, link.count)
                if b >= MOST:
                    dve.wait_ge(heads_turned, b - MOST + 1)
                for half in range(2):
                    to = heads[b % MOST][:, half, :].rearrange("p (d g j) -> p g j d", g=4, j=4)
                    last = nc.vector.tensor_tensor(to, sums[:, half, :, :, 0:HD],
                                                   share[:, j, half].unsqueeze(3).broadcast_to([P, 4, 4, HD]), ALU.mult)
                last.then_inc(heads_ready, 1)

            def add(b):
                dve.wait_ge(merged_ready, b + 1)
                nc.vector.scalar_tensor_tensor(x_all[:, b, :], ps_merged[:], bias[:, 3:4], x_all[:, b, :],
                                               ALU.add, ALU.add).then_inc(x_ready, 1)

            dve.wait_ge(inputs.weights_loaded, 48)
            routing.dve_start(link)
            for i in range(len(layer.groups) + 1):
                for j, b in enumerate(of(i)):
                    divide(b, j)
                if i >= 1:
                    routing.dve_logits(dve, link, i - 1)
                for b in of(i):
                    add(b)
                if i >= 1:
                    routing.dve_choose(dve, link, i - 1)
                if of(i):
                    dve.wait_ge(x_ready, layer.groups[i][-1] + 1)
                    routing.dve_normalise(link, i, x_all)
                if i >= 1:
                    routing.dve_places(dve, link, i - 1)
            plan.dve_plan(dve, link)

        @block.gpsimd
        def _(pool):
            for i in range(len(layer.groups)):
                routing.pool_scatter(pool, i)
            routing.pool_finish(pool)


def tiles_phase(nc, layer, consts, kept, table, normed_dram, experts, rows_out, spare_rows=None):
    with ExitStack() as stack:
        s = Space(nc, stack, layer.name)
        E, U, C, W = layer.experts, layer.unroll, layer.chunks, layer.width
        lists = s.sbuf("lists", [P, layer.list_columns, 1 + layer.by_token], I32)
        choices = s.sbuf("choices", [P, layer.list_columns], I32)
        tile_column, groups_between = kept.tile_column, kept.groups_between
        lists_loaded, lists_ready, shifted = s.sem("lists_loaded"), s.sem("lists_ready"), s.sem("shifted")
        up_w, down_w, weights_loaded = experts.up, experts.down, experts.loaded
        column = [s.sbuf(f"column{u}", [P, 1, 1 + layer.by_token], I32) for u in range(U)]
        target = [s.sbuf(f"target{u}", [P, 1], I32) for u in range(U)]
        rows = [s.sbuf(f"rows{u}", [P, D], F32) for u in range(U)]
        out = [s.sbuf(f"out{u}", [P, D], F32) for u in range(U)]
        x_turned = [s.sbuf(f"x_turned{n}", [P, 2, P], F32) for n in range(2)]
        silu = [s.sbuf(f"silu{n}", [W, C * P], F32) for n in range(2)]
        inner = [s.sbuf(f"inner{n}", [W, C * P], F32) for n in range(2)]
        ps_x = [s.psum(f"ps_x{n}", [P, 2, P]) for n in range(2)]
        ps_up = [s.psum(f"ps_up{n}", [W, 2, C * P]) for n in range(2)]
        ps_out = [s.psum(f"ps_out{n}", [P, D]) for n in range(2)]
        gathered = [s.sem(f"gathered{u}") for u in range(U)]
        stored = [s.sem(f"stored{u}") for u in range(U)]
        column_copied, parted, turned, turned_kept, up_done, silu_done, inner_ready, down_done, out_kept = (
            s.sem(n) for n in ("column_copied", "parted", "turned", "turned_kept", "up_done", "silu_done",
                               "inner_ready", "down_done", "out_kept"))
        block = stack.enter_context(nc.Block())
        most_groups = layer.tiles // U

        def groups(engine):
            return engine.value_load(groups_between[0:1, 0:1], min_val=0, max_val=most_groups - 2) + 1

        def apart(engine):
            engine.sem_inc(parted, 1)

        @block.sync
        def _(sp):
            sp.dma_start(choices[:, 0:layer.columns], table.rearrange("(p c) a -> p (c a)", p=P)).then_inc(lists_loaded, 16)
            if layer.by_token:
                sp.dma_start(choices[:, layer.columns:], spare_rows[:, layer.columns:]).then_inc(lists_loaded, 16)
            last = groups(sp)

            with sp.Fori(1, last + 1) as i:
                for u in range(U):
                    sp.wait_ge(down_done, i * U + u - U + 1)
                    experts.load(sp, i, u)

        @block.gpsimd
        def _(pool):
            last = groups(pool)
            pool.wait_ge(lists_ready, 1)
            apart(pool)

            def gather(i, u):
                c = pool.value_load(tile_column[0:1, bass.ds(i * U + u, 1)], min_val=0, max_val=layer.list_columns - 1)
                nc.gpsimd.tensor_copy(column[u][:], lists[:, bass.ds(c, 1), :]).then_inc(column_copied, 1)
                pool.wait_ge(column_copied, i * U + u + 1)
                apart(pool)
                of = bass.IndirectOffsetOnAxis(ap=column[u][:, 0, 0:1], axis=0)
                nc.gpsimd.indirect_dma_start(rows[u][:], None, normed_dram, of).then_inc(gathered[u], 16)

            def scatter(u):
                to = bass.IndirectOffsetOnAxis(ap=target[u][:], axis=0)
                nc.gpsimd.indirect_dma_start(rows_out, to, out[u][:], None).then_inc(stored[u], 16)

            for u in range(U):
                gather(0, u)
            with pool.Fori(1, last + 1) as i:
                for u in range(U):
                    if layer.by_token:
                        pool.wait_ge(out_kept, i * U + u - U + 1)
                    else:
                        pool.wait_ge(turned, i * U + u - U + 1)
                    gather(i, u)
                    if layer.by_token:
                        scatter(u)
            if layer.by_token:
                for u in range(U):
                    pool.wait_ge(out_kept, last * U + u + 1)
                    apart(pool)
                    scatter(u)
                for u in range(U):
                    pool.wait_ge(stored[u], last * 16 + 16)
                    apart(pool)

        @block.tensor
        def _(pe):
            last = groups(pe)

            def down(t, u):
                pe.wait_ge(inner_ready, t + 1)
                for c in range(C):
                    op = nc.tensor.matmul(ps_out[u % 2][:], inner[u % 2][:, c * P:(c + 1) * P], down_w[u][:, c, :],
                                          start=c == 0, stop=c == C - 1)
                op.then_inc(down_done, 1)

            def turn(i, u):
                pe.wait_ge(gathered[u], i * 16 + 16)
                for k in range(2):
                    op = nc.tensor.transpose(ps_x[u % 2][:, k, :], rows[u][:, k * P:(k + 1) * P], consts.identity[:])
                op.then_inc(turned, 1)

            def up(i, u):
                pe.wait_ge(turned_kept, i * U + u + 1)
                pe.wait_ge(weights_loaded[u], (i + 1) * (16 * len(experts.transfers)))
                for part in range(2):
                    for c in range(C):
                        at = (part * C + c) * W
                        for k in range(2):
                            op = nc.tensor.matmul(ps_up[u % 2][:, part, c * P:(c + 1) * P], up_w[u][:, k, at:at + W],
                                                  x_turned[u % 2][:, k, :], start=k == 0, stop=k == 1)
                op.then_inc(up_done, 1)

            def step(i, u, first=False, final=False):
                if not (final and u == U - 1):
                    turn(i if u + 1 < U else i + 1, (u + 1) % U)
                if not (first and u < 2):
                    down(i * U + u - 2, (u - 2) % U)
                up(i, u)

            turn(0, 0)
            for u in range(U):
                step(0, u, True)
            with pe.Fori(1, last) as i:
                for u in range(U):
                    step(i, u)
            for u in range(U):
                step(last, u, final=True)
            down(last * U + U - 2, U - 2)
            down(last * U + U - 1, U - 1)

        @block.scalar
        def _(act):
            last = groups(act)

            def store(i, u):
                act.wait_ge(out_kept, i * U + u + 1)
                act.dma_start(rows_out[bass.ds(i * U + u, 1)].rearrange("a p n -> (a p) n"), out[u][:]).then_inc(stored[u], 16)

            def keep_turned(i, u):
                act.wait_ge(turned, i * U + u + 1)
                nc.scalar.activation(x_turned[u % 2][:], ps_x[u % 2][:], ACT.Copy).then_inc(turned_kept, 1)

            def step(i, u, first=False, final=False):
                if not (final and u == U - 1):
                    keep_turned(i if u + 1 < U else i + 1, (u + 1) % U)
                act.wait_ge(up_done, i * U + u + 1)
                nc.scalar.activation(silu[u % 2][:], ps_up[u % 2][:, 0, :], ACT.Silu).then_inc(silu_done, 1)
                if not (layer.by_token or first and u < 2):
                    store(i if u >= 2 else i - 1, (u - 2) % U)

            keep_turned(0, 0)
            for u in range(U):
                step(0, u, True)
            with act.Fori(1, last) as i:
                for u in range(U):
                    step(i, u)
            for u in range(U):
                step(last, u, final=True)
            if not layer.by_token:
                store(last, U - 2)
                store(last, U - 1)
                for u in range(U):
                    act.wait_ge(stored[u], last * 16 + 32)
                    apart(act)

        @block.vector
        def _(dve):
            last = groups(dve)
            if not layer.by_token:
                for u in range(U):
                    dve.sem_inc(stored[u], 16)
            if layer.by_token:
                dve.wait_ge(lists_loaded, 32)
                nc.vector.tensor_copy(lists[:, :, 1], choices[:])
                nc.vector.tensor_scalar(lists[:, :, 0], choices[:], layer.chosen.bit_length() - 1, None,
                                        ALU.logical_shift_right).then_inc(shifted, 1)
                dve.wait_ge(shifted, 1)
                nc.vector.tensor_scalar(lists[:, :, 0], lists[:, :, 0], TOKENS - 1, None, ALU.min).then_inc(lists_ready, 1)
            else:
                nc.vector.memset(lists[:, layer.columns:, 0], 0)
                dve.wait_ge(lists_loaded, 16)
                nc.vector.tensor_copy(lists[:, 0:layer.columns, 0], choices[:, 0:layer.columns]).then_inc(lists_ready, 1)

            def keep(i, u, free=False):
                if not free:
                    dve.wait_ge(stored[u], i * 16 + (0 if layer.by_token else 16))
                dve.wait_ge(down_done, i * U + u + 1)
                if layer.by_token:
                    nc.vector.tensor_copy(target[u][:], column[u][:, 0, 1:2])
                nc.vector.tensor_copy(out[u][:], ps_out[u % 2][:]).then_inc(out_kept, 1)

            def step(i, u, free=False):
                if not (isinstance(i, int) and i == 0 and u < 2):
                    keep(i if u >= 2 else i - 1, (u - 2) % U, free)
                dve.wait_ge(silu_done, i * U + u + 1)
                nc.vector.tensor_tensor(inner[u % 2][:], silu[u % 2][:], ps_up[u % 2][:, 1, :], ALU.mult).then_inc(inner_ready, 1)

            for u in range(U):
                step(0, u, free=True)
            for u in range(U):
                step(1, u, free=u < 2)
            with dve.Fori(2, last + 1) as i:
                for u in range(U):
                    step(i, u)
            keep(last, U - 2)
            keep(last, U - 1)


class Plan:

    def __init__(self, nc, s, layer, consts, kept, routing):
        self.nc, self.layer, self.consts, self.kept, self.routing = nc, layer, consts, kept, routing
        E = layer.experts
        self.count = s.sbuf("p_count", [P, E], I32)
        self.tiles = s.sbuf("p_tiles", [P, E], F32)
        self.ends = [s.sbuf(f"p_ends{n}", [P, E], F32) for n in range(2)]
        self.first_row = s.sbuf("p_first_row", [P, E], F32)
        self.rank = s.sbuf("p_rank", [P, B, E], F32)
        self.junk = s.sbuf("p_junk", [P, 8, P], F32)
        self.groups = s.sbuf("p_groups", [P, P], F32)
        self.own = s.sbuf("p_own", [P, 8], F32)
        self.place = s.sbuf("p_place", [P, B, 8], F32)
        self.ps_count, self.ps_row = routing.ps_count, routing.ps_turned
        self.counted, self.own_ready, self.rows_ready, self.planned = (
            s.sem("p_" + n) for n in ("counted", "own_ready", "rows_ready", "planned"))

    def pe_count(self, pe):
        pe.wait_ge(self.routing.rank_kept, len(self.layer.groups))
        for b in range(B):
            last = self.nc.tensor.matmul(self.ps_count, self.consts.ones[:], self.kept.mask[:, b, :],
                                         start=b == 0, stop=b == B - 1)
        last.then_inc(self.counted, 1)

    def pe_rows(self, pe):
        pe.wait_ge(self.own_ready, 1)
        for n in range(2):
            last = self.nc.tensor.transpose(self.ps_row[0:1, n, :], self.own[:, n:n + 1], self.consts.identity[:])
        last.then_inc(self.rows_ready, 1)

    def dve_plan(self, dve, link):
        nc, layer, consts, kept = self.nc, self.layer, self.consts, self.kept
        E, U = layer.experts, layer.unroll
        count, tiles, ends, junk, groups = self.count, self.tiles, self.ends, self.junk, self.groups
        expert, col, done_experts, done_tiles, last_group = (self.own[:, n:n + 1] for n in range(5))
        dve.wait_ge(self.counted, 1)
        link(nc.vector.tensor_scalar(count[:], self.ps_count, float(P - 1), None, ALU.add))
        link(nc.vector.tensor_scalar(count[:], count[:], P.bit_length() - 1, None, ALU.logical_shift_right))
        link(nc.vector.tensor_copy(tiles[:], count[:]))
        link(nc.vector.tensor_copy(ends[0][:], tiles[:]))
        n, step = 0, 1
        while step < E:
            link.free(nc.vector.tensor_copy(ends[1 - n][:, 0:step], ends[n][:, 0:step]))
            link(nc.vector.tensor_tensor(ends[1 - n][:, step:], ends[n][:, step:], ends[n][:, 0:E - step], ALU.add))
            n, step = 1 - n, 2 * step
        end = ends[n]
        link.free(nc.vector.tensor_scalar(junk[:, 0, 0:E], end[:], consts.number[:, 0:1], None, ALU.is_le, ALU.add,
                                          accum_out=done_experts))
        link(nc.vector.scalar_tensor_tensor(junk[:, 1, 0:E], end[:], consts.number[:, 0:1], tiles[:], ALU.is_le, ALU.mult,
                                            accum_out=done_tiles))
        link.free(nc.vector.tensor_scalar(expert, done_experts, float(E - 1), None, ALU.min))
        link(nc.vector.scalar_tensor_tensor(col, done_experts, float(layer.lists), consts.number[:, 0:1], ALU.mult, ALU.add))
        link(nc.vector.tensor_tensor(col, col, done_tiles, ALU.subtract))
        link(nc.vector.tensor_scalar(col, col, float(layer.list_columns - 1), None, ALU.min))
        nc.vector.engine_nop().then_inc(self.own_ready, 1)
        most = layer.tiles // U
        link(nc.vector.tensor_scalar(groups[:, 0:most], consts.ramp[:, 0:most], float(U), float(U + 1), ALU.mult, ALU.add))
        link(nc.vector.tensor_scalar(junk[:, 2, 0:most], groups[:, 0:most], end[:, E - 1:E], None, ALU.is_le, ALU.add,
                                     accum_out=last_group))
        link(nc.vector.tensor_scalar(kept.groups_between[:], last_group[0:1, :], -1.0, None, ALU.add))
        dve.wait_ge(self.rows_ready, 1)
        link(nc.vector.tensor_copy(kept.tile_column[:], self.ps_row[0:1, 1, :]))
        nc.vector.tensor_copy(kept.tile_expert[:], self.ps_row[0:1, 0, :]).then_inc(self.planned, 1)
        if layer.by_token:
            return
        link(nc.vector.tensor_tensor(self.first_row[:], end[:], tiles[:], ALU.subtract))
        link(nc.vector.tensor_scalar(self.first_row[:], self.first_row[:], float(P), None, ALU.mult))
        link(nc.vector.tensor_tensor(self.rank[:], kept.rank[:], self.first_row[:].unsqueeze(1).broadcast_to([P, B, E]), ALU.add))
        link(nc.vector.memset(self.place[:], 0.0))
        for b in range(B):
            look_up(nc, link, layer, consts.ramp, kept.index[:, b, :], self.rank[:, b, :], junk[:, :, 0:E], self.place[:, b, :])
        link(nc.vector.tensor_copy(kept.row[:], self.place[:]))


class Gather:

    DEEP = B

    def __init__(self, nc, s, layer, kept, rows_dram):
        self.nc, self.layer, self.kept = nc, layer, kept
        self.rows_dram = rows_dram.rearrange("t p n -> (t p) n")
        self.rows = [s.sbuf(f"g_rows{n}", [P, layer.chosen, D], F32) for n in range(self.DEEP)]
        self.gathered = [s.sem(f"g_gathered{n}") for n in range(self.DEEP)]
        self.summed = s.sem("g_summed")

    def pool_gather(self, pool, b):
        n = b % self.DEEP
        if b >= self.DEEP:
            pool.wait_ge(self.summed, b - self.DEEP + 1)
        for k in range(self.layer.chosen):
            of = bass.IndirectOffsetOnAxis(ap=self.kept.row[:, b, k:k + 1], axis=0)
            self.nc.gpsimd.indirect_dma_start(self.rows[n][:, k, :], None, self.rows_dram, of)\
                .then_inc(self.gathered[n], 16)

    def dve_sum(self, dve, link, group, x, out):
        nc, last = self.nc, self.layer.chosen - 1
        for b in group:
            dve.wait_ge(self.gathered[b % self.DEEP], 16 * self.layer.chosen * (b // self.DEEP + 1))
        for k in range(last + 1):
            for b in group:
                op = nc.vector.scalar_tensor_tensor(out[:, b, :], self.rows[b % self.DEEP][:, k, :], self.kept.weight[:, b, k:k + 1],
                                                    (x if k == 0 else out)[:, b, :], ALU.mult, ALU.add)
                if k < last:
                    link.free(op)
                else:
                    op.then_inc(self.summed, 1)
            if k < last:
                dve.wait_ge(link.semaphore, link.count)


def features_phase(nc, consts, kept0, kept1, x_all, ctx, ctx_turned, rows_dram, gate_dram, gate_bias_dram, table, normed_dram, experts):
    layer = LAYER1
    scale = 1.0 / float(np.sqrt(D))
    with ExitStack() as stack:
        s = Space(nc, stack, "ft_")
        gate = s.sbuf("gate", [P, 2, layer.experts], F32)
        gate_bias = s.sbuf("gate_bias", [P, layer.experts], F32)
        keys = s.sbuf("keys", [P, B, D], F32)
        vals = s.sbuf("vals", [P, B, 2, P], F32)
        x_sum = s.sbuf("x_sum", [P, B, D], F32)
        norm = Norm(nc, s, "", MOST)
        x_norm = s.sbuf("x_norm", [P, B, D], F32)
        top = s.sbuf("top", [P, MOST, 2], F32)
        minus_top = s.sbuf("minus_top", [P, MOST, 2], F32)
        expo = s.sbuf("expo", [P, MOST, 2, D], F32)
        total = s.sbuf("total", [P, MOST, 2], F32)
        share = s.sbuf("share", [P, MOST, 2], F32)
        vals_shared = s.sbuf("vals_shared", [P, MOST, 2, P], F32)
        ps_scores = [s.psum(f"ps_scores{n}", [P, 2, D]) for n in range(MOST)]
        ps_out = [s.psum(f"ps_out{n}", [P, D]) for n in range(2)]
        gather = Gather(nc, s, LAYER0, kept0, rows_dram)
        routing = Routing(nc, s, layer, kept1, consts, gate, gate_bias, table, normed_dram)
        plan = Plan(nc, s, layer, consts, kept1, routing)
        inputs_loaded, link_v = s.sem("inputs_loaded"), s.sem("link_v")
        normed, scored, top_known, expo_ready, share_ready, vals_ready, attended, x_ready = (
            s.sem(n) for n in ("normed", "scored", "top_known", "expo_ready", "share_ready", "vals_ready", "attended", "x_ready"))
        block = stack.enter_context(nc.Block())
        STEPS = range(len(layer.groups) + 1)

        def of(i):
            return list(enumerate(layer.groups[i])) if i < len(layer.groups) else []

        @block.sync
        def _(sp):
            sp.dma_start(keys[:], ctx.rearrange("b p n -> p b n")).then_inc(inputs_loaded, 16)
            sp.dma_start(vals[:], ctx_turned.rearrange("b p k n -> p b k n")).then_inc(inputs_loaded, 16)
            sp.dma_start(gate[:], gate_dram).then_inc(inputs_loaded, 16)
            sp.dma_start(gate_bias[:], gate_bias_dram).then_inc(inputs_loaded, 16)
            for i in range(len(layer.groups)):
                routing.sp_store(sp, i)
            experts.load_first(sp, plan.planned)
            routing.sp_finish(sp)

        @block.gpsimd
        def _(pool):
            for b in range(B):
                gather.pool_gather(pool, b)
            for i in range(len(layer.groups)):
                routing.pool_scatter(pool, i)
            routing.pool_finish(pool)

        @block.tensor
        def _(pe):
            pe.wait_ge(inputs_loaded, 64)
            for i in STEPS:
                for j, b in of(i):
                    pe.wait_ge(normed, b + 1)
                    if i >= 1:
                        pe.wait_ge(expo_ready, b - j)
                    for c in range(2):
                        op = nc.tensor.matmul(ps_scores[j][:, c, :], keys[:, b, c * P:(c + 1) * P], x_norm[:, b, :], start=True, stop=True)
                    op.then_inc(scored, 1)
                if i >= 1:
                    routing.pe_rank(pe, i - 1)
                for j, b in of(i):
                    pe.wait_ge(vals_ready, b + 1)
                    if b >= 2:
                        pe.wait_ge(x_ready, b - 1)
                    for c in range(2):
                        op = nc.tensor.matmul(ps_out[b % 2][:], vals_shared[:, j, c, :], expo[:, j, c, :], start=c == 0, stop=c == 1)
                    op.then_inc(attended, 1)
                if of(i):
                    routing.pe_turn_and_score(pe, i)
            plan.pe_count(pe)
            plan.pe_rows(pe)

        @block.scalar
        def _(act):
            for i in STEPS:
                if i >= 1:
                    routing.act_exponentials(act, i - 1)
                for j, b in of(i):
                    act.wait_ge(top_known, b + 1)
                    if i >= 1:
                        act.wait_ge(attended, b - j)
                    for c in range(2):
                        op = nc.scalar.activation(expo[:, j, c, :], ps_scores[j][:, c, :], ACT.Exp, bias=minus_top[:, j, c:c + 1],
                                                  scale=scale, accum_out=total[:, j, c:c + 1])
                    op.then_inc(expo_ready, 1)
                for j, b in of(i):
                    act.wait_ge(share_ready, b + 1)
                    for c in range(2):
                        op = nc.scalar.activation(vals_shared[:, j, c, :], vals[:, b, c, :], ACT.Copy, scale=share[:, j, c:c + 1])
                    op.then_inc(vals_ready, 1)
                for j, b in of(i):
                    routing.act_keep_turned(act, b)

        @block.vector
        def _(dve):
            link = Link(dve, link_v)
            routing.dve_start(link)
            for i in STEPS:
                if of(i):
                    gather.dve_sum(dve, link, layer.groups[i], x_all, x_sum)
                    dve.wait_ge(gather.summed, layer.groups[i][-1] + 1)
                    norm(link, layer.groups[i], x_sum, x_norm, normed)
                if i >= 1:
                    if i == 1:
                        dve.wait_ge(inputs_loaded, 64)
                    routing.dve_logits(dve, link, i - 1)
                for j, b in of(i):
                    dve.wait_ge(scored, b + 1)
                    link(nc.vector.reduce_max(top[:, j, :], ps_scores[j][:], AX_X))
                    nc.vector.tensor_scalar(minus_top[:, j, :], top[:, j, :], -scale, None, ALU.mult).then_inc(top_known, 1)
                if i >= 1:
                    routing.dve_choose(dve, link, i - 1)
                for j, b in of(i):
                    dve.wait_ge(expo_ready, b + 1)
                    nc.vector.reciprocal(share[:, j, :], total[:, j, :]).then_inc(share_ready, 1)
                if i >= 1:
                    routing.dve_places(dve, link, i - 1)
                for j, b in of(i):
                    dve.wait_ge(attended, b + 1)
                    nc.vector.tensor_tensor(x_all[:, b, :], x_sum[:, b, :], ps_out[b % 2][:], ALU.add).then_inc(x_ready, 1)
                if of(i):
                    dve.wait_ge(x_ready, layer.groups[i][-1] + 1)
                    routing.dve_normalise(link, i, x_all)
            plan.dve_plan(dve, link)


def last_phase(nc, kept, x_all, rows_dram, out):
    chosen = LAYER1.chosen
    with ExitStack() as stack:
        s = Space(nc, stack, "ls_")
        x_sum = s.sbuf("x_sum", [P, B, D], F32)
        rows = s.sbuf("rows", [P, B, chosen, D], F32)
        link_v, summed, stored = s.sem("link_v"), s.sem("summed"), s.sem("stored")
        loaded = [s.sem(f"loaded{b}") for b in range(B)]
        block = stack.enter_context(nc.Block())
        by_batch = rows_dram[0:TOKENS * chosen].rearrange("(b p k) n -> b p k n", b=B, k=chosen)

        @block.sync
        def _(sp):
            for b in range(B):
                sp.dma_start(rows[:, b], by_batch[b]).then_inc(loaded[b], 16)
            sp.wait_ge(stored, 16 * B)

        @block.scalar
        def _(act):
            for b in range(B):
                act.wait_ge(summed, b + 1)
                act.dma_start(out[b], x_sum[:, b, :]).then_inc(stored, 16)

        @block.vector
        def _(dve):
            link = Link(dve, link_v)
            for pair in range(0, B, 2):
                for b in (pair, pair + 1):
                    dve.wait_ge(loaded[b], 16)
                for k in range(chosen):
                    for b in (pair, pair + 1):
                        op = nc.vector.scalar_tensor_tensor(x_sum[:, b, :], rows[:, b, k, :], kept.weight[:, b, k:k + 1],
                                                            (x_sum if k else x_all)[:, b, :], ALU.mult, ALU.add)
                        if k + 1 < chosen:
                            link.free(op)
                        else:
                            op.then_inc(summed, 1)
                    if k + 1 < chosen:
                        dve.wait_ge(link_v, link.count)


def two_layers(nc, x, ctx, ctx_turned, consts_f, token_numbers, choice_numbers, spare_rows, weights, biases, rotary, gate0, weights0,
               gate1, gate1_bias, up1, down1, out):
    def scratch(name, shape, dtype=F32):
        return nc.dram_tensor(name, shape, dtype, kind="Internal").ap()

    parts_dram = scratch("parts", [B, Operands.SLOTS, P, D], BF16)
    attended = scratch("attended", [B, P, 4, D])
    normed = [scratch(f"normed{n}", [TOKENS, D]) for n in range(2)]
    tables = [scratch(f"table{n}", [P * layer.columns, 1], I32) for n, layer in enumerate((LAYER0, LAYER1))]
    rows = [scratch("rows0", [LAYER0.tiles, P, D]),
            scratch("rows1", [TOKENS * LAYER1.chosen + P * LAYER1.list_columns, D])]
    with ExitStack() as stack:
        s = Space(nc, stack, "")
        consts, kept0, kept1 = Consts(s), Kept(s, LAYER0), Kept(s, LAYER1)
        x_all = s.sbuf("x_all", [P, B, D], F32)
        with ExitStack() as expert_stack:
            experts = Experts(Space(nc, expert_stack, "e0_"), LAYER0, kept0, weights0)
            with ExitStack() as merging:
                inputs = MergeInputs(Space(nc, merging, "mi_"), attended, weights, biases, gate0)
                with ExitStack() as attention:
                    operands = Operands(Space(nc, attention, "op_"), parts_dram)
                    project_phase(nc, x, x_all, ctx, weights, biases, rotary, operands,
                                  consts, consts_f, token_numbers, choice_numbers, spare_rows, *tables)
                    attend_phase(nc, consts.identity, operands, attended,
                                 [rows[0][LAYER0.least:]], inputs)
                merge_phase(nc, consts, kept0, x_all, inputs, tables[0], normed[0], experts)
            tiles_phase(nc, LAYER0, consts, kept0, tables[0], normed[0], experts, rows[0])
        with ExitStack() as expert_stack:
            experts = Experts(Space(nc, expert_stack, "e1_"), LAYER1, kept1, up1, down1)
            features_phase(nc, consts, kept0, kept1, x_all, ctx, ctx_turned, rows[0], gate1, gate1_bias, tables[1],
                           normed[1], experts)
            tiles_phase(nc, LAYER1, consts, kept1, tables[1], normed[1], experts, rows[1], spare_rows)
        last_phase(nc, kept1, x_all, rows[1], out)


def laid_out(x, ctx_2048, L0_xattn_encoding, L0_xattn_Wq, L0_xattn_bq, L0_xattn_Wk, L0_xattn_bk, L0_xattn_Wv,
             L0_xattn_bv, L0_xattn_Wm, L0_xattn_bm, L0_ffn_gate_w, L0_ffn_w13, L0_ffn_w2, L1_ffn_router_w,
             L1_ffn_expert_bias, L1_ffn_gate_proj, L1_ffn_up_proj, L1_ffn_down_proj):
    at = np.arange(P)
    tokens = at[:, None] + P * np.arange(B)[None, :]
    identity = np.eye(P, dtype=np.float32)
    earlier = (at[:, None] < at[None, :]).astype(np.float32)
    ramp = np.broadcast_to(at.astype(np.float32), (P, P))
    sign = np.where(at // H % 2 == 0, -1.0, 1.0).astype(np.float32)
    swap = at ^ H
    bq, bk = L0_xattn_bq, L0_xattn_bk
    rotary = np.repeat(L0_xattn_encoding[:, 0, 0].transpose(2, 0, 1), H, axis=0)

    def by_contraction(w):
        return w.reshape(w.shape[0], 2, P, -1).transpose(0, 2, 1, 3)

    def gates(w):
        return w.T.reshape(2, P, -1).transpose(1, 0, 2)

    up1 = np.concatenate([L1_ffn_gate_proj, L1_ffn_up_proj], axis=2)
    return {
        "x": x,
        "ctx": ctx_2048,
        "ctx_turned": ctx_2048.transpose(0, 2, 1).reshape(B, 2, P, P).transpose(0, 2, 1, 3),
        "consts_f": np.stack([identity, earlier, ramp], axis=1),
        "token_numbers": tokens.astype(np.int32),
        "choice_numbers": (tokens[:, :, None] * LAYER1.chosen + np.arange(LAYER1.chosen)).astype(np.int32),
        "spare_rows": (TOKENS * LAYER1.chosen + np.arange(P * LAYER1.list_columns).reshape(P, -1)).astype(np.int32),
        "weights": np.stack([w.T for w in (L0_xattn_Wq, L0_xattn_Wk, L0_xattn_Wv, L0_xattn_Wm)], axis=1),
        "biases": np.stack([bq, bk, L0_xattn_bv, L0_xattn_bm, bq[swap], bk[swap], sign], axis=1),
        "rotary": rotary,
        "gate0": gates(L0_ffn_gate_w),
        "weights0": np.concatenate([by_contraction(L0_ffn_w13.transpose(0, 2, 1)),
                                    L0_ffn_w2.transpose(0, 2, 1)[:, :, None, :]], axis=2),
        "gate1": gates(L1_ffn_router_w),
        "gate1_bias": np.broadcast_to(L1_ffn_expert_bias, (P, LAYER1.experts)),
        "up1": by_contraction(up1),
        "down1": L1_ffn_down_proj.reshape(LAYER1.experts, LAYER1.chunks, LAYER1.width, D).transpose(0, 2, 1, 3),
    }


def kernel(**inputs):
    import concourse.bacc as bacc
    from concourse.bass_utils import run_bass_kernel_spmd

    nc = bacc.Bacc("TRN2", target_bir_lowering=False, num_devices=1)
    arrays, args = {}, []
    for name, a in laid_out(**{k: np.asarray(v) for k, v in inputs.items()}).items():
        a = np.ascontiguousarray(a)
        arrays["in_" + name] = a
        args.append(nc.dram_tensor("in_" + name, a.shape, mybir.dt.from_np(a.dtype), kind="ExternalInput").ap())
    out = nc.dram_tensor("out", (B, P, D), F32, kind="ExternalOutput").ap()
    two_layers(nc, *args, out)
    result = run_bass_kernel_spmd(nc, [arrays], core_ids=[0])
    return result.results[0]["out"]
```
